# Optimizing a Trainium2 kernel written in Bass

```python
import numpy as np
import jax
import jax.numpy as jnp

def _softmax(x, axis=-1):
    return jax.nn.softmax(x, axis=axis)

def _gelu(x):
    return jax.nn.gelu(x, approximate=True)

def _silu(x):
    return jax.nn.silu(x)

def _sigmoid(x):
    return jax.nn.sigmoid(x)

def _layernorm(x, axis=-1, eps=1e-05):
    m = jnp.mean(x, axis=axis, keepdims=True)
    v = jnp.var(x, axis=axis, keepdims=True)
    return (x - m) / jnp.sqrt(v + eps)

def _scatter_add(tgt, idx, src, axis=0):
    return tgt.at[idx].add(src)

def _segment_sum(src, seg, n):
    return jax.ops.segment_sum(src, seg, n)
kernel_name = 'mk_macaron_d2_jaxref_r8_d2c130'

def setup_inputs(seed: int=0):
    np.random.seed(seed)
    _w = jnp.asarray

    def _L0_attn_setup():
        import jax, jax.numpy as jnp
        import numpy as np
        D_CONV = 4
        CHUNK = 64

        def segsum(x):
            T = x.shape[-1]
            strict = jnp.tril(jnp.ones((T, T), dtype=bool), -1)
            xr = jnp.where(strict, x[..., :, None], 0.0)
            x_segsum = jnp.cumsum(xr, axis=-2)
            return jnp.where(jnp.tril(jnp.ones((T, T), dtype=bool)), x_segsum, -jnp.inf)

        def ssd(x, A, B, C, chunk):
            b, s, h, p = x.shape
            c = s // chunk
            x = x.reshape(b, c, chunk, h, p)
            B = B.reshape(b, c, chunk, h, -1)
            C = C.reshape(b, c, chunk, h, -1)
            A = A.reshape(b, c, chunk, h).transpose(0, 3, 1, 2)
            A_cumsum = jnp.cumsum(A, axis=-1)
            L = jnp.exp(segsum(A))
            Y_diag = jnp.einsum('bclhn,bcshn,bhcls,bcshp->bclhp', C, B, L, x)
            decay_states = jnp.exp(A_cumsum[..., -1:] - A_cumsum)
            states = jnp.einsum('bclhn,bhcl,bclhp->bchpn', B, decay_states, x)
            states = jnp.concatenate([jnp.zeros_like(states[:, :1]), states], axis=1)
            A_last = jnp.pad(A_cumsum[..., -1], ((0, 0), (0, 0), (1, 0)))
            decay_chunk = jnp.exp(segsum(A_last))
            states = jnp.einsum('bhzc,bchpn->bzhpn', decay_chunk, states)[:, :-1]
            Y_off = jnp.einsum('bclhn,bchpn,bhcl->bclhp', C, states, jnp.exp(A_cumsum))
            return (Y_diag + Y_off).reshape(b, s, h, p)
        key = jax.random.key(seed)
        ks = jax.random.split(key, 6)
        d_model, d_state, d_inner, n_heads = (128, 128, 128, 16)
        d_in_proj = 2 * d_state + d_inner + n_heads
        d_conv_c = 2 * d_state + d_inner
        b, s = (4, 512)

        def xavier(k, shape):
            bnd = float(np.sqrt(6.0 / (shape[0] + shape[1])))
            return jax.random.uniform(k, shape, minval=-bnd, maxval=bnd, dtype=jnp.float32)
        return {'x': jax.random.normal(ks[0], (b, s, d_model), dtype=jnp.float32), 'W_in': xavier(ks[1], (d_in_proj, d_model)), 'conv_w': jax.random.uniform(ks[2], (d_conv_c, D_CONV), minval=-0.8, maxval=0.8, dtype=jnp.float32), 'conv_b': jnp.zeros((d_conv_c,), dtype=jnp.float32), 'A_param': jax.random.uniform(ks[3], (16,), minval=-0.01, maxval=0.01, dtype=jnp.float32), 'dt_bias': jax.random.uniform(ks[4], (16,), minval=-0.1, maxval=0.1, dtype=jnp.float32), 'W_out': xavier(ks[5], (d_model, d_inner))}
    _L0_attn_in = _L0_attn_setup()

    def _L0_ffn_setup():
        import jax, jax.numpy as jnp
        import numpy as np
        D_MODEL = 128
        N_EXPERTS = 8
        TOP_K = 2
        FFN_HIDDEN = 4 * D_MODEL
        key = jax.random.key(seed)
        ks = jax.random.split(key, 6)

        def xavier(k, shape):
            fan_in, fan_out = (shape[-2], shape[-1])
            lim = jnp.sqrt(6.0 / (fan_in + fan_out))
            return jax.random.uniform(k, shape, jnp.float32, -lim, lim)
        x = jax.random.normal(ks[0], (4, 256, D_MODEL), jnp.float32)
        w_gate = xavier(ks[1], (N_EXPERTS, D_MODEL))
        W1 = xavier(ks[2], (N_EXPERTS, D_MODEL, FFN_HIDDEN))
        b1 = jnp.zeros((N_EXPERTS, FFN_HIDDEN), jnp.float32)
        W2 = xavier(ks[3], (N_EXPERTS, FFN_HIDDEN, D_MODEL))
        b2 = jnp.zeros((N_EXPERTS, D_MODEL), jnp.float32)
        return {'x': x, 'w_gate': w_gate, 'W1': W1, 'b1': b1, 'W2': W2, 'b2': b2}
    _L0_ffn_in = _L0_ffn_setup()

    def _L1_attn_setup():
        import jax, jax.numpy as jnp
        import numpy as np
        EPS = 1e-12

        def _l2norm(t):
            n = jnp.linalg.norm(t, axis=-1, keepdims=True)
            return t / jnp.maximum(n, EPS)
        key = jax.random.key(seed)
        kx, kq, kk, kv = jax.random.split(key, 4)
        B, N, D = (8, 512, 128)
        s = 1.0 / np.sqrt(D)
        return {'x': jax.random.normal(kx, (B, N, D), dtype=jnp.float32), 'W_q': jax.random.normal(kq, (D, D), dtype=jnp.float32) * s, 'W_k': jax.random.normal(kk, (D, D), dtype=jnp.float32) * s, 'W_v': jax.random.normal(kv, (D, D), dtype=jnp.float32) * s}
    _L1_attn_in = _L1_attn_setup()

    def _L1_ffn_setup():
        import jax, jax.numpy as jnp
        import numpy as np
        DIM = 128
        DEPTH = 2
        HEADS = 8
        DIM_HEAD = 64
        WINDOW = 64
        INNER = HEADS * DIM_HEAD
        HID = int(DIM * 4 * 2 / 3)
        B, N = (2, 1024)
        QK_SCALE = 8.0

        def shift_token(t):
            t1, t2 = jnp.split(t, 2, axis=-1)
            t2 = jnp.pad(t2, ((0, 0), (1, 0), (0, 0)))[:, :-1]
            return jnp.concatenate([t1, t2], axis=-1)

        def l2norm(t):
            return t / jnp.clip(jnp.linalg.norm(t, axis=-1, keepdims=True), 1e-12)

        def rotate_half(x):
            x1, x2 = jnp.split(x, 2, axis=-1)
            return jnp.concatenate([-x2, x1], axis=-1)

        def rotary_xpos(q, k):
            n = q.shape[-2]
            half_idx = jnp.arange(0, DIM_HEAD, 2, dtype=jnp.float32)
            inv_freq = 1.0 / 10000.0 ** (half_idx / DIM_HEAD)
            t = jnp.arange(n, dtype=jnp.float32)
            freqs = t[:, None] * inv_freq[None, :]
            freqs = jnp.concatenate([freqs, freqs], axis=-1)
            base = (half_idx + 0.4 * DIM_HEAD) / (1.4 * DIM_HEAD)
            power = (t - n // 2) / float(WINDOW // 2)
            scale = base[None, :] ** power[:, None]
            scale = jnp.concatenate([scale, scale], axis=-1)
            cos, sin = (jnp.cos(freqs), jnp.sin(freqs))
            q = q * cos * scale + rotate_half(q) * sin * scale
            k = k * cos / scale + rotate_half(k) * sin / scale
            return (q, k)

        def local_attention(q, k, v):
            b, h, n, d = q.shape
            w = n // WINDOW
            bq = q.reshape(b, h, w, WINDOW, d) * QK_SCALE
            bk = k.reshape(b, h, w, WINDOW, d)
            bv = v.reshape(b, h, w, WINDOW, d)

            def look_around(t):
                p = jnp.pad(t, ((0, 0), (0, 0), (1, 0), (0, 0), (0, 0)))
                return jnp.concatenate([p[:, :, :w], p[:, :, 1:]], axis=3)
            bk, bv = (look_around(bk), look_around(bv))
            bt = jnp.arange(n).reshape(w, WINDOW)
            btp = jnp.pad(bt, ((1, 0), (0, 0)), constant_values=-1)
            btk = jnp.concatenate([btp[:w], btp[1:]], axis=1)
            sim = jnp.einsum('bhwid,bhwjd->bhwij', bq, bk)
            i = bt[:, :, None]
            j = btk[:, None, :]
            mask = (i < j) | (i > j + WINDOW) | (j == -1)
            sim = jnp.where(mask, -jnp.finfo(sim.dtype).max, sim)
            attn = jax.nn.softmax(sim, axis=-1)
            out = jnp.einsum('bhwij,bhwjd->bhwid', attn, bv)
            return out.reshape(b, h, n, d)

        def _layer(x, wqkv, qs, ksc, wo, lg, lb, w1, b1, w2, b2):
            b, n, _ = x.shape
            h = shift_token(x)
            qkv = h @ wqkv
            q, k, v = jnp.split(qkv, 3, axis=-1)
            to_heads = lambda t: t.reshape(b, n, HEADS, DIM_HEAD).transpose(0, 2, 1, 3)
            q, k, v = (to_heads(q), to_heads(k), to_heads(v))
            q = l2norm(q) * qs
            k = l2norm(k) * ksc
            q, k = rotary_xpos(q, k)
            o = local_attention(q, k, v)
            o = o.transpose(0, 2, 1, 3).reshape(b, n, INNER)
            x = x + o @ wo
            h = shift_token(x)
            mu = h.mean(-1, keepdims=True)
            var = h.var(-1, keepdims=True)
            h = (h - mu) / jnp.sqrt(var + 1e-05) * lg + lb
            h = h @ w1 + b1
            a, g = jnp.split(h, 2, axis=-1)
            h = a * jax.nn.gelu(g, approximate=False)
            x = x + h @ w2 + b2
            return x
        key = jax.random.key(seed)
        ks = jax.random.split(key, 6)
        return {'x': jax.random.normal(ks[0], (B, N, DIM), jnp.float32), 'wqkv': jax.random.normal(ks[1], (DEPTH, DIM, 3 * INNER), jnp.float32) * 0.02, 'q_scale': jnp.ones((DEPTH, DIM_HEAD), jnp.float32), 'k_scale': jnp.ones((DEPTH, DIM_HEAD), jnp.float32), 'wo': jax.random.normal(ks[2], (DEPTH, INNER, DIM), jnp.float32) * 0.02, 'ln_g': jnp.ones((DEPTH, DIM), jnp.float32), 'ln_b': jnp.zeros((DEPTH, DIM), jnp.float32), 'w1': jax.random.normal(ks[3], (DEPTH, DIM, 2 * HID), jnp.float32) * 0.02, 'b1': jnp.zeros((DEPTH, 2 * HID), jnp.float32), 'w2': jax.random.normal(ks[4], (DEPTH, HID, DIM), jnp.float32) * 0.02, 'b2': jnp.zeros((DEPTH, DIM), jnp.float32)}
    _L1_ffn_in = _L1_ffn_setup()
    _d = {'L0_attn_x': _L0_attn_in['x'], 'L0_attn_W_in': _L0_attn_in['W_in'], 'L0_attn_conv_w': _L0_attn_in['conv_w'], 'L0_attn_conv_b': _L0_attn_in['conv_b'], 'L0_attn_A_param': _L0_attn_in['A_param'], 'L0_attn_dt_bias': _L0_attn_in['dt_bias'], 'L0_attn_W_out': _L0_attn_in['W_out'], 'L0_ffn_w_gate': _L0_ffn_in['w_gate'], 'L0_ffn_W1': _L0_ffn_in['W1'], 'L0_ffn_b1': _L0_ffn_in['b1'], 'L0_ffn_W2': _L0_ffn_in['W2'], 'L0_ffn_b2': _L0_ffn_in['b2'], 'L1_attn_W_q': _L1_attn_in['W_q'], 'L1_attn_W_k': _L1_attn_in['W_k'], 'L1_attn_W_v': _L1_attn_in['W_v'], 'L1_ffn_wqkv': _L1_ffn_in['wqkv'], 'L1_ffn_q_scale': _L1_ffn_in['q_scale'], 'L1_ffn_k_scale': _L1_ffn_in['k_scale'], 'L1_ffn_wo': _L1_ffn_in['wo'], 'L1_ffn_ln_g': _L1_ffn_in['ln_g'], 'L1_ffn_ln_b': _L1_ffn_in['ln_b'], 'L1_ffn_w1': _L1_ffn_in['w1'], 'L1_ffn_b1': _L1_ffn_in['b1'], 'L1_ffn_w2': _L1_ffn_in['w2'], 'L1_ffn_b2': _L1_ffn_in['b2']}
    _x0 = _d['L0_attn_x']
    _d['L0_attn_x'] = jax.random.normal(jax.random.fold_in(jax.random.key(seed), 1), (8, 512, 128), dtype=_x0.dtype)
    del _x0
    return _d

def reference(L0_attn_x, L0_attn_W_in, L0_attn_conv_w, L0_attn_conv_b, L0_attn_A_param, L0_attn_dt_bias, L0_attn_W_out, L0_ffn_w_gate, L0_ffn_W1, L0_ffn_b1, L0_ffn_W2, L0_ffn_b2, L1_attn_W_q, L1_attn_W_k, L1_attn_W_v, L1_ffn_wqkv, L1_ffn_q_scale, L1_ffn_k_scale, L1_ffn_wo, L1_ffn_ln_g, L1_ffn_ln_b, L1_ffn_w1, L1_ffn_b1, L1_ffn_w2, L1_ffn_b2):

    def _L0_attn_ref(x, W_in, conv_w, conv_b, A_param, dt_bias, W_out):
        import jax, jax.numpy as jnp
        import numpy as np
        D_CONV = 4
        CHUNK = 64

        def segsum(x):
            T = x.shape[-1]
            strict = jnp.tril(jnp.ones((T, T), dtype=bool), -1)
            xr = jnp.where(strict, x[..., :, None], 0.0)
            x_segsum = jnp.cumsum(xr, axis=-2)
            return jnp.where(jnp.tril(jnp.ones((T, T), dtype=bool)), x_segsum, -jnp.inf)

        def ssd(x, A, B, C, chunk):
            b, s, h, p = x.shape
            c = s // chunk
            x = x.reshape(b, c, chunk, h, p)
            B = B.reshape(b, c, chunk, h, -1)
            C = C.reshape(b, c, chunk, h, -1)
            A = A.reshape(b, c, chunk, h).transpose(0, 3, 1, 2)
            A_cumsum = jnp.cumsum(A, axis=-1)
            L = jnp.exp(segsum(A))
            Y_diag = jnp.einsum('bclhn,bcshn,bhcls,bcshp->bclhp', C, B, L, x)
            decay_states = jnp.exp(A_cumsum[..., -1:] - A_cumsum)
            states = jnp.einsum('bclhn,bhcl,bclhp->bchpn', B, decay_states, x)
            states = jnp.concatenate([jnp.zeros_like(states[:, :1]), states], axis=1)
            A_last = jnp.pad(A_cumsum[..., -1], ((0, 0), (0, 0), (1, 0)))
            decay_chunk = jnp.exp(segsum(A_last))
            states = jnp.einsum('bhzc,bchpn->bzhpn', decay_chunk, states)[:, :-1]
            Y_off = jnp.einsum('bclhn,bchpn,bhcl->bclhp', C, states, jnp.exp(A_cumsum))
            return (Y_diag + Y_off).reshape(b, s, h, p)
        b, src_len, d_model = x.shape
        n_heads = A_param.shape[0]
        d_conv_c = conv_w.shape[0]
        d_inner = W_out.shape[1]
        d_state = (d_conv_c - d_inner) // 2
        pad = -src_len % CHUNK
        xs = jnp.pad(x, ((0, 0), (0, pad), (0, 0)))
        s = xs.shape[1]
        proj = xs @ W_in.T
        xBC, dt = (proj[..., :d_conv_c], proj[..., d_conv_c:])
        xp = jnp.pad(xBC, ((0, 0), (D_CONV - 1, 0), (0, 0)))
        conv_out = sum((xp[:, k:k + s, :] * conv_w[:, k] for k in range(D_CONV))) + conv_b
        C_ = conv_out[..., :d_state]
        B_ = conv_out[..., d_state:2 * d_state]
        xin = conv_out[..., 2 * d_state:]
        dt = jax.nn.softplus(dt + dt_bias)
        Ch = C_.reshape(b, s, n_heads, -1)
        Bh = B_.reshape(b, s, n_heads, -1)
        xh = xin.reshape(b, s, n_heads, -1)
        A = A_param * dt
        cumA = jnp.cumsum(A, axis=1)
        norm = (jnp.exp(cumA) * jnp.cumsum(jnp.exp(-cumA), axis=1))[..., None]
        Y = ssd(xh, A, Bh, Ch, CHUNK)
        out = Y[0] / norm
        out = out.reshape(b, s, -1) @ W_out.T
        return out[:, :src_len]

    def _L0_ffn_ref(x, w_gate, W1, b1, W2, b2):
        import jax, jax.numpy as jnp
        import numpy as np
        D_MODEL = 128
        N_EXPERTS = 8
        TOP_K = 2
        FFN_HIDDEN = 4 * D_MODEL
        B, S, D = x.shape
        flat_x = x.reshape(-1, D)
        gate = jax.nn.softmax(flat_x @ w_gate.T, axis=-1)
        topk_scores, topk_idx = jax.lax.top_k(gate, TOP_K)
        cw = (jax.nn.one_hot(topk_idx, N_EXPERTS, dtype=flat_x.dtype) * topk_scores[..., None]).sum(axis=1)
        h = jax.nn.gelu(jnp.einsum('td,edh->teh', flat_x, W1) + b1, approximate=False)
        y = jnp.einsum('teh,ehd->ted', h, W2) + b2
        out = jnp.einsum('ted,te->td', y, cw)
        return out.reshape(B, S, D)

    def _L1_attn_ref(x, W_q, W_k, W_v):
        import jax, jax.numpy as jnp
        import numpy as np
        EPS = 1e-12

        def _l2norm(t):
            n = jnp.linalg.norm(t, axis=-1, keepdims=True)
            return t / jnp.maximum(n, EPS)
        Q = _l2norm(jnp.einsum('bnd,ed->bne', x, W_q))
        K = _l2norm(jnp.einsum('bnd,ed->bne', x, W_k))
        V = jnp.einsum('bnd,ed->bne', x, W_v)
        C = x.shape[1]
        global_feat = jnp.sum(K * V, axis=1, keepdims=True) / C
        return Q * global_feat

    def _L1_ffn_ref(x, wqkv, q_scale, k_scale, wo, ln_g, ln_b, w1, b1, w2, b2):
        import jax, jax.numpy as jnp
        import numpy as np
        DIM = 128
        DEPTH = 2
        HEADS = 8
        DIM_HEAD = 64
        WINDOW = 64
        INNER = HEADS * DIM_HEAD
        HID = int(DIM * 4 * 2 / 3)
        B, N = (2, 1024)
        QK_SCALE = 8.0

        def shift_token(t):
            t1, t2 = jnp.split(t, 2, axis=-1)
            t2 = jnp.pad(t2, ((0, 0), (1, 0), (0, 0)))[:, :-1]
            return jnp.concatenate([t1, t2], axis=-1)

        def l2norm(t):
            return t / jnp.clip(jnp.linalg.norm(t, axis=-1, keepdims=True), 1e-12)

        def rotate_half(x):
            x1, x2 = jnp.split(x, 2, axis=-1)
            return jnp.concatenate([-x2, x1], axis=-1)

        def rotary_xpos(q, k):
            n = q.shape[-2]
            half_idx = jnp.arange(0, DIM_HEAD, 2, dtype=jnp.float32)
            inv_freq = 1.0 / 10000.0 ** (half_idx / DIM_HEAD)
            t = jnp.arange(n, dtype=jnp.float32)
            freqs = t[:, None] * inv_freq[None, :]
            freqs = jnp.concatenate([freqs, freqs], axis=-1)
            base = (half_idx + 0.4 * DIM_HEAD) / (1.4 * DIM_HEAD)
            power = (t - n // 2) / float(WINDOW // 2)
            scale = base[None, :] ** power[:, None]
            scale = jnp.concatenate([scale, scale], axis=-1)
            cos, sin = (jnp.cos(freqs), jnp.sin(freqs))
            q = q * cos * scale + rotate_half(q) * sin * scale
            k = k * cos / scale + rotate_half(k) * sin / scale
            return (q, k)

        def local_attention(q, k, v):
            b, h, n, d = q.shape
            w = n // WINDOW
            bq = q.reshape(b, h, w, WINDOW, d) * QK_SCALE
            bk = k.reshape(b, h, w, WINDOW, d)
            bv = v.reshape(b, h, w, WINDOW, d)

            def look_around(t):
                p = jnp.pad(t, ((0, 0), (0, 0), (1, 0), (0, 0), (0, 0)))
                return jnp.concatenate([p[:, :, :w], p[:, :, 1:]], axis=3)
            bk, bv = (look_around(bk), look_around(bv))
            bt = jnp.arange(n).reshape(w, WINDOW)
            btp = jnp.pad(bt, ((1, 0), (0, 0)), constant_values=-1)
            btk = jnp.concatenate([btp[:w], btp[1:]], axis=1)
            sim = jnp.einsum('bhwid,bhwjd->bhwij', bq, bk)
            i = bt[:, :, None]
            j = btk[:, None, :]
            mask = (i < j) | (i > j + WINDOW) | (j == -1)
            sim = jnp.where(mask, -jnp.finfo(sim.dtype).max, sim)
            attn = jax.nn.softmax(sim, axis=-1)
            out = jnp.einsum('bhwij,bhwjd->bhwid', attn, bv)
            return out.reshape(b, h, n, d)

        def _layer(x, wqkv, qs, ksc, wo, lg, lb, w1, b1, w2, b2):
            b, n, _ = x.shape
            h = shift_token(x)
            qkv = h @ wqkv
            q, k, v = jnp.split(qkv, 3, axis=-1)
            to_heads = lambda t: t.reshape(b, n, HEADS, DIM_HEAD).transpose(0, 2, 1, 3)
            q, k, v = (to_heads(q), to_heads(k), to_heads(v))
            q = l2norm(q) * qs
            k = l2norm(k) * ksc
            q, k = rotary_xpos(q, k)
            o = local_attention(q, k, v)
            o = o.transpose(0, 2, 1, 3).reshape(b, n, INNER)
            x = x + o @ wo
            h = shift_token(x)
            mu = h.mean(-1, keepdims=True)
            var = h.var(-1, keepdims=True)
            h = (h - mu) / jnp.sqrt(var + 1e-05) * lg + lb
            h = h @ w1 + b1
            a, g = jnp.split(h, 2, axis=-1)
            h = a * jax.nn.gelu(g, approximate=False)
            x = x + h @ w2 + b2
            return x
        for l in range(DEPTH):
            x = _layer(x, wqkv[l], q_scale[l], k_scale[l], wo[l], ln_g[l], ln_b[l], w1[l], b1[l], w2[l], b2[l])
        return x
    x = L0_attn_x
    x = x + 0.5 * _L0_ffn_ref(_layernorm(x, axis=-1), L0_ffn_w_gate, L0_ffn_W1, L0_ffn_b1, L0_ffn_W2, L0_ffn_b2)
    x = x + _L0_attn_ref(_layernorm(x, axis=-1), L0_attn_W_in, L0_attn_conv_w, L0_attn_conv_b, L0_attn_A_param, L0_attn_dt_bias, L0_attn_W_out)
    x = x + 0.5 * _L0_ffn_ref(_layernorm(x, axis=-1), L0_ffn_w_gate, L0_ffn_W1, L0_ffn_b1, L0_ffn_W2, L0_ffn_b2)
    x = x + 0.5 * _L1_ffn_ref(_layernorm(x, axis=-1), L1_ffn_wqkv, L1_ffn_q_scale, L1_ffn_k_scale, L1_ffn_wo, L1_ffn_ln_g, L1_ffn_ln_b, L1_ffn_w1, L1_ffn_b1, L1_ffn_w2, L1_ffn_b2)
    x = x + _L1_attn_ref(_layernorm(x, axis=-1), L1_attn_W_q, L1_attn_W_k, L1_attn_W_v)
    x = x + 0.5 * _L1_ffn_ref(_layernorm(x, axis=-1), L1_ffn_wqkv, L1_ffn_q_scale, L1_ffn_k_scale, L1_ffn_wo, L1_ffn_ln_g, L1_ffn_ln_b, L1_ffn_w1, L1_ffn_b1, L1_ffn_w2, L1_ffn_b2)
    return x

_drawn_inputs = setup_inputs


def setup_inputs(seed=0):
    import zlib

    import numpy as np

    out = dict(_drawn_inputs(seed))
    spreads = {'L0_attn_conv_b': (0.0, 0.1),
     'L0_ffn_b1': (0.0, 0.1),
     'L0_ffn_b2': (0.0, 0.1),
     'L1_ffn_q_scale': (1.0, 0.6),
     'L1_ffn_k_scale': (1.0, 0.6),
     'L1_ffn_ln_g': (1.0, 0.6),
     'L1_ffn_ln_b': (0.0, 0.8),
     'L1_ffn_b1': (0.0, 0.8),
     'L1_ffn_b2': (0.0, 0.1)}
    factors = {'L0_attn_dt_bias': 35.996,
     'L1_attn_W_q': 64.0,
     'L1_attn_W_k': 189.573,
     'L1_attn_W_v': 178.497,
     'L1_ffn_wqkv': 3.077,
     'L1_ffn_wo': 3.071,
     'L1_ffn_w1': 5.762,
     'L1_ffn_w2': 5.634}
    for name, (base, spread) in spreads.items():
        noise = np.random.default_rng([zlib.crc32(name.encode()), seed]).standard_normal(out[name].shape)
        drawn = base * np.exp(spread * noise) if base else spread * noise
        out[name] = jnp.asarray(drawn.astype(out[name].dtype))
    for name, factor in factors.items():
        out[name] = (out[name] * factor).astype(out[name].dtype)
    return out
```

```python
import math
from contextlib import ExitStack

import numpy as np
import concourse.bass as bass
from concourse import mybir

F32 = mybir.dt.float32
F32R = mybir.dt.float32r
BF16 = mybir.dt.bfloat16
ALU = mybir.AluOpType
ACT = mybir.ActivationFunctionType
AX = mybir.AxisListType

P = 128
NB = 8
T = 512
TT = T // P
NE = 8
HC = 4
NH = 16
NS = 8
CHUNK = 64
WIN = 64
NW = T // WIN
HP = 4
DH = 64
HID = 341
MC = 3
MW = 114
LN_EPS = 1e-5
MASKED = -1e30
SS_SCALE = 65536.0


def mm3(pe, out, w, x, start=True, stop=True):
    (wh, wl), (xh, xl) = w, x
    pe.matmul(out, wh, xh, start=start, stop=False)
    pe.matmul(out, wl, xh, start=False, stop=False)
    return pe.matmul(out, wh, xl, start=False, stop=stop)


class Phase(ExitStack):

    def __init__(self, nc):
        super().__init__()
        self.nc, self.sems = nc, []
        self.callback(self.clear)

    def sem(self, name):
        self.sems.append(self.nc.alloc_semaphore(name=name))
        return self.sems[-1]

    def clear(self):
        if self.sems:
            self.nc.clear_and_free_semaphores(self.sems)
            self.nc.all_engine_barrier()


class Mem:
    pass


def seq(t, b):
    return t[:, bass.ds(b * T, T)]


def split_weights(dve, pairs, sem, count):
    for raw, hi, lo in pairs:
        dve.tensor_copy(hi, raw).then_inc(sem, 1)
        count += 1
        dve.wait_ge(sem, count)
        dve.tensor_tensor(lo, raw, hi, ALU.subtract).then_inc(sem, 1)
        count += 1
    return count


def load_phase(nc, m, x_in, consts):
    with Phase(nc) as c:
        xin = c.enter_context(nc.sbuf_tensor("x_tokens", [P, NB * TT, P], F32))
        consts_in = c.sem("consts_in")
        x_tokens_in = c.sem("x_tokens_in")
        turned = c.sem("x_turned")
        stored = c.sem("x_stored")
        made = c.sem("load_made")
        block = c.enter_context(nc.Block())

        @block.sync
        def _(sp):
            sp.dma_start(m.ident[:], consts["ident"]).then_inc(consts_in, 16)
            sp.dma_start(xin[:], x_in.rearrange("b (t p) d -> p (b t) d", p=P)).then_inc(x_tokens_in, 16)
            sp.dma_start(m.center[:], consts["center"]).then_inc(consts_in, 16)
            sp.wait_ge(consts_in, 32)

        @block.vector
        def _(dve):
            dve.memset(m.x[:, NB * T:], 0.0)
            dve.memset(m.mean_of[:], 1.0 / P)
            dve.memset(m.eps[:], LN_EPS)

        @block.tensor
        def _(pe):
            pe.wait_ge(consts_in, 32)
            pe.wait_ge(x_tokens_in, 16)
            for b in range(NB):
                if b >= 2:
                    pe.wait_ge(stored, b - 1)
                for t in range(TT):
                    tr = pe.transpose(m.ps[:, b % 2, t * P:(t + 1) * P], xin[:, b * TT + t, :], m.ident[:])
                tr.then_inc(turned, 1)

        @block.scalar
        def _(act):
            for b in range(NB):
                act.wait_ge(turned, b + 1)
                act.activation(m.x[:, b * T:(b + 1) * T], m.ps[:, b % 2, :], ACT.Copy).then_inc(stored, 1)


def store_phase(nc, m, out):
    with Phase(nc) as c:
        xout = c.enter_context(nc.sbuf_tensor("out_tokens", [P, NB * TT, P], F32))
        turned = c.sem("out_turned")
        ready = c.sem("out_ready")
        written = c.sem("out_written")
        block = c.enter_context(nc.Block())
        dst = out.rearrange("b (t p) d -> p (b t) d", p=P)

        @block.tensor
        def _(pe):
            for b in range(NB):
                if b >= 2:
                    pe.wait_ge(ready, b - 1)
                for t in range(TT):
                    col = b * T + t * P
                    tr = pe.transpose(m.ps[:, b % 2, t * P:(t + 1) * P], m.x[:, col:col + P], m.ident[:])
                tr.then_inc(turned, 1)

        @block.scalar
        def _(act):
            for b in range(NB):
                act.wait_ge(turned, b + 1)
                act.activation(xout[:, b * TT:(b + 1) * TT, :].rearrange("p t d -> p (t d)"),
                               m.ps[:, b % 2, :], ACT.Copy).then_inc(ready, 1)

        @block.sync
        def _(sp):
            for b in range(NB):
                sp.wait_ge(ready, b + 1)
                sp.dma_start(dst[:, b * TT:(b + 1) * TT, :], xout[:, b * TT:(b + 1) * TT, :]).then_inc(written, 16)
            sp.wait_ge(written, 16 * NB)


class Norm:

    def __init__(self, nc, c, m, name, cb, vb, shift=False):
        self.m, self.cb, self.vb, self.shift = m, cb, vb, shift
        sb = lambda n: c.enter_context(nc.sbuf_tensor(f"{name}_{n}", [P, T], F32))
        self.xs, self.sq, self.rstd, self.out = sb("xs"), sb("sq"), sb("rstd"), sb("xn")
        sem = lambda n: c.sem(f"{name}_{n}")
        self.taken, self.centred, self.squared = sem("taken"), sem("centred"), sem("squared")
        self.varied, self.logged, self.scaled, self.normed = sem("varied"), sem("logged"), sem("scaled"), sem("normed")
        self.zeroed = sem("zeroed")

    def start(self, eng):
        if self.shift:
            eng.memset(self.xs[P // 2:, 0:1], 0.0).then_inc(self.zeroed, 1)
            eng.wait_ge(self.zeroed, 1)

    def take(self, eng, n, src, b, after=None):
        eng.wait_ge(self.centred, n)
        if self.shift:
            eng.tensor_copy(self.xs[:P // 2, :], src[:P // 2, bass.ds(b * T, T)]).then_inc(self.taken, 1)
            eng.tensor_copy(self.xs[P // 2:, 1:], src[P // 2:, bass.ds(b * T, T - 1)]).then_inc(self.taken, 1)
        else:
            eng.tensor_copy(self.xs[:], seq(src, b)).then_inc(self.taken, 1)

    def centre(self, pe, n):
        pe.wait_ge(self.taken, (n + 1) * (1 + self.shift))
        pe.wait_ge(self.normed, n)
        pe.matmul(self.m.ps[:, self.cb, :], self.m.center[:], self.xs[:], start=True, stop=True).then_inc(self.centred, 1)

    def square(self, act, n):
        act.wait_ge(self.centred, n + 1)
        act.wait_ge(self.varied, n)
        act.activation(self.sq[:], self.m.ps[:, self.cb, :], ACT.Square).then_inc(self.squared, 1)

    def variance(self, pe, n):
        pe.wait_ge(self.squared, n + 1)
        pe.wait_ge(self.logged, n)
        pe.matmul(self.m.ps[:, self.vb, :], self.m.mean_of[:], self.sq[:], start=True, stop=True).then_inc(self.varied, 1)

    def scale(self, act, n):
        act.preload_act_table_set(EXP_LN)
        act.wait_ge(self.varied, n + 1)
        act.wait_ge(self.normed, n)
        act.activation(self.rstd[:], self.m.ps[:, self.vb, :], ACT.Ln, bias=self.m.eps[:, 0:1]).then_inc(self.logged, 1)
        act.wait_ge(self.logged, n + 1)
        act.activation(self.rstd[:], self.rstd[:], ACT.Exp, scale=-0.5).then_inc(self.scaled, 1)

    def norm(self, dve, n, out=None):
        dve.wait_ge(self.scaled, n + 1)
        dve.tensor_tensor(self.out[:] if out is None else out, self.m.ps[:, self.cb, :], self.rstd[:],
                          ALU.mult).then_inc(self.normed, 1)


def moe_phase(nc, m, app, w, cw_dram):
    NC = NE * HC
    UP = [2, 3, 4]
    YB = [5, 6]
    GB = 7
    SLOTS = 3
    LOOK = 2
    with Phase(nc) as c:
        name = f"moe{app}"
        sb = lambda n, s, d=F32: c.enter_context(nc.sbuf_tensor(f"{name}_{n}", s, d))
        sem = lambda n: c.sem(f"{name}_{n}")
        ln = Norm(nc, c, m, name + "_ln", 0, 1)
        xh, xl = sb("xh", [P, T], F32R), sb("xl", [P, T], F32R)
        g32 = sb("g32", [P, SLOTS, T])
        gh, gl = sb("gh", [P, SLOTS, T], F32R), sb("gl", [P, SLOTS, T], F32R)
        cwb = sb("cwb", [P, NE, T])
        part, acc = sb("part", [P, 2, T]), sb("acc", [P, T])
        peak, total, rtotal = sb("peak", [P, TT]), sb("total", [P, TT]), sb("rtotal", [P, TT])
        gate = sb("gate", [P, TT, NE])
        more, ties = sb("more", [P, TT, NE, NE]), sb("ties", [P, TT, NE, NE])
        rank, cw = sb("rank", [P, TT, NE]), sb("cw", [P, TT, NE])
        cwt = sb("cwt", [NE, T])
        split, up_done, gelu_done, rounded, lo_done = sem("split"), sem("up_done"), sem("gelu_done"), sem("rounded"), sem("lo_done")
        down_done, part_done, summed, x_done = sem("down_done"), sem("part_done"), sem("summed"), sem("x_done")
        logits_done, peeled, exped, gated, turned = sem("logits"), sem("peeled"), sem("exped"), sem("gated"), sem("turned")
        cwt_done, cw_out, gchain, xh_done = sem("cwt_done"), sem("cw_out"), sem("gchain"), sem("xh_done")
        wchain = sem("wchain")
        cw_in = [sem(f"cw_in{e}") for e in range(NE)]
        GSTEPS = 8
        block = c.enter_context(nc.Block())

        @block.tensor
        def _(pe):
            def logits(n):
                pe.wait_ge(ln.normed, n + 1)
                pe.wait_ge(cwt_done, n)
                for t in range(TT):
                    mm = pe.matmul(m.ps[:, GB, t * NE:(t + 1) * NE], ln.out[:, t * P:(t + 1) * P], w.gate[:],
                                   start=True, stop=True)
                mm.then_inc(logits_done, 1)

            def turn(n):
                pe.wait_ge(gated, n + 1)
                for t in range(TT):
                    tr = pe.transpose(m.ps[:NE, GB, t * P:(t + 1) * P], cw[:, t, :], m.ident[:])
                tr.then_inc(turned, 1)

            def up(b, i):
                pe.wait_ge(rounded, b * NC + i + 1)
                cols = slice((i % HC) * P, (i % HC + 1) * P)
                mm3(pe, m.ps[:, UP[i % 3], :], (w.w1h[:, i // HC, cols], w.w1l[:, i // HC, cols]),
                    (xh[:], xl[:])).then_inc(up_done, 1)

            def down(b, i):
                e, k = i // HC, i % HC
                pe.wait_ge(lo_done, b * NC + i + 1 + SLOTS)
                if k == 0:
                    pe.wait_ge(part_done, b * NE + e + 1)
                s = i % SLOTS
                mm3(pe, m.ps[:, YB[e % 2], :], (w.w2h[:, e, k, :], w.w2l[:, e, k, :]), (gh[:, s, :], gl[:, s, :]),
                    start=(k == 0), stop=(k == HC - 1)).then_inc(down_done, 1)

            ln.centre(pe, 0)
            ln.variance(pe, 0)
            logits(0)
            turn(0)
            with pe.Fori(0, NB) as b:
                pe.wait_ge(split, b + 1)
                for i in range(NC + LOOK):
                    if i < NC:
                        up(b, i)
                    if i >= LOOK:
                        down(b, i - LOOK)
                    if i == 6:
                        ln.centre(pe, b + 1)
                    if i == 9:
                        ln.variance(pe, b + 1)
                    if i == 14:
                        logits(b + 1)
                    if i == 22:
                        turn(b + 1)

        @block.scalar
        def _(act):
            def exps(n):
                act.wait_ge(peeled, n + 1)
                act.wait_ge(gated, n)
                act.activation(gate[:], gate[:], ACT.Exp).then_inc(exped, 1)

            act.sem_inc(rounded, 3)
            ln.square(act, 0)
            ln.scale(act, 0)
            exps(0)
            with act.Fori(0, NB) as b:
                for i in range(NC):
                    s = i % SLOTS
                    e, k = i // HC, i % HC
                    act.wait_ge(up_done, b * NC + i + 1)
                    act.wait_ge(lo_done, b * NC + i + 1)
                    act.activation(g32[:, s, :], m.ps[:, UP[i % 3], :], ACT.Gelu,
                                   bias=w.b1[:, i:i + 1]).then_inc(gelu_done, 1)
                    act.wait_ge(down_done, b * NC + i + 1)
                    act.activation(gh[:, s, :], m.ps[:, UP[i % 3], :], ACT.Gelu,
                                   bias=w.b1[:, i:i + 1]).then_inc(rounded, 1)
                    if i == 6:
                        ln.square(act, b + 1)
                    if i == 9:
                        ln.scale(act, b + 1)
                    if i == 17:
                        exps(b + 1)

        @block.vector
        def _(dve):
            def gates(n):
                l3 = m.ps[:, GB, :TT * NE].rearrange("p (t e) -> p t e", e=NE)
                dve.wait_ge(logits_done, n + 1)
                dve.tensor_reduce(peak[:], l3, AX.X, ALU.max).then_inc(gchain, 1)
                dve.wait_ge(gchain, n * GSTEPS + 1)
                dve.tensor_tensor(gate[:], l3, peak[:].unsqueeze(2).to_broadcast([P, TT, NE]),
                                  ALU.subtract).then_inc(peeled, 1)

            def weights(n):
                a = gate[:].unsqueeze(2).to_broadcast([P, TT, NE, NE])
                z = gate[:].unsqueeze(3).to_broadcast([P, TT, NE, NE])
                dve.wait_ge(exped, n + 1)
                dve.tensor_reduce(total[:], gate[:], AX.X, ALU.add).then_inc(gchain, 1)
                dve.tensor_tensor(more[:], a, z, ALU.is_gt).then_inc(gchain, 1)
                dve.tensor_tensor(ties[:], a, z, ALU.is_ge).then_inc(gchain, 1)
                dve.wait_ge(gchain, n * GSTEPS + 4)
                dve.reciprocal(rtotal[:], total[:]).then_inc(gchain, 1)
                dve.tensor_tensor(ties[:], ties[:], m.before[:].unsqueeze(1).to_broadcast([P, TT, NE, NE]),
                                  ALU.mult).then_inc(gchain, 1)
                dve.wait_ge(gchain, n * GSTEPS + 6)
                dve.tensor_tensor(more[:], more[:], ties[:], ALU.max).then_inc(gchain, 1)
                dve.wait_ge(gchain, n * GSTEPS + 7)
                dve.tensor_reduce(rank[:], more[:], AX.X, ALU.add).then_inc(gchain, 1)
                dve.wait_ge(gchain, n * GSTEPS + 8)
                dve.wait_ge(turned, n)
                dve.scalar_tensor_tensor(out=cw[:], in0=rank[:], scalar=2.0, in1=gate[:], op0=ALU.is_lt,
                                         op1=ALU.mult).then_inc(wchain, 1)
                dve.wait_ge(wchain, n + 1)
                dve.tensor_tensor(cw[:], cw[:], rtotal[:].unsqueeze(2).to_broadcast([P, TT, NE]),
                                  ALU.mult).then_inc(gated, 1)

            def keep_cwt(n):
                dve.wait_ge(turned, n + 1)
                dve.wait_ge(cw_out, 16 * n)
                dve.tensor_copy(cwt[:], m.ps[:NE, GB, :]).then_inc(cwt_done, 1)

            def halves(n):
                dve.wait_ge(up_done, n * NC)
                dve.wait_ge(ln.normed, n + 1)
                dve.tensor_copy(xh[:], ln.out[:]).then_inc(xh_done, 1)
                dve.wait_ge(xh_done, n + 1)
                dve.tensor_tensor(xl[:], ln.out[:], xh[:], ALU.subtract).then_inc(split, 1)

            def take_part(b, e):
                dve.wait_ge(down_done, b * NC + HC * (e + 1) + SLOTS)
                dve.wait_ge(cw_in[e], 16 * (b + 1))
                if e >= 2:
                    dve.wait_ge(summed, b * (NE - 1) + e - 1)
                else:
                    dve.wait_ge(summed, b * (NE - 1))
                dve.scalar_tensor_tensor(out=part[:, e % 2, :], in0=m.ps[:, YB[e % 2], :], scalar=w.b2[:, e:e + 1],
                                         in1=cwb[:, e, :], op0=ALU.add, op1=ALU.mult).then_inc(part_done, 1)

            dve.sem_inc(lo_done, SLOTS)
            dve.sem_inc(down_done, SLOTS)
            dve.sem_inc(part_done, 2)
            ln.norm(dve, 0)
            gates(0)
            weights(0)
            keep_cwt(0)
            halves(0)
            with dve.Fori(0, NB) as b:
                for i in range(NC + 3):
                    if i < NC:
                        s = i % SLOTS
                        dve.wait_ge(rounded, b * NC + i + 1 + 3)
                        dve.tensor_tensor(gl[:, s, :], g32[:, s, :], gh[:, s, :], ALU.subtract).then_inc(lo_done, 1)
                    if i >= 6 and (i - 6) % HC == 0 and (i - 6) // HC < NE:
                        take_part(b, (i - 6) // HC)
                    if i == 11:
                        ln.norm(dve, b + 1)
                    if i == 16:
                        gates(b + 1)
                    if i == 19:
                        weights(b + 1)
                    if i == 24:
                        keep_cwt(b + 1)
                halves(b + 1)
                dve.wait_ge(summed, (b + 1) * (NE - 1))
                dve.scalar_tensor_tensor(out=seq(m.x, b), in0=acc[:], scalar=0.5, in1=seq(m.x, b), op0=ALU.mult,
                                         op1=ALU.add).then_inc(x_done, 1)

        @block.gpsimd
        def _(pool):
            ln.take(pool, 0, m.x, 0)
            with pool.Fori(0, NB) as b:
                ln.take(pool, b + 1, m.x, b + 1)
                for e in range(1, NE):
                    pool.wait_ge(part_done, b * NE + e + 1 + 2)
                    if e == 1:
                        pool.wait_ge(x_done, b)
                        pool.tensor_tensor(acc[:], part[:, 0, :], part[:, 1, :], ALU.add).then_inc(summed, 1)
                    else:
                        pool.wait_ge(summed, b * (NE - 1) + e - 1)
                        pool.tensor_tensor(acc[:], acc[:], part[:, e % 2, :], ALU.add).then_inc(summed, 1)

        @block.sync
        def _(sp):
            def spread(n, used=None):
                sp.wait_ge(cwt_done, n + 1)
                if used is not None:
                    for e in range(NE):
                        sp.wait_ge(cw_in[e], 16 * used + 16)
                sp.dma_start(cw_dram[:], cwt[:]).then_inc(cw_out, 16)
                sp.wait_ge(cw_out, 16 * (n + 1))
                for e in range(NE):
                    if used is not None:
                        sp.wait_ge(part_done, used * NE + e + 1 + 2)
                    sp.dma_start(cwb[:, e, :], cw_dram[e:e + 1, :].to_broadcast([P, T])).then_inc(cw_in[e], 16)

            spread(0)
            with sp.Fori(0, NB) as b:
                spread(b + 1, used=b)
            for e in range(NE):
                sp.wait_ge(cw_in[e], 16 * (NB + 1))


def moe_weights(nc, c, m, ins):
    w = Mem()
    sb = lambda n, s, d=F32: c.enter_context(nc.sbuf_tensor(n, s, d))
    w.w1h, w.w1l = sb("w1h", [P, NE, T], F32R), sb("w1l", [P, NE, T], F32R)
    w.w2h, w.w2l = sb("w2h", [P, NE, HC, P], F32R), sb("w2l", [P, NE, HC, P], F32R)
    w.b1, w.b2, w.gate = sb("b1", [P, NE * HC]), sb("b2", [P, NE]), sb("w_gate", [P, NE])
    with Phase(nc) as s:
        raw1 = s.enter_context(nc.sbuf_tensor("raw_w1", [P, NE, T], F32))
        raw2 = s.enter_context(nc.sbuf_tensor("raw_w2", [P, NE, HC, P], F32))
        w1_in, w2_in, rest_in = (s.sem(n) for n in ("w1_in", "w2_in", "moe_rest_in"))
        steps = s.sem("moe_split_steps")
        block = s.enter_context(nc.Block())

        @block.sync
        def _(sp):
            sp.dma_start(raw1[:], ins["L0_ffn_W1"].rearrange("e d h -> d e h")).then_inc(w1_in, 16)
            sp.dma_start(w.gate[:], ins["gate_t"]).then_inc(rest_in, 16)
            sp.dma_start(w.b1[:], ins["b1_t"]).then_inc(rest_in, 16)
            sp.dma_start(w.b2[:], ins["b2_t"]).then_inc(rest_in, 16)
            sp.dma_start(m.before[:], ins["before"]).then_inc(rest_in, 16)
            sp.wait_ge(rest_in, 64)

        @block.scalar
        def _(act):
            act.dma_start(raw2[:], ins["L0_ffn_W2"].rearrange("e (k p) d -> p e k d", p=P)).then_inc(w2_in, 16)

        @block.vector
        def _(dve):
            dve.wait_ge(w1_in, 16)
            n = split_weights(dve, [(raw1[:], w.w1h[:], w.w1l[:])], steps, 0)
            dve.wait_ge(w2_in, 16)
            split_weights(dve, [(raw2[:], w.w2h[:], w.w2l[:])], steps, n)
    return w


def ssm_phase(nc, m, ins):
    with Phase(nc) as c:
        sb = lambda n, s, d=F32: c.enter_context(nc.sbuf_tensor(f"ssm_{n}", s, d))
        sem = lambda n: c.sem(f"ssm_{n}")
        ln = Norm(nc, c, m, "ssm_ln", 0, 1)
        DTB, ZB = 2, 3
        CONV = 4
        w_in = sb("w_in", [P, 3 * P])
        w_dt, w_dtx = sb("w_dt", [P, 2 * P - NH]), sb("w_dtx", [P, P])
        w_out = sb("w_out", [P, P])
        conv_w, conv_b = sb("conv_w", [P, 3, 4]), sb("conv_b", [P, 3])
        a_par, dt_b = sb("a_par", [P, 2]), sb("dt_b", [P, 2])
        spread_p, gather_p = sb("spread_p", [P, NS, P]), sb("gather_p", [P, NS, P])
        spread_h = sb("spread_h", [P, NB, P])
        chunk_mask = sb("chunk_mask", [P, T])
        raw = sb("raw", [P, 3, T + 3])
        cbx = sb("cbx", [P, 3, T])
        z, az, ez, lz = (sb(n, [P, 2, T]) for n in ("z", "az", "ez", "lz"))
        cum, grow, fall = (sb(n, [P, 2, T]) for n in ("cum", "grow", "fall"))
        carry = sb("carry", [P, 2, T])
        state, rnorm = sb("state", [P, T]), sb("rnorm", [P, T])
        be, ce = sb("be", [P, T]), sb("ce", [P, T])
        d1, g, cg = sb("d1", [P, 2, T]), sb("g", [P, 2, T]), sb("cg", [P, 2, T])
        y, yb = sb("y", [P, T]), sb("yb", [P, 2, T])
        ins_in, zeroed, stepped, conved = sem("ins_in"), sem("zeroed"), sem("stepped"), sem("conv_in")
        chain, absd, exped, logged, curves = sem("chain"), sem("absd"), sem("exped"), sem("logged"), sem("curves")
        xrep, cg_done, y_done, d1_done = sem("xrep"), sem("cg_done"), sem("y_done"), sem("d1_done")
        rn_ready, yb_done, out_done, x_done, y_kept = sem("rn_ready"), sem("yb_done"), sem("out_done"), sem("x_done"), sem("y_kept")
        rnormed, raw_done, cx_done, cum_done = sem("rnormed"), sem("raw_done"), sem("cx_done"), sem("cum_done")
        block = c.enter_context(nc.Block())
        LOADS = [(w_in, "ssm_w_in"), (w_dtx, "ssm_w_dtx"), (w_out, "ssm_w_out"), (conv_w, "ssm_conv_w"),
                 (conv_b, "ssm_conv_b"), (a_par, "ssm_a"), (dt_b, "ssm_dt_b"), (spread_p, "spread_p"),
                 (gather_p, "gather_p"), (spread_h, "spread_h"), (chunk_mask, "chunk_mask")]

        @block.sync
        def _(sp):
            for t, n in LOADS:
                sp.dma_start(t[:], ins[n]).then_inc(ins_in, 16)
            sp.wait_ge(zeroed, 1)
            sp.dma_start(w_dt[:, P - NH:P], ins["ssm_w_dt"]).then_inc(ins_in, 16)

        ALL_IN = 16 * (len(LOADS) + 1)

        @block.gpsimd
        def _(pool):
            pool.memset(w_dt[:], 0.0).then_inc(zeroed, 1)
            pool.memset(raw[:, :, 0:3], 0.0).then_inc(zeroed, 1)
            for b in range(NB):
                ln.take(pool, b, m.x, b)

        @block.tensor
        def _(pe):
            pe.wait_ge(ins_in, ALL_IN)
            for b in range(NB + 1):
                if b < NB:
                    ln.centre(pe, b)
                if b > 0:
                    pe.wait_ge(ln.normed, b)
                    lo = P - NH - NH * (b - 1)
                    pe.matmul(m.ps[:, DTB, :], w_dt[:, lo:lo + P], ln.out[:], start=(b == 1), stop=(b == NB)).then_inc(stepped, 1)
                    if b == 1:
                        for k in range(3):
                            pe.matmul(m.ps[:, CONV + k, :], w_in[:, k * P:(k + 1) * P], ln.out[:], start=True,
                                      stop=True).then_inc(conved, 1)
                        pe.matmul(m.ps[:, ZB, :], w_dtx[:], ln.out[:], start=True, stop=True).then_inc(conved, 1)
                if b < NB:
                    ln.variance(pe, b)
            pe.wait_ge(cx_done, 1)
            for p in range(NS + 1):
                if p < NS:
                    if p >= 2:
                        pe.wait_ge(d1_done, p - 1)
                    elif p == 0:
                        pe.wait_ge(ln.normed, NB)
                        pe.wait_ge(ln.logged, NB)
                    pe.matmul(m.ps[:, p % 2, :], spread_p[:, p, :], cbx[:, 2, :], start=True, stop=True).then_inc(xrep, 1)
                if p > 0:
                    pe.wait_ge(cg_done, p)
                    pe.matmul(m.ps[:, 7, :], gather_p[:, p - 1, :], cg[:, (p - 1) % 2, :], start=(p == 1),
                              stop=(p == NS)).then_inc(y_done, 1)
            pe.wait_ge(rnormed, 1)
            for b in range(NB + 1):
                if b < NB:
                    if b >= 2:
                        pe.wait_ge(yb_done, b - 1)
                    pe.matmul(m.ps[:, b % 2, :], spread_h[:, b, :], rnorm[:], start=True, stop=True).then_inc(rn_ready, 1)
                if b > 0:
                    pe.wait_ge(yb_done, b)
                    if b > 2:
                        pe.wait_ge(x_done, b - 2)
                    pe.matmul(m.ps[:, 2 + b % 2, :], w_out[:], yb[:, (b - 1) % 2, :], start=True, stop=True).then_inc(out_done, 1)

        @block.scalar
        def _(act):
            for b in range(NB):
                ln.square(act, b)
                ln.scale(act, b)
                if b == 0:
                    act.wait_ge(conved, 3)
                    act.wait_ge(zeroed, 2)
                    for k in range(3):
                        act.activation(raw[:, k, 3:], m.ps[:, CONV + k, :], ACT.Copy).then_inc(raw_done, 1)
            act.wait_ge(absd, 1)
            act.activation(ez[:], az[:], ACT.Exp, scale=-1.0).then_inc(exped, 1)
            act.wait_ge(exped, 1)
            act.activation(lz[:], ez[:], ACT.Ln, bias=1.0).then_inc(logged, 1)
            act.wait_ge(cum_done, 1)
            act.activation(fall[:], cum[:], ACT.Exp, scale=-1.0).then_inc(curves, 1)
            act.activation(grow[:], cum[:], ACT.Exp).then_inc(curves, 1)

        @block.vector
        def _(dve):
            count = [0]

            def step(ins_):
                ins_.then_inc(chain, 1)
                count[0] += 1
                dve.wait_ge(chain, count[0])

            dve.wait_ge(ins_in, ALL_IN)
            for b in range(NB):
                if b >= 1:
                    dve.wait_ge(stepped, b)
                    if b == 1:
                        dve.wait_ge(conved, 4)
                ln.norm(dve, b)
            dve.wait_ge(raw_done, 3)
            for k in range(3):
                step(dve.tensor_scalar(cbx[:, k, :], raw[:, k, 0:T], conv_w[:, k, 0:1], conv_b[:, k:k + 1], ALU.mult, ALU.add))
                for j in range(1, 4):
                    step(dve.scalar_tensor_tensor(out=cbx[:, k, :], in0=raw[:, k, j:j + T], scalar=conv_w[:, k, j:j + 1],
                                                  in1=cbx[:, k, :], op0=ALU.mult, op1=ALU.add))
            dve.sem_inc(cx_done, 1)
            dve.wait_ge(stepped, NB)
            for i in range(2):
                step(dve.tensor_scalar(z[:, i, :], m.ps[:, DTB + i, :], dt_b[:, i:i + 1], None, ALU.add))
            step(dve.tensor_scalar(az[:], z[:], -1.0, None, ALU.mult))
            dve.tensor_tensor(az[:], az[:], z[:], ALU.max).then_inc(absd, 1)
            dve.wait_ge(logged, 1)
            step(dve.scalar_tensor_tensor(out=z[:], in0=z[:], scalar=0.0, in1=lz[:], op0=ALU.max, op1=ALU.add))
            for i in range(2):
                step(dve.tensor_scalar(z[:, i, :], z[:, i, :], a_par[:, i:i + 1], None, ALU.mult))
            for i in range(2):
                step(dve.tensor_tensor_scan(cum[:, i, :], chunk_mask[:], z[:, i, :], 0.0, ALU.mult, ALU.add))
            dve.sem_inc(cum_done, 1)
            dve.wait_ge(curves, 2)
            for i in range(2):
                step(dve.memset(carry[:, i, :], 1.0))
                step(dve.tensor_copy(carry[:, i, CHUNK::CHUNK], grow[:, i, CHUNK - 1:T - 1:CHUNK]))
            step(dve.tensor_tensor_scan(state[:], carry[:, 0, :], fall[:, 0, :], 0.0, ALU.mult, ALU.add))
            step(dve.tensor_tensor(state[:], state[:], grow[:, 0, :], ALU.mult))
            dve.reciprocal(rnorm[:], state[:]).then_inc(rnormed, 1)
            step(dve.tensor_tensor(be[:], cbx[:, 1, :], fall[:, 1, :], ALU.mult))
            step(dve.tensor_tensor(ce[:], cbx[:, 0, :], grow[:, 1, :], ALU.mult))
            for p in range(NS):
                s = p % 2
                dve.wait_ge(xrep, p + 1)
                dve.tensor_tensor(d1[:, s, :], m.ps[:, s, :], be[:], ALU.mult).then_inc(d1_done, 1)
                dve.wait_ge(d1_done, p + 1)
                step(dve.tensor_tensor_scan(g[:, s, :], carry[:, 1, :], d1[:, s, :], 0.0, ALU.mult, ALU.add))
                if p >= 2:
                    dve.wait_ge(y_done, p - 1)
                dve.tensor_tensor(cg[:, s, :], g[:, s, :], ce[:], ALU.mult).then_inc(cg_done, 1)
            dve.wait_ge(y_done, NS)
            dve.tensor_copy(y[:], m.ps[:, 7, :]).then_inc(y_kept, 1)
            dve.wait_ge(y_kept, 1)
            for b in range(NB + 1):
                if b < NB:
                    dve.wait_ge(rn_ready, b + 1)
                    if b >= 2:
                        dve.wait_ge(out_done, b - 1)
                    dve.tensor_tensor(yb[:, b % 2, :], m.ps[:, b % 2, :], y[:], ALU.mult).then_inc(yb_done, 1)
                if b > 0:
                    dve.wait_ge(out_done, b)
                    xb = m.x[:, (b - 1) * T:b * T]
                    dve.tensor_tensor(xb, m.ps[:, 2 + b % 2, :], xb, ALU.add).then_inc(x_done, 1)


EXP_LN = "natural_log_exp_and_others"


def entry_phase(nc, m, app):
    with Phase(nc) as c:
        lns = [Norm(nc, c, m, f"entry{app}_{i}", 2 * i, 2 * i + 1) for i in range(2)]
        block = c.enter_context(nc.Block())

        @block.gpsimd
        def _(pool):
            with pool.Fori(0, NB // 2) as i:
                for k in range(2):
                    lns[k].take(pool, i, m.x, 2 * i + k)

        @block.tensor
        def _(pe):
            with pe.Fori(0, NB // 2) as i:
                for k in range(2):
                    lns[k].centre(pe, i)
                for k in range(2):
                    lns[k].variance(pe, i)

        @block.scalar
        def _(act):
            with act.Fori(0, NB // 2) as i:
                for k in range(2):
                    lns[k].square(act, i)
                for k in range(2):
                    lns[k].scale(act, i)

        @block.vector
        def _(dve):
            with dve.Fori(0, NB // 2) as i:
                for k in range(2):
                    lns[k].norm(dve, i, seq(m.u, 2 * i + k))


def extras_phase(nc, c, m, ins):
    sb = lambda n, s, d=F32: c.enter_context(nc.sbuf_tensor(n, s, d))
    m.per_head, m.ident_bf, m.masks = sb("per_head", [P, P]), sb("ident_bf", [P, P], BF16), sb("masks_bf", [P, 2, T], BF16)
    m.tiny, m.unscale = sb("tiny", [P, 1]), sb("unscale", [P, 2])
    with Phase(nc) as s:
        raw = s.enter_context(nc.sbuf_tensor("raw_masks", [P, 2, T], F32))
        extras_in = s.sem("extras_in")
        block = s.enter_context(nc.Block())

        @block.sync
        def _(sp):
            sp.dma_start(raw[:], ins["masks"]).then_inc(extras_in, 16)
            sp.dma_start(m.per_head[:], ins["per_head"]).then_inc(extras_in, 16)
            sp.wait_ge(extras_in, 32)

        @block.vector
        def _(dve):
            dve.memset(m.tiny[:], 2.0 ** -64)
            dve.memset(m.unscale[:, 0:1], 8 * math.log(2.0) + math.log(8.0))
            dve.memset(m.unscale[:, 1:2], 8 * math.log(2.0))
            dve.memset(m.u[:, NB * T:], 0.0)
            dve.tensor_copy(m.ident_bf[:], m.ident[:])
            dve.wait_ge(extras_in, 32)
            dve.tensor_copy(m.masks[:], raw[:])


def gated_weights(nc, c, m, ins):
    ws = []
    sb = lambda n, s, d=F32: c.enter_context(nc.sbuf_tensor(n, s, d))
    for l in range(2):
        w = Mem()
        w.qkh, w.qkl = sb(f"wqk_h{l}", [P, 4, T], F32R), sb(f"wqk_l{l}", [P, 4, T], F32R)
        w.vh, w.vl = sb(f"wv_h{l}", [P, T], F32R), sb(f"wv_l{l}", [P, T], F32R)
        w.wo = sb(f"wo{l}", [P, HP, P])
        w.w1h, w.w1l = sb(f"w1_h{l}", [P, 2 * HID], F32R), sb(f"w1_l{l}", [P, 2 * HID], F32R)
        w.w2 = sb(f"w2_{l}", [P, MC, P])
        w.bias, w.b2 = sb(f"w1_bias{l}", [P, 2 * MC]), sb(f"b2_{l}", [P, 1])
        w.tables = sb(f"tables{l}", [P, 4, T])
        ws.append(w)
    with Phase(nc) as s:
        tb = lambda n, sh, d=F32: s.enter_context(nc.sbuf_tensor(n, sh, d))
        raw, raw1 = tb("raw_qkv", [P, 3 * T]), tb("raw_gated_w1", [P, 2 * HID])
        scales, lnw, b1 = tb("qk_scales", [P, 2, 4]), tb("ln_w", [P, 2, 2]), tb("b1_raw", [P, 2, 2 * MC])
        raw_in, rest_in, biased, steps = (s.sem(n) for n in ("gw_raw", "gw_rest", "gw_biased", "gw_steps"))
        rest2_in, cleared = s.sem("gw_rest2"), s.sem("gw_cleared")
        block = s.enter_context(nc.Block())
        LAYER_STEPS = 2 * 7 + 4 + 2 + 2
        REST = 16 * (3 + 2 * 4)

        @block.sync
        def _(sp):
            sp.dma_start(scales[:], ins["qk_scales"]).then_inc(rest_in, 16)
            sp.dma_start(lnw[:], ins["ln_w"]).then_inc(rest_in, 16)
            sp.dma_start(b1[:], ins["b1_gated"]).then_inc(rest_in, 16)
            for l, w in enumerate(ws):
                sp.dma_start(w.tables[:], ins["rotary"]).then_inc(rest_in, 16)
                sp.dma_start(w.wo[:], ins["L1_ffn_wo"][l].rearrange("(j p) d -> p j d", p=P)).then_inc(rest_in, 16)
                sp.dma_start(w.w2[:MW, 0:2, :], ins["L1_ffn_w2"][l][0:2 * MW, :].rearrange("(j p) d -> p j d", p=MW)).then_inc(rest_in, 16)
                sp.dma_start(w.w2[:HID - 2 * MW, 2, :], ins["L1_ffn_w2"][l][2 * MW:HID, :]).then_inc(rest_in, 16)
                sp.dma_start(w.b2[:], ins["b2_gated"][l]).then_inc(rest2_in, 16)
            for l, w in enumerate(ws):
                if l:
                    sp.wait_ge(steps, LAYER_STEPS)
                    sp.wait_ge(biased, 1)
                sp.dma_start(raw[:], ins["L1_ffn_wqkv"][l]).then_inc(raw_in, 16)
                sp.dma_start(raw1[:], ins["L1_ffn_w1"][l]).then_inc(raw_in, 16)
            sp.wait_ge(rest2_in, 32)

        @block.vector
        def _(dve):
            n = 0
            dve.memset(m.ps[:, 0:2, :2 * MC], 0.0).then_inc(cleared, 1)
            dve.wait_ge(rest_in, REST)
            for l, w in enumerate(ws):
                dve.wait_ge(raw_in, 32 * (l + 1))
                sw = lambda t: t.rearrange("p (h s j) -> p h s j", s=2, j=DH // 2)
                pairs = [(raw[:, 2 * T:], w.vh[:], w.vl[:])]
                for i in range(2):
                    src = raw[:, i * T:(i + 1) * T]
                    pairs.append((src, w.qkh[:, 2 * i, :], w.qkl[:, 2 * i, :]))
                    for half in range(2):
                        pairs.append((sw(src)[:, :, 1 - half, :], sw(w.qkh[:, 2 * i + 1, :])[:, :, half, :],
                                      sw(w.qkl[:, 2 * i + 1, :])[:, :, half, :]))
                n = split_weights(dve, pairs, steps, n)
                for k in range(4):
                    dve.tensor_scalar(w.tables[:, k, :], w.tables[:, k, :], scales[:, l, k:k + 1], None,
                                      ALU.mult).then_inc(steps, 1)
                    n += 1
                dve.wait_ge(biased, l + 1)
                dve.tensor_tensor(w.bias[:], m.ps[:, l, :2 * MC], b1[:, l, :], ALU.add).then_inc(steps, 1)
                dve.tensor_scalar(raw1[:], raw1[:], lnw[:, l, 0:1], None, ALU.mult).then_inc(steps, 1)
                n += 2
                dve.wait_ge(steps, n)
                n = split_weights(dve, [(raw1[:], w.w1h[:], w.w1l[:])], steps, n)
                assert n == (l + 1) * LAYER_STEPS

        @block.tensor
        def _(pe):
            pe.wait_ge(rest_in, REST)
            pe.wait_ge(cleared, 1)
            for l in range(2):
                pe.wait_ge(raw_in, 32 * (l + 1))
                for i in range(2 * MC):
                    lo = (i // MC) * HID + (i % MC) * MW
                    n = min(MW, HID - (i % MC) * MW)
                    mm = pe.matmul(m.ps[:n, l, i:i + 1], raw1[:, lo:lo + n], lnw[:, l, 1:2], start=True, stop=True)
                mm.then_inc(biased, 1)
    return ws


def attention_phase(nc, m, app, l, w):
    Q, QR, K, KR, S, PT, O = 0, 1, 2, 3, 4, 6, 7
    HW = NW // 2
    with Phase(nc) as c:
        name = f"att{app}{l}"
        sb = lambda n, s, d=F32: c.enter_context(nc.sbuf_tensor(f"{name}_{n}", s, d))
        sem = lambda n: c.sem(f"{name}_{n}")
        hs = sb("hs", [P, T])
        hh, hl = sb("hh", [P, WIN + T], F32R), sb("hl", [P, WIN + T], F32R)
        v = sb("v", [P, NW, T])
        turned = sb("turned", [P, 4, T])
        sums = sb("sums", [P, 2, T])
        squares = sb("squares", [P, 2, T])
        rn = sb("rn", [P, 2, T])
        qn, kn = sb("qn", [P, 2, T]), sb("kn", [P, 2, WIN + T])
        probs = sb("probs", [P, 2, NW, P])
        nmax, psum_, rsum = sb("nmax", [P, 2, NW]), sb("psum", [P, 2, NW]), sb("rsum", [P, 2, NW])
        pts = sb("pts", [P, 2, T])
        o = sb("o", [P, HP, T])
        zeroed, taken, hi_done, split = sem("zeroed"), sem("taken"), sem("hi_done"), sem("split")
        projected, rotated, squared, added = sem("projected"), sem("rotated"), sem("squared"), sem("added")
        ss_done, ss_logged, rn_done, qk_done = sem("ss_done"), sem("ss_logged"), sem("rn_done"), sem("qk_done")
        sim_done, maxed, exped, recip, normed = sem("sim_done"), sem("maxed"), sem("exped"), sem("recip"), sem("normed")
        pt_done, pt_kept0, pt_kept1, pv_done = sem("pt_done"), sem("pt_kept0"), sem("pt_kept1"), sem("pv_done")
        zeroed2 = sem("zeroed2")
        o_kept, wo_done, u_done = sem("o_kept"), sem("wo_done"), sem("u_done")
        v_done, v_kept0, v_kept1 = sem("v_done"), sem("v_kept0"), sem("v_kept1")
        block = c.enter_context(nc.Block())
        pt_kept = [pt_kept0, pt_kept1]
        v_kept = [v_kept0, v_kept1]

        @block.tensor
        def _(pe):
            def project(n, j, kinds):
                cols = slice(j * P, (j + 1) * P)
                for k in kinds:
                    if k % 2 == 0:
                        pe.wait_ge(ss_logged, 2 * n + k // 2 + 1)
                    else:
                        pe.wait_ge(rotated, 4 * n + k)
                    mm3(pe, m.ps[:, Q + k, :], (w.qkh[:, k, cols], w.qkl[:, k, cols]),
                        (hh[:, WIN:], hl[:, WIN:])).then_inc(projected, 1)

            def norms(n, i):
                pe.wait_ge(squared, 2 * n + i + 1)
                pe.wait_ge(rotated, 4 * n + 2 * i + 2 + 4)
                pe.matmul(m.ps[:, Q + 2 * i, :], m.per_head[:], squares[:, i, :], start=True, stop=True).then_inc(ss_done, 1)

            def sims(n, j, b):
                for half in range(2):
                    if half == 0:
                        pe.wait_ge(qk_done, 2 * n + 2)
                    pe.wait_ge(exped, NW * n + HW * (half + 1))
                    if j == 0 and half == 0:
                        pe.wait_ge(u_done, b)
                    pe.matmul(m.ps[:, S + half, :], m.ident_bf[:], m.masks[:, half, :], start=True, stop=True)
                    for i in range(HW):
                        win = half * HW + i
                        for h in range(2):
                            r = slice(DH * h, DH * h + DH)
                            mm = pe.matmul(m.ps[r, S + half, i * P:(i + 1) * P], qn[r, j % 2, win * WIN:(win + 1) * WIN],
                                           kn[r, j % 2, win * WIN:win * WIN + P], start=False,
                                           stop=True, skip_group_check=True)
                    mm.then_inc(sim_done, 1)

            def turn(n, j, half):
                pe.wait_ge(normed, 2 * n + half + 1)
                if half == 0:
                    pe.wait_ge(pt_kept[1], n + 1)
                else:
                    pe.wait_ge(pt_kept[0], n + 1 + 1)
                for i in range(HW):
                    tr = pe.transpose(m.ps[:, PT, i * P:(i + 1) * P], probs[:, j % 2, half * HW + i, :], m.ident[:])
                tr.then_inc(pt_done, 1)

            def values(n, j, half):
                pe.wait_ge(pt_kept[half], n + 1 + 1)
                if half == 0:
                    pe.wait_ge(o_kept, n + 1)
                for i in range(HW):
                    win = half * HW + i
                    for h in range(2):
                        mm = pe.matmul(m.ps[DH * h:DH * h + DH, O, win * WIN:(win + 1) * WIN],
                                       v[:, win, j * P + DH * h:j * P + DH * h + DH],
                                       pts[:, half, i * P + DH * h:i * P + DH * h + DH], start=True, stop=True)
                mm.then_inc(pv_done, 1)

            def all_values(b):
                for win in range(NW):
                    k = win % 2
                    if win < 2:
                        pe.wait_ge(pt_kept[1], HP * b + 1)
                        pe.wait_ge(o_kept, HP * b + 1)
                    else:
                        pe.wait_ge(v_kept[k], (NW // 2) * b + win // 2)
                    mm3(pe, m.ps[:, PT + k, :], (hh[:, win * WIN:win * WIN + P], hl[:, win * WIN:win * WIN + P]),
                        (w.vh[:], w.vl[:])).then_inc(v_done, 1)

            pe.sem_inc(pt_done, 2)
            pe.wait_ge(split, 1)
            project(0, 0, range(4))
            norms(0, 0)
            norms(0, 1)
            with pe.Fori(0, NB) as b:
                all_values(b)
                for j in range(HP):
                    n = b * HP + j
                    if j == HP - 1:
                        pe.wait_ge(split, b + 2)
                    project(n + 1, (j + 1) % HP, range(4))
                    sims(n, j, b)
                    if j == 1:
                        for k in range(2):
                            pe.wait_ge(v_kept[k], (NW // 2) * (b + 1))
                    if j > 0:
                        turn(n - 1, j - 1, 0)
                    norms(n + 1, 0)
                    if j > 0:
                        turn(n - 1, j - 1, 1)
                        values(n - 1, j - 1, 0)
                    norms(n + 1, 1)
                    if j > 0:
                        values(n - 1, j - 1, 1)
                n = b * HP + HP - 1
                turn(n, HP - 1, 0)
                turn(n, HP - 1, 1)
                values(n, HP - 1, 0)
                values(n, HP - 1, 1)
                pe.wait_ge(exped, NW * (n + 2))
                for j in range(HP):
                    pe.wait_ge(o_kept, HP * b + j + 1 + 1)
                    mm = pe.matmul(m.ps[:, S, :], w.wo[:, j, :], o[:, j, :], start=(j == 0), stop=(j == HP - 1))
                mm.then_inc(wo_done, 1)

        @block.scalar
        def _(act):
            def square(n, i):
                act.wait_ge(projected, 4 * n + 2 * i + 1)
                act.wait_ge(ss_done, 2 * n)
                act.activation(squares[:, i, :], m.ps[:, Q + 2 * i, :], ACT.Square).then_inc(squared, 1)

            def scale(n, i):
                act.wait_ge(ss_done, 2 * n + i + 1)
                act.wait_ge(qk_done, 2 * n)
                act.activation(rn[:, i, :], m.ps[:, Q + 2 * i, :], ACT.Ln, bias=m.tiny[:, 0:1],
                               scale=SS_SCALE).then_inc(ss_logged, 1)
                act.wait_ge(ss_logged, 2 * n + i + 1 + 2)
                act.activation(rn[:, i, :], rn[:, i, :], ACT.Exp, scale=-0.5,
                               bias=m.unscale[:, i:i + 1]).then_inc(rn_done, 1)

            def exps(n, j):
                for win in range(NW):
                    if win % HW == 0:
                        act.wait_ge(maxed, 2 * n + win // HW + 1)
                        act.wait_ge(pt_done, 2 * n)
                    act.activation(probs[:, j % 2, win, :], m.ps[:, S + win // HW, (win % HW) * P:(win % HW + 1) * P],
                                   ACT.Exp, bias=nmax[:, j % 2, win:win + 1],
                                   accum_out=psum_[:, j % 2, win:win + 1]).then_inc(exped, 1)

            def keep_turned(n):
                act.wait_ge(pt_done, 2 * n + 1 + 2)
                act.wait_ge(pv_done, 2 * n)
                act.activation(pts[:, 0, :], m.ps[:, PT, :], ACT.Copy).then_inc(pt_kept[0], 1)

            act.preload_act_table_set(EXP_LN)
            act.sem_inc(ss_logged, 2)
            act.sem_inc(exped, NW)
            act.sem_inc(pt_kept[0], 1)
            for i in range(2):
                square(0, i)
            for i in range(2):
                scale(0, i)
            with act.Fori(0, NB) as b:
                for win in range(0, NW, 2):
                    act.wait_ge(v_done, NW * b + win + 1)
                    act.activation(v[:, win, :], m.ps[:, PT, :], ACT.Copy).then_inc(v_kept[0], 1)
                for j in range(HP):
                    n = b * HP + j
                    for i in range(2):
                        square(n + 1, i)
                    if j > 0:
                        keep_turned(n - 1)
                    exps(n, j)
                    for i in range(2):
                        scale(n + 1, i)
                keep_turned(b * HP + HP - 1)

        @block.vector
        def _(dve):
            def halves(b):
                dve.wait_ge(taken, 2 * (b + 1))
                dve.wait_ge(projected, 4 * HP * b)
                dve.tensor_copy(hh[:, WIN:], hs[:]).then_inc(hi_done, 1)
                dve.wait_ge(hi_done, b + 1)
                dve.tensor_tensor(hl[:, WIN:], hs[:], hh[:, WIN:], ALU.subtract).then_inc(split, 1)

            def rotate(n):
                for k in (1, 0, 3, 2):
                    dve.wait_ge(projected, 4 * n + k + 1)
                    if k % 2 == 0:
                        dve.wait_ge(squared, 2 * n + k // 2 + 1)
                    dve.wait_ge(added, 2 * n)
                    dve.tensor_tensor(turned[:, k, :], m.ps[:, Q + k, :], w.tables[:, k, :], ALU.mult).then_inc(rotated, 1)

            def maxima(n, j):
                for half in range(2):
                    dve.wait_ge(sim_done, 2 * n + half + 1)
                    dve.wait_ge(exped, NW * n + HW * (half + 1))
                    dve.tensor_reduce(nmax[:, j % 2, half * HW:(half + 1) * HW],
                                      m.ps[:, S + half, :].rearrange("p (w k) -> p w k", k=P), AX.X, ALU.max,
                                      negate=True).then_inc(maxed, 1)

            def scale_qk(n, j):
                dve.wait_ge(sim_done, 2 * n)
                dve.wait_ge(rn_done, 2 * n + 1)
                dve.wait_ge(added, 2 * n + 1)
                dve.scalar_tensor_tensor(out=qn[:, j % 2, :], in0=rn[:, 0, :], scalar=8e12, in1=sums[:, 0, :], op0=ALU.min,
                                         op1=ALU.mult).then_inc(qk_done, 1)
                dve.wait_ge(rn_done, 2 * n + 2)
                dve.wait_ge(added, 2 * n + 2)
                dve.scalar_tensor_tensor(out=kn[:, j % 2, WIN:], in0=rn[:, 1, :], scalar=1e12, in1=sums[:, 1, :], op0=ALU.min,
                                         op1=ALU.mult).then_inc(qk_done, 1)

            def reciprocals(n, j):
                dve.wait_ge(exped, NW * (n + 2))
                dve.wait_ge(normed, 2 * n)
                dve.reciprocal(rsum[:, j % 2, :], psum_[:, j % 2, :]).then_inc(recip, 1)

            def keep_turned(n):
                dve.wait_ge(pt_done, 2 * n + 2 + 2)
                dve.wait_ge(pv_done, 2 * n)
                dve.tensor_copy(pts[:, 1, :], m.ps[:, PT, :]).then_inc(pt_kept[1], 1)

            def keep_out(n, j, b):
                dve.wait_ge(pv_done, 2 * n + 2)
                dve.wait_ge(wo_done, b)
                dve.tensor_copy(o[:, j, :], m.ps[:, O, :]).then_inc(o_kept, 1)

            dve.sem_inc(rotated, 4)
            dve.sem_inc(pt_kept[1], 1)
            dve.sem_inc(o_kept, 1)
            dve.memset(hh[:, :WIN].bitcast(F32), 0.0).then_inc(zeroed, 1)
            dve.memset(hl[:, :WIN].bitcast(F32), 0.0).then_inc(zeroed, 1)
            for k in range(2):
                dve.memset(kn[:, k, :WIN], 0.0).then_inc(zeroed, 1)
            halves(0)
            rotate(0)
            scale_qk(0, 0)
            with dve.Fori(0, NB) as b:
                for win in range(1, NW, 2):
                    dve.wait_ge(v_done, NW * b + win + 1)
                    dve.tensor_copy(v[:, win, :], m.ps[:, O, :]).then_inc(v_kept[1], 1)
                for j in range(HP):
                    n = b * HP + j
                    if j == HP - 1:
                        halves(b + 1)
                    rotate(n + 1)
                    maxima(n, j)
                    if j > 0:
                        keep_turned(n - 1)
                        keep_out(n - 1, j - 1, b)
                    reciprocals(n, j)
                    scale_qk(n + 1, (j + 1) % HP)
                n = b * HP + HP - 1
                keep_turned(n)
                keep_out(n, HP - 1, b)
                dve.wait_ge(wo_done, b + 1)
                dve.tensor_tensor(seq(m.u, b), m.ps[:, S, :], seq(m.u, b), ALU.add).then_inc(u_done, 1)

        @block.gpsimd
        def _(pool):
            def take(b):
                pool.wait_ge(split, b)
                pool.tensor_copy(hs[:P // 2, :], m.u[:P // 2, bass.ds(b * T, T)]).then_inc(taken, 1)
                pool.tensor_copy(hs[P // 2:, 1:], m.u[P // 2:, bass.ds(b * T, T - 1)]).then_inc(taken, 1)
                pool.wait_ge(taken, 2 * b + 2)

            def add(n):
                for i in range(2):
                    pool.wait_ge(rotated, 4 * n + 2 * i + 2 + 4)
                    pool.wait_ge(qk_done, 2 * n)
                    pool.tensor_tensor(sums[:, i, :], turned[:, 2 * i, :], turned[:, 2 * i + 1, :], ALU.add).then_inc(added, 1)

            def norm(n, j):
                pool.wait_ge(recip, n + 1)
                for half in range(2):
                    ws = slice(half * HW, (half + 1) * HW)
                    pool.tensor_tensor(probs[:, j % 2, ws, :], probs[:, j % 2, ws, :],
                                       rsum[:, j % 2, ws].unsqueeze(2).to_broadcast([P, HW, P]),
                                       ALU.mult).then_inc(normed, 1)

            pool.memset(hs[P // 2:, 0:1], 0.0).then_inc(zeroed2, 1)
            pool.wait_ge(zeroed2, 1)
            take(0)
            add(0)
            pool.wait_ge(added, 2)
            with pool.Fori(0, NB) as b:
                pool.wait_ge(normed, 2 * HP * b)
                take(b + 1)
                for j in range(HP):
                    n = b * HP + j
                    add(n + 1)
                    norm(n, j)


def gated_phase(nc, m, app, l, w, last):
    A, G, Y = [2, 3, 2], [4, 5, 4], 6
    with Phase(nc) as c:
        name = f"ff{app}{l}"
        sb = lambda n, s, d=F32: c.enter_context(nc.sbuf_tensor(f"{name}_{n}", s, d))
        sem = lambda n: c.sem(f"{name}_{n}")
        ln = Norm(nc, c, m, name + "_ln", 0, 1, shift=True)
        xh, xl = sb("xh", [P, T], F32R), sb("xl", [P, T], F32R)
        gate, prod = sb("gate", [P, MC, T]), sb("prod", [P, MC, T])
        hi_done, split, up_done, gelued, gated = sem("hi_done"), sem("split"), sem("up_done"), sem("gelued"), sem("gated")
        down_done, u_done, x_done = sem("down_done"), sem("u_done"), sem("x_done")
        block = c.enter_context(nc.Block())
        width = [MW, MW, HID - 2 * MW]

        @block.gpsimd
        def _(pool):
            ln.start(pool)
            ln.take(pool, 0, m.u, 0)
            with pool.Fori(0, NB) as b:
                ln.take(pool, b + 1, m.u, b + 1)

        @block.tensor
        def _(pe):
            def up(b, i):
                pe.wait_ge(gated, MC * b if i < 2 else MC * b + 1)
                for k, bank in ((1, G[i]), (0, A[i])):
                    cols = slice(k * HID + i * MW, k * HID + i * MW + width[i])
                    mm3(pe, m.ps[:width[i], bank, :], (w.w1h[:, cols], w.w1l[:, cols]), (xh[:], xl[:])).then_inc(up_done, 1)

            def down(b, i):
                pe.wait_ge(gated, MC * b + i + 1)
                if i == 0:
                    pe.wait_ge(u_done, b)
                pe.matmul(m.ps[:, Y, :], w.w2[:width[i], i, :], prod[:width[i], i, :], start=(i == 0),
                          stop=(i == MC - 1)).then_inc(down_done, 1)

            ln.centre(pe, 0)
            ln.variance(pe, 0)
            with pe.Fori(0, NB) as b:
                pe.wait_ge(split, b + 1)
                ln.centre(pe, b + 1)
                up(b, 0)
                up(b, 1)
                ln.variance(pe, b + 1)
                down(b, 0)
                up(b, 2)
                down(b, 1)
                down(b, 2)

        @block.scalar
        def _(act):
            def gelu(b, i):
                act.wait_ge(up_done, 2 * (MC * b + i) + 1)
                act.wait_ge(gated, MC * b)
                act.activation(gate[:width[i], i, :], m.ps[:width[i], G[i], :], ACT.Gelu,
                               bias=w.bias[:width[i], MC + i:MC + i + 1]).then_inc(gelued, 1)

            ln.square(act, 0)
            ln.scale(act, 0)
            with act.Fori(0, NB) as b:
                ln.square(act, b + 1)
                for i in range(MC):
                    gelu(b, i)
                ln.scale(act, b + 1)

        @block.vector
        def _(dve):
            def halves(n):
                dve.wait_ge(up_done, 2 * MC * n)
                dve.wait_ge(ln.normed, n + 1)
                dve.tensor_copy(xh[:], ln.out[:]).then_inc(hi_done, 1)
                dve.wait_ge(hi_done, n + 1)
                dve.tensor_tensor(xl[:], ln.out[:], xh[:], ALU.subtract).then_inc(split, 1)

            ln.norm(dve, 0)
            halves(0)
            with dve.Fori(0, NB) as b:
                for i in range(MC):
                    dve.wait_ge(up_done, 2 * (MC * b + i) + 2)
                    dve.wait_ge(gelued, MC * b + i + 1)
                    dve.wait_ge(down_done, MC * b)
                    dve.scalar_tensor_tensor(out=prod[:width[i], i, :], in0=m.ps[:width[i], A[i], :],
                                             scalar=w.bias[:width[i], i:i + 1], in1=gate[:width[i], i, :],
                                             op0=ALU.add, op1=ALU.mult).then_inc(gated, 1)
                ln.norm(dve, b + 1)
                halves(b + 1)
                dve.wait_ge(down_done, MC * (b + 1))
                dve.scalar_tensor_tensor(out=seq(m.u, b), in0=m.ps[:, Y, :], scalar=w.b2[:, 0:1], in1=seq(m.u, b),
                                         op0=ALU.add, op1=ALU.add).then_inc(u_done, 1)
                if last:
                    dve.wait_ge(u_done, b + 1)
                    dve.scalar_tensor_tensor(out=seq(m.x, b), in0=seq(m.u, b), scalar=0.5, in1=seq(m.x, b),
                                             op0=ALU.mult, op1=ALU.add).then_inc(x_done, 1)


def global_phase(nc, m, ins):
    with Phase(nc) as c:
        sb = lambda n, s, d=F32: c.enter_context(nc.sbuf_tensor(f"glob_{n}", s, d))
        sem = lambda n: c.sem(f"glob_{n}")
        ln = Norm(nc, c, m, "glob_ln", 0, 1)
        raw = sb("raw", [P, 3, P])
        wh, wl = sb("wh", [P, 3, P], F32R), sb("wl", [P, 3, P], F32R)
        xh, xl = sb("xh", [P, T], F32R), sb("xl", [P, T], F32R)
        ones = sb("ones", [P, P])
        squares, rn, v = sb("squares", [P, 2, T]), sb("rn", [P, 2, T]), sb("v", [P, T])
        kn, kv, qn, feat = sb("kn", [P, T]), sb("kv", [P, T]), sb("qn", [P, T]), sb("feat", [P, 1])
        w_in, steps, hi_done, split, projected = sem("w_in"), sem("steps"), sem("hi_done"), sem("split"), sem("projected")
        squared, v_kept, ss_done, ss_logged, rn_done = sem("squared"), sem("v_kept"), sem("ss_done"), sem("ss_logged"), sem("rn_done")
        k_scaled, q_scaled, feated, x_done = sem("k_scaled"), sem("q_scaled"), sem("feated"), sem("x_done")
        block = c.enter_context(nc.Block())
        Q, K, V, SS = 2, 3, 4, 5

        @block.sync
        def _(sp):
            sp.dma_start(raw[:], ins["qkv_global"]).then_inc(w_in, 16)

        @block.gpsimd
        def _(pool):
            ln.take(pool, 0, m.x, 0)
            with pool.Fori(0, NB) as b:
                ln.take(pool, b + 1, m.x, b + 1)

        @block.tensor
        def _(pe):
            ln.centre(pe, 0)
            ln.variance(pe, 0)
            with pe.Fori(0, NB) as b:
                pe.wait_ge(split, b + 1)
                for k in range(3):
                    if k == Q - 2:
                        pe.wait_ge(q_scaled, b)
                    if k == K - 2:
                        pe.wait_ge(k_scaled, b)
                    if k == V - 2:
                        pe.wait_ge(v_kept, b)
                    mm3(pe, m.ps[:, Q + k, :], (wh[:, k, :], wl[:, k, :]), (xh[:], xl[:])).then_inc(projected, 1)
                ln.centre(pe, b + 1)
                for i in range(2):
                    pe.wait_ge(squared, 2 * b + i + 1)
                    pe.wait_ge(ss_logged, 2 * b)
                    pe.matmul(m.ps[:, SS + i, :], ones[:], squares[:, i, :], start=True, stop=True).then_inc(ss_done, 1)
                ln.variance(pe, b + 1)

        @block.scalar
        def _(act):
            act.preload_act_table_set(EXP_LN)
            ln.square(act, 0)
            ln.scale(act, 0)
            with act.Fori(0, NB) as b:
                for i in range(2):
                    act.wait_ge(projected, 3 * b + i + 1)
                    act.wait_ge(ss_done, 2 * b)
                    act.activation(squares[:, i, :], m.ps[:, Q + i, :], ACT.Square).then_inc(squared, 1)
                act.wait_ge(projected, 3 * b + 3)
                act.wait_ge(feated, b)
                act.activation(v[:], m.ps[:, V, :], ACT.Copy).then_inc(v_kept, 1)
                ln.square(act, b + 1)
                for i in range(2):
                    act.wait_ge(ss_done, 2 * b + i + 1)
                    act.wait_ge(k_scaled, b)
                    act.wait_ge(q_scaled, b)
                    act.activation(rn[:, i, :], m.ps[:, SS + i, :], ACT.Ln, bias=m.tiny[:, 0:1],
                                   scale=SS_SCALE).then_inc(ss_logged, 1)
                    act.wait_ge(ss_logged, 2 * b + i + 1)
                    act.activation(rn[:, i, :], rn[:, i, :], ACT.Exp, scale=-0.5,
                                   bias=m.unscale[:, 1:2]).then_inc(rn_done, 1)
                ln.scale(act, b + 1)

        @block.vector
        def _(dve):
            def halves(n):
                dve.wait_ge(projected, 3 * n)
                dve.wait_ge(ln.normed, n + 1)
                dve.tensor_copy(xh[:], ln.out[:]).then_inc(hi_done, 1)
                dve.wait_ge(hi_done, n + 1)
                dve.tensor_tensor(xl[:], ln.out[:], xh[:], ALU.subtract).then_inc(split, 1)

            dve.memset(ones[:], 1.0)
            dve.wait_ge(w_in, 16)
            split_weights(dve, [(raw[:], wh[:], wl[:])], steps, 0)
            ln.norm(dve, 0)
            halves(0)
            with dve.Fori(0, NB) as b:
                dve.wait_ge(rn_done, 2 * b + 2)
                dve.scalar_tensor_tensor(out=kn[:], in0=rn[:, 1, :], scalar=1e12, in1=m.ps[:, K, :], op0=ALU.min,
                                         op1=ALU.mult).then_inc(k_scaled, 1)
                dve.wait_ge(x_done, b)
                dve.scalar_tensor_tensor(out=qn[:], in0=rn[:, 0, :], scalar=1e12, in1=m.ps[:, Q, :], op0=ALU.min,
                                         op1=ALU.mult).then_inc(q_scaled, 1)
                dve.wait_ge(v_kept, b + 1)
                dve.wait_ge(k_scaled, b + 1)
                dve.tensor_tensor_reduce(out=kv[:], in0=kn[:], in1=v[:], scale=1.0 / T, scalar=0.0, op0=ALU.mult,
                                         op1=ALU.add, accum_out=feat[:]).then_inc(feated, 1)
                ln.norm(dve, b + 1)
                halves(b + 1)
                dve.wait_ge(feated, b + 1)
                dve.wait_ge(q_scaled, b + 1)
                dve.scalar_tensor_tensor(out=seq(m.x, b), in0=qn[:], scalar=feat[:, 0:1], in1=seq(m.x, b),
                                         op0=ALU.mult, op1=ALU.add).then_inc(x_done, 1)


IDENT = np.eye(P, dtype=np.float32)


def constants():
    k = {"ident": IDENT, "center": IDENT - np.float32(1.0 / P)}
    e = np.arange(NE)
    k["before"] = np.tile((e[None, :] < e[:, None]).astype(np.float32), (P, 1, 1))
    r = np.arange(P)
    sp = np.zeros((P, NS, P), np.float32)
    sh = np.zeros((P, NB, P), np.float32)
    for p in range(NS):
        for q in r:
            sp[(q // NS) * NS + p, p, q] = 1.0
    for b in range(NB):
        for q in r:
            sh[b * NH + q // NS, b, q] = 1.0
    k["spread_p"], k["spread_h"] = sp, sh
    k["gather_p"] = np.ascontiguousarray(sp.transpose(2, 1, 0))
    cm = np.ones((P, T), np.float32)
    cm[:, ::CHUNK] = 0.0
    k["chunk_mask"] = cm
    k["per_head"] = np.kron(np.eye(2), np.ones((DH, DH))).astype(np.float32)
    q, key = np.arange(WIN)[:, None], np.arange(2 * WIN)[None, :]
    seen = (key <= q + WIN) & (key >= q)
    later = np.where(seen, 0.0, MASKED)
    first = np.where(seen & (key >= WIN), 0.0, MASKED)
    rows = np.stack([np.concatenate([w0, later, later, later], 1) for w0 in (first, later)], 1)
    k["masks"] = np.tile(rows, (2, 1, 1)).astype(np.float32)
    f32 = np.float32
    half = np.arange(0, DH, 2, dtype=f32)
    inv = (1.0 / (f32(10000.0) ** (half / f32(DH)))).astype(f32)
    t = np.arange(T, dtype=f32)
    freqs = (t[:, None] * inv[None, :]).astype(f32)
    base = (half + f32(0.4 * DH)) / f32(1.4 * DH)
    power = (t - T // 2) / f32(WIN // 2)
    scale = (base[None, :] ** power[:, None]).astype(f32)
    cos, sin = np.cos(freqs), np.sin(freqs)
    tab = []
    for sc in (scale, 1.0 / scale):
        cc, ss = (cos * sc).T, (sin * sc).T
        tab += [np.concatenate([cc, cc] * 2), np.concatenate([-ss, ss] * 2)]
    k["rotary"] = np.ascontiguousarray(np.stack(tab, 1).astype(f32))
    return k


def build(nc, ins, out, upto="s6"):
    with ExitStack() as c:
        m = Mem()
        sb = lambda n, s, d=F32: c.enter_context(nc.sbuf_tensor(n, s, d))
        m.x = sb("x", [P, (NB + 1) * T])
        m.ident, m.center, m.mean_of = sb("ident", [P, P]), sb("center", [P, P]), sb("mean_of", [P, P])
        m.eps, m.before = sb("eps", [P, 1]), sb("before", [P, NE, NE])
        m.ps = c.enter_context(nc.psum_tensor("banks", [P, 8, T], F32))
        cw_dram = nc.dram_tensor("cw_dram", [NE, T], F32)
        load_phase(nc, m, ins["L0_attn_x"], ins)
        with ExitStack() as moe:
            w = moe_weights(nc, moe, m, ins)
            moe_phase(nc, m, 0, w, cw_dram.ap())
            if upto >= "s2":
                ssm_phase(nc, m, ins)
            if upto >= "s3":
                moe_phase(nc, m, 1, w, cw_dram.ap())
        with ExitStack() as gated:
            if upto >= "s4":
                m.u = gated.enter_context(nc.sbuf_tensor("u", [P, (NB + 1) * T], F32))
                extras_phase(nc, gated, m, ins)
                ws = gated_weights(nc, gated, m, ins)
            for app in range(2):
                if upto >= ("s4", "s6")[app]:
                    entry_phase(nc, m, app)
                    for l in range(2):
                        attention_phase(nc, m, app, l, ws[l])
                        gated_phase(nc, m, app, l, ws[l], last=(l == 1))
                if app == 0 and upto >= "s5":
                    global_phase(nc, m, ins)
        store_phase(nc, m, out)


def arrays(inp):
    import numpy as np
    a = {n: np.ascontiguousarray(np.asarray(v)) for n, v in inp.items()}
    t = np.ascontiguousarray
    a.update(constants())
    a["gate_t"] = t(a["L0_ffn_w_gate"].T)
    a["b1_t"] = t(a["L0_ffn_b1"].reshape(NE * HC, P).T)
    a["b2_t"] = t(a["L0_ffn_b2"].T)
    w_in = a["L0_attn_W_in"]
    a["ssm_w_in"] = t(w_in[:3 * P].T)
    a["ssm_w_dt"] = t(w_in[3 * P:].T)
    a["ssm_w_dtx"] = t(np.repeat(w_in[3 * P:], NS, axis=0).T)
    a["ssm_w_out"] = t(a["L0_attn_W_out"].T)
    a["ssm_conv_w"] = t(a["L0_attn_conv_w"].reshape(3, P, 4).transpose(1, 0, 2))
    a["ssm_conv_b"] = t(a["L0_attn_conv_b"].reshape(3, P).T)
    a["ssm_a"] = t(np.stack([np.tile(a["L0_attn_A_param"], NB), np.repeat(a["L0_attn_A_param"], NS)], 1))
    a["ssm_dt_b"] = t(np.stack([np.tile(a["L0_attn_dt_bias"], NB), np.repeat(a["L0_attn_dt_bias"], NS)], 1))
    a["b2_gated"] = t(a["L1_ffn_b2"][:, :, None])
    other = np.roll(np.arange(DH), DH // 2)
    qs, ks = a["L1_ffn_q_scale"], a["L1_ffn_k_scale"]
    a["qk_scales"] = t(np.stack([np.tile(z, (1, 2)) for z in (qs, qs[:, other], ks, ks[:, other])], 2).transpose(1, 0, 2))
    a["ln_w"] = t(np.stack([a["L1_ffn_ln_g"], a["L1_ffn_ln_b"]], 2).transpose(1, 0, 2))
    b1 = np.zeros((P, 2, 2 * MC), np.float32)
    for i in range(2 * MC):
        n = min(MW, HID - (i % MC) * MW)
        lo = (i // MC) * HID + (i % MC) * MW
        b1[:n, :, i] = a["L1_ffn_b1"][:, lo:lo + n].T
    a["b1_gated"] = b1
    a["qkv_global"] = t(np.stack([a[f"L1_attn_W_{n}"].T for n in "qkv"], 1))
    return a


USED = ["L0_attn_x", "L0_ffn_W1", "L0_ffn_W2", "gate_t", "b1_t", "b2_t", "before", "ident", "center",
        "ssm_w_in", "ssm_w_dt", "ssm_w_dtx", "ssm_w_out", "ssm_conv_w", "ssm_conv_b", "ssm_a", "ssm_dt_b",
        "spread_p", "gather_p", "spread_h", "chunk_mask", "per_head", "masks", "rotary", "b2_gated", "qk_scales", "ln_w", "b1_gated", "qkv_global",
        "L1_ffn_wqkv", "L1_ffn_wo", "L1_ffn_w1", "L1_ffn_w2"]


def kernel(**inputs):
    import numpy as np
    import concourse.bacc as bacc
    from concourse.bass_utils import run_bass_kernel_spmd

    nc = bacc.Bacc("TRN2", target_bir_lowering=False, num_devices=1)
    a = arrays(inputs)
    fed = {f"in_{n}": a[n] for n in USED}
    ins = {n: nc.dram_tensor(f"in_{n}", a[n].shape, mybir.dt.from_np(a[n].dtype), kind="ExternalInput").ap() for n in USED}
    out = nc.dram_tensor("out_0", (NB, T, P), F32, kind="ExternalOutput").ap()
    build(nc, ins, out)
    r = run_bass_kernel_spmd(nc, [fed], core_ids=[0])
    return r.results[0]["out_0"]
```

```python
import math
from contextlib import ExitStack

import numpy as np
import concourse.bass as bass
from concourse import mybir

F32 = mybir.dt.float32
F32R = mybir.dt.float32r
BF16 = mybir.dt.bfloat16
ALU = mybir.AluOpType
ACT = mybir.ActivationFunctionType
AX = mybir.AxisListType

P = 128
NB = 8
T = 512
TT = T // P
NE = 8
HC = 4
NH = 16
NS = 8
CHUNK = 64
WIN = 64
NW = T // WIN
HP = 4
DH = 64
HID = 341
MC = 3
MW = 114
LN_EPS = 1e-5
MASKED = -1e30
SS_SCALE = 65536.0


def mm3(pe, out, w, x, start=True, stop=True):
    (wh, wl), (xh, xl) = w, x
    pe.matmul(out, wh, xh, start=start, stop=False)
    pe.matmul(out, wl, xh, start=False, stop=False)
    return pe.matmul(out, wh, xl, start=False, stop=stop)


START = 1


class Phase(ExitStack):

    def __init__(self, nc):
        super().__init__()
        self.nc, self.sems = nc, []
        self.callback(self.clear)

    def sem(self, name):
        self.sems.append(self.nc.alloc_semaphore(name=name))
        return self.sems[-1]

    def block(self):
        engines = (self.nc.tensor, self.nc.scalar, self.nc.vector, self.nc.gpsimd)
        for i, s in enumerate(self.sems):
            engines[i % len(engines)].sem_inc(s, START)
        self.nc.all_engine_barrier()
        return self.enter_context(self.nc.Block())

    def clear(self):
        if self.sems:
            self.nc.clear_and_free_semaphores(self.sems)
            self.nc.all_engine_barrier()


class Mem:
    pass


def seq(t, b):
    return t[:, bass.ds(b * T, T)]


def split_weights(dve, pairs, sem, count):
    for raw, hi, lo in pairs:
        dve.tensor_copy(hi, raw).then_inc(sem, 1)
        count += 1
        dve.wait_ge(sem, count)
        dve.tensor_tensor(lo, raw, hi, ALU.subtract).then_inc(sem, 1)
        count += 1
    return count


def load_phase(nc, m, x_in, consts):
    with Phase(nc) as c:
        xin = c.enter_context(nc.sbuf_tensor("x_tokens", [P, NB * TT, P], F32))
        consts_in = c.sem("consts_in")
        x_tokens_in = c.sem("x_tokens_in")
        turned = c.sem("x_turned")
        stored = c.sem("x_stored")
        made = c.sem("load_made")
        block = c.enter_context(nc.Block())

        @block.sync
        def _(sp):
            sp.dma_start(m.ident[:], consts["ident"]).then_inc(consts_in, 16)
            sp.dma_start(xin[:], x_in.rearrange("b (t p) d -> p (b t) d", p=P)).then_inc(x_tokens_in, 16)
            sp.dma_start(m.center[:], consts["center"]).then_inc(consts_in, 16)
            sp.wait_ge(consts_in, 32)

        @block.vector
        def _(dve):
            dve.memset(m.x[:, NB * T:], 0.0)
            dve.memset(m.mean_of[:], 1.0 / P)
            dve.memset(m.eps[:], LN_EPS)

        @block.tensor
        def _(pe):
            pe.wait_ge(consts_in, 32)
            pe.wait_ge(x_tokens_in, 16)
            for b in range(NB):
                if b >= 2:
                    pe.wait_ge(stored, b - 1)
                for t in range(TT):
                    tr = pe.transpose(m.ps[:, b % 2, t * P:(t + 1) * P], xin[:, b * TT + t, :], m.ident[:])
                tr.then_inc(turned, 1)

        @block.scalar
        def _(act):
            for b in range(NB):
                act.wait_ge(turned, b + 1)
                act.activation(m.x[:, b * T:(b + 1) * T], m.ps[:, b % 2, :], ACT.Copy).then_inc(stored, 1)


def store_phase(nc, m, out):
    with Phase(nc) as c:
        xout = c.enter_context(nc.sbuf_tensor("out_tokens", [P, NB * TT, P], F32))
        turned = c.sem("out_turned")
        ready = c.sem("out_ready")
        written = c.sem("out_written")
        block = c.enter_context(nc.Block())
        dst = out.rearrange("b (t p) d -> p (b t) d", p=P)

        @block.tensor
        def _(pe):
            for b in range(NB):
                if b >= 2:
                    pe.wait_ge(ready, b - 1)
                for t in range(TT):
                    col = b * T + t * P
                    tr = pe.transpose(m.ps[:, b % 2, t * P:(t + 1) * P], m.x[:, col:col + P], m.ident[:])
                tr.then_inc(turned, 1)

        @block.scalar
        def _(act):
            for b in range(NB):
                act.wait_ge(turned, b + 1)
                act.activation(xout[:, b * TT:(b + 1) * TT, :].rearrange("p t d -> p (t d)"),
                               m.ps[:, b % 2, :], ACT.Copy).then_inc(ready, 1)

        @block.sync
        def _(sp):
            for b in range(NB):
                sp.wait_ge(ready, b + 1)
                sp.dma_start(dst[:, b * TT:(b + 1) * TT, :], xout[:, b * TT:(b + 1) * TT, :]).then_inc(written, 16)
            sp.wait_ge(written, 16 * NB)


class Norm:

    def __init__(self, nc, c, m, name, cb, vb, shift=False):
        self.m, self.cb, self.vb, self.shift = m, cb, vb, shift
        sb = lambda n: c.enter_context(nc.sbuf_tensor(f"{name}_{n}", [P, T], F32))
        self.xs, self.sq, self.rstd, self.out = sb("xs"), sb("sq"), sb("rstd"), sb("xn")
        sem = lambda n: c.sem(f"{name}_{n}")
        self.taken, self.centred, self.squared = sem("taken"), sem("centred"), sem("squared")
        self.varied, self.logged, self.scaled, self.normed = sem("varied"), sem("logged"), sem("scaled"), sem("normed")
        self.zeroed = sem("zeroed")

    def start(self, eng):
        if self.shift:
            eng.memset(self.xs[P // 2:, 0:1], 0.0).then_inc(self.zeroed, 1)
            eng.wait_ge(self.zeroed, START + 1)

    def take(self, eng, n, src, b, after=None):
        eng.wait_ge(self.centred, START + n)
        if self.shift:
            eng.tensor_copy(self.xs[:P // 2, :], src[:P // 2, bass.ds(b * T, T)]).then_inc(self.taken, 1)
            eng.tensor_copy(self.xs[P // 2:, 1:], src[P // 2:, bass.ds(b * T, T - 1)]).then_inc(self.taken, 1)
        else:
            eng.tensor_copy(self.xs[:], seq(src, b)).then_inc(self.taken, 1)

    def centre(self, pe, n):
        pe.wait_ge(self.taken, START + (n + 1) * (1 + self.shift))
        pe.wait_ge(self.normed, START + n)
        pe.matmul(self.m.ps[:, self.cb, :], self.m.center[:], self.xs[:], start=True, stop=True).then_inc(self.centred, 1)

    def square(self, act, n):
        act.wait_ge(self.centred, START + n + 1)
        act.wait_ge(self.varied, START + n)
        act.activation(self.sq[:], self.m.ps[:, self.cb, :], ACT.Square).then_inc(self.squared, 1)

    def variance(self, pe, n):
        pe.wait_ge(self.squared, START + n + 1)
        pe.wait_ge(self.logged, START + n)
        pe.matmul(self.m.ps[:, self.vb, :], self.m.mean_of[:], self.sq[:], start=True, stop=True).then_inc(self.varied, 1)

    def scale(self, act, n):
        act.preload_act_table_set(EXP_LN)
        act.wait_ge(self.varied, START + n + 1)
        act.wait_ge(self.normed, START + n)
        act.activation(self.rstd[:], self.m.ps[:, self.vb, :], ACT.Ln, bias=self.m.eps[:, 0:1]).then_inc(self.logged, 1)
        act.wait_ge(self.logged, START + n + 1)
        act.activation(self.rstd[:], self.rstd[:], ACT.Exp, scale=-0.5).then_inc(self.scaled, 1)

    def norm(self, dve, n, out=None):
        dve.wait_ge(self.scaled, START + n + 1)
        dve.tensor_tensor(self.out[:] if out is None else out, self.m.ps[:, self.cb, :], self.rstd[:],
                          ALU.mult).then_inc(self.normed, 1)


def moe_phase(nc, m, app, w, cw_dram):
    NC = NE * HC
    UP = [1, 2, 3, 4]
    YB = [5, 6]
    GB = 7
    SLOTS = 4
    TAKE = 6
    LOOK = 3
    AT_CENTRE, AT_SCALE, AT_NORM, AT_LOGITS, AT_PEAK, AT_WEIGHTS, AT_TURN, AT_KEEP = 3, 6, 8, 11, 11, 18, 24, 25
    by_dve = lambda i: i % 2 == 0
    ROUNDED = [sum(by_dve(j) == k for j in range(NC)) for k in (False, True)]
    nth = lambda i: sum(by_dve(j) == by_dve(i) for j in range(i))
    with Phase(nc) as c:
        name = f"moe{app}"
        sb = lambda n, s, d=F32: c.enter_context(nc.sbuf_tensor(f"{name}_{n}", s, d))
        sem = lambda n: c.sem(f"{name}_{n}")
        ln = Norm(nc, c, m, name + "_ln", 0, GB)
        xh, xl = sb("xh", [P, T], F32R), sb("xl", [P, T], F32R)
        g32 = sb("g32", [P, SLOTS, T])
        gh, gl = sb("gh", [P, SLOTS, T], F32R), sb("gl", [P, SLOTS, T], F32R)
        cwb = sb("cwb", [P, NE, T])
        part, acc = sb("part", [P, 2, T]), sb("acc", [P, T])
        peak, total, rtotal = sb("peak", [P, TT]), sb("total", [P, TT]), sb("rtotal", [P, TT])
        gate = sb("gate", [P, TT, NE])
        more, ties = sb("more", [P, TT, NE, NE]), sb("ties", [P, TT, NE, NE])
        rank, cw = sb("rank", [P, TT, NE]), sb("cw", [P, TT, NE])
        cwt = sb("cwt", [NE, T])
        split, up_done, gelu_done, rounded, lo_done = sem("split"), sem("up_done"), sem("gelu_done"), sem("rounded"), sem("lo_done")
        copied = sem("copied")
        down_done, part_done, summed, x_done = sem("down_done"), sem("part_done"), sem("summed"), sem("x_done")
        logits_done, peeled, exped, gated, turned = sem("logits"), sem("peeled"), sem("exped"), sem("gated"), sem("turned")
        cwt_done, cw_out, gchain, xh_done = sem("cwt_done"), sem("cw_out"), sem("gchain"), sem("xh_done")
        wchain = sem("wchain")
        cw_in = [sem(f"cw_in{e}") for e in range(NE)]
        GSTEPS = 8
        block = c.block()

        @block.tensor
        def _(pe):
            def logits(n):
                pe.wait_ge(ln.normed, START + n + 1)
                pe.wait_ge(cwt_done, START + n)
                for t in range(TT):
                    mm = pe.matmul(m.ps[:, GB, t * NE:(t + 1) * NE], ln.out[:, t * P:(t + 1) * P], w.gate[:],
                                   start=True, stop=True)
                mm.then_inc(logits_done, 1)

            def turn(n):
                pe.wait_ge(gated, START + n + 1)
                for t in range(TT):
                    tr = pe.transpose(m.ps[:NE, GB, t * P:(t + 1) * P], cw[:, t, :], m.ident[:])
                tr.then_inc(turned, 1)

            def up(b, i):
                if i >= len(UP):
                    j = i - len(UP)
                    if by_dve(j):
                        pe.wait_ge(gelu_done, START + b * NC + j + 1)
                    else:
                        pe.wait_ge(rounded, START + b * ROUNDED[0] + nth(j) + 1)
                cols = slice((i % HC) * P, (i % HC + 1) * P)
                mm3(pe, m.ps[:, UP[i % len(UP)], :], (w.w1h[:, i // HC, cols], w.w1l[:, i // HC, cols]),
                    (xh[:], xl[:])).then_inc(up_done, 1)

            def down(b, i):
                e, k = i // HC, i % HC
                pe.wait_ge(lo_done, START + b * NC + i + 1 + SLOTS)
                if k == 0:
                    pe.wait_ge(part_done, START + b * NE + e + 1)
                s = i % SLOTS
                mm3(pe, m.ps[:, YB[e % 2], :], (w.w2h[:, e, k, :], w.w2l[:, e, k, :]), (gh[:, s, :], gl[:, s, :]),
                    start=(k == 0), stop=(k == HC - 1)).then_inc(down_done, 1)

            ln.centre(pe, 0)
            ln.variance(pe, 0)
            logits(0)
            turn(0)
            with pe.Fori(0, NB) as b:
                pe.wait_ge(split, START + b + 1)
                for i in range(NC + LOOK):
                    if i < NC:
                        up(b, i)
                    if i >= LOOK:
                        down(b, i - LOOK)
                    if i == AT_CENTRE:
                        ln.centre(pe, b + 1)
                    if i == AT_SCALE:
                        pe.wait_ge(cwt_done, START + b + 1)
                        ln.variance(pe, b + 1)
                    if i == AT_LOGITS:
                        logits(b + 1)
                    if i == AT_TURN:
                        turn(b + 1)

        @block.scalar
        def _(act):
            def exps(n):
                act.wait_ge(peeled, START + n + 1)
                act.wait_ge(gated, START + n)
                act.activation(gate[:], gate[:], ACT.Exp).then_inc(exped, 1)

            ln.square(act, 0)
            ln.scale(act, 0)
            exps(0)
            with act.Fori(0, NB) as b:
                for i in range(NC):
                    s = i % SLOTS
                    e, k = i // HC, i % HC
                    act.wait_ge(up_done, START + b * NC + i + 1)
                    act.wait_ge(lo_done, START + b * NC + i + 1)
                    act.activation(g32[:, s, :], m.ps[:, UP[i % len(UP)], :], ACT.Gelu,
                                   bias=w.b1[:, i:i + 1]).then_inc(gelu_done, 1)
                    if not by_dve(i):
                        act.wait_ge(down_done, START + b * NC + i + 1)
                        act.activation(gh[:, s, :], m.ps[:, UP[i % len(UP)], :], ACT.Gelu,
                                       bias=w.b1[:, i:i + 1]).then_inc(rounded, 1)
                    if i == AT_CENTRE:
                        ln.square(act, b + 1)
                    if i == AT_SCALE:
                        ln.scale(act, b + 1)
                    if i == AT_PEAK + 1:
                        exps(b + 1)

        @block.vector
        def _(dve):
            def gates(n):
                l3 = m.ps[:, GB, :TT * NE].rearrange("p (t e) -> p t e", e=NE)
                dve.wait_ge(logits_done, START + n + 1)
                dve.tensor_reduce(peak[:], l3, AX.X, ALU.max).then_inc(gchain, 1)
                dve.wait_ge(gchain, START + n * GSTEPS + 1)
                dve.tensor_tensor(gate[:], l3, peak[:].unsqueeze(2).to_broadcast([P, TT, NE]),
                                  ALU.subtract).then_inc(peeled, 1)

            def weights(n, step):
                a = gate[:].unsqueeze(2).to_broadcast([P, TT, NE, NE])
                z = gate[:].unsqueeze(3).to_broadcast([P, TT, NE, NE])
                if step == 0:
                    dve.wait_ge(exped, START + n + 1)
                    dve.tensor_reduce(total[:], gate[:], AX.X, ALU.add).then_inc(gchain, 1)
                    dve.tensor_tensor(more[:], a, z, ALU.is_gt).then_inc(gchain, 1)
                    dve.tensor_tensor(ties[:], a, z, ALU.is_ge).then_inc(gchain, 1)
                elif step == 1:
                    dve.wait_ge(gchain, START + n * GSTEPS + 4)
                    dve.reciprocal(rtotal[:], total[:]).then_inc(gchain, 1)
                    dve.tensor_tensor(ties[:], ties[:], m.before[:].unsqueeze(1).to_broadcast([P, TT, NE, NE]),
                                      ALU.mult).then_inc(gchain, 1)
                elif step == 2:
                    dve.wait_ge(gchain, START + n * GSTEPS + 6)
                    dve.tensor_tensor(more[:], more[:], ties[:], ALU.max).then_inc(gchain, 1)
                elif step == 3:
                    dve.wait_ge(gchain, START + n * GSTEPS + 7)
                    dve.tensor_reduce(rank[:], more[:], AX.X, ALU.add).then_inc(gchain, 1)
                    dve.wait_ge(gchain, START + n * GSTEPS + 8)
                    dve.wait_ge(turned, START + n)
                    dve.scalar_tensor_tensor(out=cw[:], in0=rank[:], scalar=2.0, in1=gate[:], op0=ALU.is_lt,
                                             op1=ALU.mult).then_inc(wchain, 1)
                    dve.wait_ge(wchain, START + n + 1)
                    dve.tensor_tensor(cw[:], cw[:], rtotal[:].unsqueeze(2).to_broadcast([P, TT, NE]),
                                      ALU.mult).then_inc(gated, 1)

            def keep_cwt(n):
                dve.wait_ge(turned, START + n + 1)
                dve.wait_ge(cw_out, START + 16 * n)
                dve.tensor_copy(cwt[:], m.ps[:NE, GB, :]).then_inc(cwt_done, 1)

            def halves(n):
                dve.wait_ge(up_done, START + n * NC)
                dve.wait_ge(ln.normed, START + n + 1)
                dve.tensor_copy(xh[:], ln.out[:]).then_inc(xh_done, 1)
                dve.wait_ge(xh_done, START + n + 1)
                dve.tensor_tensor(xl[:], ln.out[:], xh[:], ALU.subtract).then_inc(split, 1)

            def take_part(b, e):
                dve.wait_ge(down_done, START + b * NC + HC * (e + 1) + SLOTS)
                dve.wait_ge(cw_in[e], START + 16 * (b + 1))
                if e >= 2:
                    dve.wait_ge(summed, START + b * (NE - 1) + e - 1)
                else:
                    dve.wait_ge(summed, START + b * (NE - 1))
                dve.scalar_tensor_tensor(out=part[:, e % 2, :], in0=m.ps[:, YB[e % 2], :], scalar=w.b2[:, e:e + 1],
                                         in1=cwb[:, e, :], op0=ALU.add, op1=ALU.mult).then_inc(part_done, 1)

            dve.sem_inc(lo_done, SLOTS)
            dve.sem_inc(down_done, SLOTS)
            dve.sem_inc(part_done, 2)
            ln.norm(dve, 0)
            gates(0)
            for step in range(4):
                weights(0, step)
            keep_cwt(0)
            halves(0)
            with dve.Fori(0, NB) as b:
                for i in range(NC - HC + TAKE + 1):
                    if i < NC:
                        s = i % SLOTS
                        if by_dve(i):
                            dve.wait_ge(down_done, START + b * NC + i + 1)
                            dve.wait_ge(gelu_done, START + b * NC + i + 1)
                            dve.tensor_copy(gh[:, s, :], g32[:, s, :]).then_inc(copied, 1)
                            dve.wait_ge(copied, START + b * ROUNDED[1] + nth(i) + 1)
                        else:
                            dve.wait_ge(rounded, START + b * ROUNDED[0] + nth(i) + 1)
                        dve.tensor_tensor(gl[:, s, :], g32[:, s, :], gh[:, s, :], ALU.subtract).then_inc(lo_done, 1)
                    if i >= TAKE and (i - TAKE) % HC == 0 and (i - TAKE) // HC < NE:
                        take_part(b, (i - TAKE) // HC)
                    if i == AT_NORM:
                        ln.norm(dve, b + 1)
                    if i == AT_PEAK:
                        gates(b + 1)
                    if 0 <= i - AT_WEIGHTS < 4:
                        weights(b + 1, i - AT_WEIGHTS)
                    if i == AT_KEEP:
                        keep_cwt(b + 1)
                    if i == NC:
                        halves(b + 1)
                dve.wait_ge(summed, START + (b + 1) * (NE - 1))
                dve.scalar_tensor_tensor(out=seq(m.x, b), in0=acc[:], scalar=0.5, in1=seq(m.x, b), op0=ALU.mult,
                                         op1=ALU.add).then_inc(x_done, 1)

        @block.gpsimd
        def _(pool):
            ln.take(pool, 0, m.x, 0)
            with pool.Fori(0, NB) as b:
                ln.take(pool, b + 1, m.x, b + 1)
                for e in range(1, NE):
                    pool.wait_ge(part_done, START + b * NE + e + 1 + 2)
                    if e == 1:
                        pool.wait_ge(x_done, START + b)
                        pool.tensor_tensor(acc[:], part[:, 0, :], part[:, 1, :], ALU.add).then_inc(summed, 1)
                    else:
                        pool.wait_ge(summed, START + b * (NE - 1) + e - 1)
                        pool.tensor_tensor(acc[:], acc[:], part[:, e % 2, :], ALU.add).then_inc(summed, 1)

        @block.sync
        def _(sp):
            def spread(n, used=None):
                sp.wait_ge(cwt_done, START + n + 1)
                if used is not None:
                    for e in range(NE):
                        sp.wait_ge(cw_in[e], START + 16 * used + 16)
                sp.dma_start(cw_dram[:], cwt[:]).then_inc(cw_out, 16)
                sp.wait_ge(cw_out, START + 16 * (n + 1))
                for e in range(NE):
                    if used is not None:
                        sp.wait_ge(part_done, START + used * NE + e + 1 + 2)
                    sp.dma_start(cwb[:, e, :], cw_dram[e:e + 1, :].to_broadcast([P, T])).then_inc(cw_in[e], 16)

            spread(0)
            with sp.Fori(0, NB) as b:
                spread(b + 1, used=b)
            for e in range(NE):
                sp.wait_ge(cw_in[e], START + 16 * (NB + 1))


def moe_weights(nc, c, m, ins):
    w = Mem()
    sb = lambda n, s, d=F32: c.enter_context(nc.sbuf_tensor(n, s, d))
    w.w1h, w.w1l = sb("w1h", [P, NE, T], F32R), sb("w1l", [P, NE, T], F32R)
    w.w2h, w.w2l = sb("w2h", [P, NE, HC, P], F32R), sb("w2l", [P, NE, HC, P], F32R)
    w.b1, w.b2, w.gate = sb("b1", [P, NE * HC]), sb("b2", [P, NE]), sb("w_gate", [P, NE])
    with Phase(nc) as s:
        raw1 = s.enter_context(nc.sbuf_tensor("raw_w1", [P, NE, T], F32))
        raw2 = s.enter_context(nc.sbuf_tensor("raw_w2", [P, NE, HC, P], F32))
        w1_in, w2_in, rest_in = (s.sem(n) for n in ("w1_in", "w2_in", "moe_rest_in"))
        steps = s.sem("moe_split_steps")
        block = s.enter_context(nc.Block())

        @block.sync
        def _(sp):
            sp.dma_start(raw1[:], ins["L0_ffn_W1"].rearrange("e d h -> d e h")).then_inc(w1_in, 16)
            sp.dma_start(w.gate[:], ins["gate_t"]).then_inc(rest_in, 16)
            sp.dma_start(w.b1[:], ins["b1_t"]).then_inc(rest_in, 16)
            sp.dma_start(w.b2[:], ins["b2_t"]).then_inc(rest_in, 16)
            sp.dma_start(m.before[:], ins["before"]).then_inc(rest_in, 16)
            sp.wait_ge(rest_in, 64)

        @block.scalar
        def _(act):
            act.dma_start(raw2[:], ins["L0_ffn_W2"].rearrange("e (k p) d -> p e k d", p=P)).then_inc(w2_in, 16)

        @block.vector
        def _(dve):
            dve.wait_ge(w1_in, 16)
            n = split_weights(dve, [(raw1[:], w.w1h[:], w.w1l[:])], steps, 0)
            dve.wait_ge(w2_in, 16)
            split_weights(dve, [(raw2[:], w.w2h[:], w.w2l[:])], steps, n)
    return w


def ssm_phase(nc, m, ins):
    with Phase(nc) as c:
        sb = lambda n, s, d=F32: c.enter_context(nc.sbuf_tensor(f"ssm_{n}", s, d))
        sem = lambda n: c.sem(f"ssm_{n}")
        ln = Norm(nc, c, m, "ssm_ln", 0, 1)
        DTB, ZB = 2, 3
        CONV = 4
        w_in = sb("w_in", [P, 3 * P])
        w_dt, w_dtx = sb("w_dt", [P, 2 * P - NH]), sb("w_dtx", [P, P])
        w_out = sb("w_out", [P, P])
        conv_w, conv_b = sb("conv_w", [P, 3, 4]), sb("conv_b", [P, 3])
        a_par, dt_b = sb("a_par", [P, 2]), sb("dt_b", [P, 2])
        spread_p, gather_p = sb("spread_p", [P, NS, P]), sb("gather_p", [P, NS, P])
        spread_h = sb("spread_h", [P, NB, P])
        chunk_mask = sb("chunk_mask", [P, T])
        raw = sb("raw", [P, 3, T + 3])
        cbx = sb("cbx", [P, 3, T])
        z, az, ez, lz = (sb(n, [P, 2, T]) for n in ("z", "az", "ez", "lz"))
        cum, grow, fall = (sb(n, [P, 2, T]) for n in ("cum", "grow", "fall"))
        carry = sb("carry", [P, 2, T])
        state, rnorm = sb("state", [P, T]), sb("rnorm", [P, T])
        be, ce = sb("be", [P, T]), sb("ce", [P, T])
        d1, g, cg = sb("d1", [P, 2, T]), sb("g", [P, 2, T]), sb("cg", [P, 2, T])
        y, yb = sb("y", [P, T]), sb("yb", [P, 2, T])
        ins_in, zeroed, stepped, conved = sem("ins_in"), sem("zeroed"), sem("stepped"), sem("conv_in")
        chain, absd, exped, logged, curves = sem("chain"), sem("absd"), sem("exped"), sem("logged"), sem("curves")
        xrep, cg_done, y_done, d1_done = sem("xrep"), sem("cg_done"), sem("y_done"), sem("d1_done")
        rn_ready, yb_done, out_done, x_done, y_kept = sem("rn_ready"), sem("yb_done"), sem("out_done"), sem("x_done"), sem("y_kept")
        rnormed, raw_done, cx_done, cum_done = sem("rnormed"), sem("raw_done"), sem("cx_done"), sem("cum_done")
        block = c.block()
        LOADS = [(w_in, "ssm_w_in"), (w_dtx, "ssm_w_dtx"), (w_out, "ssm_w_out"), (conv_w, "ssm_conv_w"),
                 (conv_b, "ssm_conv_b"), (a_par, "ssm_a"), (dt_b, "ssm_dt_b"), (spread_p, "spread_p"),
                 (gather_p, "gather_p"), (spread_h, "spread_h"), (chunk_mask, "chunk_mask")]

        @block.sync
        def _(sp):
            for t, n in LOADS:
                sp.dma_start(t[:], ins[n]).then_inc(ins_in, 16)
            sp.wait_ge(zeroed, START + 1)
            sp.dma_start(w_dt[:, P - NH:P], ins["ssm_w_dt"]).then_inc(ins_in, 16)

        ALL_IN = 16 * (len(LOADS) + 1)

        @block.gpsimd
        def _(pool):
            pool.memset(w_dt[:], 0.0).then_inc(zeroed, 1)
            pool.memset(raw[:, :, 0:3], 0.0).then_inc(zeroed, 1)
            for b in range(NB):
                ln.take(pool, b, m.x, b)

        @block.tensor
        def _(pe):
            pe.wait_ge(ins_in, START + ALL_IN)
            for b in range(NB + 1):
                if b < NB:
                    ln.centre(pe, b)
                if b > 0:
                    pe.wait_ge(ln.normed, START + b)
                    lo = P - NH - NH * (b - 1)
                    pe.matmul(m.ps[:, DTB, :], w_dt[:, lo:lo + P], ln.out[:], start=(b == 1), stop=(b == NB)).then_inc(stepped, 1)
                    if b == 1:
                        for k in range(3):
                            pe.matmul(m.ps[:, CONV + k, :], w_in[:, k * P:(k + 1) * P], ln.out[:], start=True,
                                      stop=True).then_inc(conved, 1)
                        pe.matmul(m.ps[:, ZB, :], w_dtx[:], ln.out[:], start=True, stop=True).then_inc(conved, 1)
                if b < NB:
                    ln.variance(pe, b)
            pe.wait_ge(cx_done, START + 1)
            for p in range(NS + 1):
                if p < NS:
                    if p >= 2:
                        pe.wait_ge(d1_done, START + p - 1)
                    elif p == 0:
                        pe.wait_ge(ln.normed, START + NB)
                        pe.wait_ge(ln.logged, START + NB)
                    pe.matmul(m.ps[:, p % 2, :], spread_p[:, p, :], cbx[:, 2, :], start=True, stop=True).then_inc(xrep, 1)
                if p > 0:
                    pe.wait_ge(cg_done, START + p)
                    pe.matmul(m.ps[:, 7, :], gather_p[:, p - 1, :], cg[:, (p - 1) % 2, :], start=(p == 1),
                              stop=(p == NS)).then_inc(y_done, 1)
            pe.wait_ge(rnormed, START + 1)
            for b in range(NB + 1):
                if b < NB:
                    if b >= 2:
                        pe.wait_ge(yb_done, START + b - 1)
                    pe.matmul(m.ps[:, b % 2, :], spread_h[:, b, :], rnorm[:], start=True, stop=True).then_inc(rn_ready, 1)
                if b > 0:
                    pe.wait_ge(yb_done, START + b)
                    if b > 2:
                        pe.wait_ge(x_done, START + b - 2)
                    pe.matmul(m.ps[:, 2 + b % 2, :], w_out[:], yb[:, (b - 1) % 2, :], start=True, stop=True).then_inc(out_done, 1)

        @block.scalar
        def _(act):
            for b in range(NB):
                ln.square(act, b)
                ln.scale(act, b)
                if b == 0:
                    act.wait_ge(conved, START + 3)
                    act.wait_ge(zeroed, START + 2)
                    for k in range(3):
                        act.activation(raw[:, k, 3:], m.ps[:, CONV + k, :], ACT.Copy).then_inc(raw_done, 1)
            act.wait_ge(absd, START + 1)
            act.activation(ez[:], az[:], ACT.Exp, scale=-1.0).then_inc(exped, 1)
            act.wait_ge(exped, START + 1)
            act.activation(lz[:], ez[:], ACT.Ln, bias=1.0).then_inc(logged, 1)
            act.wait_ge(cum_done, START + 1)
            act.activation(fall[:], cum[:], ACT.Exp, scale=-1.0).then_inc(curves, 1)
            act.activation(grow[:], cum[:], ACT.Exp).then_inc(curves, 1)

        @block.vector
        def _(dve):
            count = [0]

            def step(ins_):
                ins_.then_inc(chain, 1)
                count[0] += 1
                dve.wait_ge(chain, START + count[0])

            dve.wait_ge(ins_in, START + ALL_IN)
            for b in range(NB):
                if b >= 1:
                    dve.wait_ge(stepped, START + b)
                    if b == 1:
                        dve.wait_ge(conved, START + 4)
                ln.norm(dve, b)
            dve.wait_ge(raw_done, START + 3)
            for k in range(3):
                step(dve.tensor_scalar(cbx[:, k, :], raw[:, k, 0:T], conv_w[:, k, 0:1], conv_b[:, k:k + 1], ALU.mult, ALU.add))
                for j in range(1, 4):
                    step(dve.scalar_tensor_tensor(out=cbx[:, k, :], in0=raw[:, k, j:j + T], scalar=conv_w[:, k, j:j + 1],
                                                  in1=cbx[:, k, :], op0=ALU.mult, op1=ALU.add))
            dve.sem_inc(cx_done, 1)
            dve.wait_ge(stepped, START + NB)
            for i in range(2):
                step(dve.tensor_scalar(z[:, i, :], m.ps[:, DTB + i, :], dt_b[:, i:i + 1], None, ALU.add))
            step(dve.tensor_scalar(az[:], z[:], -1.0, None, ALU.mult))
            dve.tensor_tensor(az[:], az[:], z[:], ALU.max).then_inc(absd, 1)
            dve.wait_ge(logged, START + 1)
            step(dve.scalar_tensor_tensor(out=z[:], in0=z[:], scalar=0.0, in1=lz[:], op0=ALU.max, op1=ALU.add))
            for i in range(2):
                step(dve.tensor_scalar(z[:, i, :], z[:, i, :], a_par[:, i:i + 1], None, ALU.mult))
            for i in range(2):
                step(dve.tensor_tensor_scan(cum[:, i, :], chunk_mask[:], z[:, i, :], 0.0, ALU.mult, ALU.add))
            dve.sem_inc(cum_done, 1)
            dve.wait_ge(curves, START + 2)
            for i in range(2):
                step(dve.memset(carry[:, i, :], 1.0))
                step(dve.tensor_copy(carry[:, i, CHUNK::CHUNK], grow[:, i, CHUNK - 1:T - 1:CHUNK]))
            step(dve.tensor_tensor_scan(state[:], carry[:, 0, :], fall[:, 0, :], 0.0, ALU.mult, ALU.add))
            step(dve.tensor_tensor(state[:], state[:], grow[:, 0, :], ALU.mult))
            dve.reciprocal(rnorm[:], state[:]).then_inc(rnormed, 1)
            step(dve.tensor_tensor(be[:], cbx[:, 1, :], fall[:, 1, :], ALU.mult))
            step(dve.tensor_tensor(ce[:], cbx[:, 0, :], grow[:, 1, :], ALU.mult))
            for p in range(NS):
                s = p % 2
                dve.wait_ge(xrep, START + p + 1)
                dve.tensor_tensor(d1[:, s, :], m.ps[:, s, :], be[:], ALU.mult).then_inc(d1_done, 1)
                dve.wait_ge(d1_done, START + p + 1)
                step(dve.tensor_tensor_scan(g[:, s, :], carry[:, 1, :], d1[:, s, :], 0.0, ALU.mult, ALU.add))
                if p >= 2:
                    dve.wait_ge(y_done, START + p - 1)
                dve.tensor_tensor(cg[:, s, :], g[:, s, :], ce[:], ALU.mult).then_inc(cg_done, 1)
            dve.wait_ge(y_done, START + NS)
            dve.tensor_copy(y[:], m.ps[:, 7, :]).then_inc(y_kept, 1)
            dve.wait_ge(y_kept, START + 1)
            for b in range(NB + 1):
                if b < NB:
                    dve.wait_ge(rn_ready, START + b + 1)
                    if b >= 2:
                        dve.wait_ge(out_done, START + b - 1)
                    dve.tensor_tensor(yb[:, b % 2, :], m.ps[:, b % 2, :], y[:], ALU.mult).then_inc(yb_done, 1)
                if b > 0:
                    dve.wait_ge(out_done, START + b)
                    xb = m.x[:, (b - 1) * T:b * T]
                    dve.tensor_tensor(xb, m.ps[:, 2 + b % 2, :], xb, ALU.add).then_inc(x_done, 1)


EXP_LN = "natural_log_exp_and_others"


def entry_phase(nc, m, app):
    with Phase(nc) as c:
        lns = [Norm(nc, c, m, f"entry{app}_{i}", 2 * i, 2 * i + 1) for i in range(2)]
        block = c.block()

        @block.gpsimd
        def _(pool):
            with pool.Fori(0, NB // 2) as i:
                for k in range(2):
                    lns[k].take(pool, i, m.x, 2 * i + k)

        @block.tensor
        def _(pe):
            with pe.Fori(0, NB // 2) as i:
                for k in range(2):
                    lns[k].centre(pe, i)
                for k in range(2):
                    lns[k].variance(pe, i)

        @block.scalar
        def _(act):
            with act.Fori(0, NB // 2) as i:
                for k in range(2):
                    lns[k].square(act, i)
                for k in range(2):
                    lns[k].scale(act, i)

        @block.vector
        def _(dve):
            with dve.Fori(0, NB // 2) as i:
                for k in range(2):
                    lns[k].norm(dve, i, seq(m.u, 2 * i + k))


def extras_phase(nc, c, m, ins):
    sb = lambda n, s, d=F32: c.enter_context(nc.sbuf_tensor(n, s, d))
    m.per_head, m.ident_bf, m.masks = sb("per_head", [P, P]), sb("ident_bf", [P, P], BF16), sb("masks_bf", [P, 2, T], BF16)
    m.tiny, m.unscale = sb("tiny", [P, 1]), sb("unscale", [P, 2])
    with Phase(nc) as s:
        raw = s.enter_context(nc.sbuf_tensor("raw_masks", [P, 2, T], F32))
        extras_in = s.sem("extras_in")
        block = s.enter_context(nc.Block())

        @block.sync
        def _(sp):
            sp.dma_start(raw[:], ins["masks"]).then_inc(extras_in, 16)
            sp.dma_start(m.per_head[:], ins["per_head"]).then_inc(extras_in, 16)
            sp.wait_ge(extras_in, 32)

        @block.vector
        def _(dve):
            dve.memset(m.tiny[:], 2.0 ** -64)
            dve.memset(m.unscale[:, 0:1], 8 * math.log(2.0) + math.log(8.0))
            dve.memset(m.unscale[:, 1:2], 8 * math.log(2.0))
            dve.memset(m.u[:, NB * T:], 0.0)
            dve.tensor_copy(m.ident_bf[:], m.ident[:])
            dve.wait_ge(extras_in, 32)
            dve.tensor_copy(m.masks[:], raw[:])


def gated_weights(nc, c, m, ins):
    ws = []
    sb = lambda n, s, d=F32: c.enter_context(nc.sbuf_tensor(n, s, d))
    for l in range(2):
        w = Mem()
        w.qkh, w.qkl = sb(f"wqk_h{l}", [P, 4, T], F32R), sb(f"wqk_l{l}", [P, 4, T], F32R)
        w.vh, w.vl = sb(f"wv_h{l}", [P, T], F32R), sb(f"wv_l{l}", [P, T], F32R)
        w.wo = sb(f"wo{l}", [P, HP, P])
        w.w1h, w.w1l = sb(f"w1_h{l}", [P, 2 * HID], F32R), sb(f"w1_l{l}", [P, 2 * HID], F32R)
        w.w2 = sb(f"w2_{l}", [P, MC, P])
        w.bias, w.b2 = sb(f"w1_bias{l}", [P, 2 * MC]), sb(f"b2_{l}", [P, 1])
        w.tables = sb(f"tables{l}", [P, 4, T])
        ws.append(w)
    with Phase(nc) as s:
        tb = lambda n, sh, d=F32: s.enter_context(nc.sbuf_tensor(n, sh, d))
        raw, raw1 = tb("raw_qkv", [P, 3 * T]), tb("raw_gated_w1", [P, 2 * HID])
        scales, lnw, b1 = tb("qk_scales", [P, 2, 4]), tb("ln_w", [P, 2, 2]), tb("b1_raw", [P, 2, 2 * MC])
        raw_in, rest_in, biased, steps = (s.sem(n) for n in ("gw_raw", "gw_rest", "gw_biased", "gw_steps"))
        rest2_in, cleared = s.sem("gw_rest2"), s.sem("gw_cleared")
        block = s.enter_context(nc.Block())
        LAYER_STEPS = 2 * 7 + 4 + 2 + 2
        REST = 16 * (3 + 2 * 4)

        @block.sync
        def _(sp):
            sp.dma_start(scales[:], ins["qk_scales"]).then_inc(rest_in, 16)
            sp.dma_start(lnw[:], ins["ln_w"]).then_inc(rest_in, 16)
            sp.dma_start(b1[:], ins["b1_gated"]).then_inc(rest_in, 16)
            for l, w in enumerate(ws):
                sp.dma_start(w.tables[:], ins["rotary"]).then_inc(rest_in, 16)
                sp.dma_start(w.wo[:], ins["L1_ffn_wo"][l].rearrange("(j p) d -> p j d", p=P)).then_inc(rest_in, 16)
                sp.dma_start(w.w2[:MW, 0:2, :], ins["L1_ffn_w2"][l][0:2 * MW, :].rearrange("(j p) d -> p j d", p=MW)).then_inc(rest_in, 16)
                sp.dma_start(w.w2[:HID - 2 * MW, 2, :], ins["L1_ffn_w2"][l][2 * MW:HID, :]).then_inc(rest_in, 16)
                sp.dma_start(w.b2[:], ins["b2_gated"][l]).then_inc(rest2_in, 16)
            for l, w in enumerate(ws):
                if l:
                    sp.wait_ge(steps, LAYER_STEPS)
                    sp.wait_ge(biased, 1)
                sp.dma_start(raw[:], ins["L1_ffn_wqkv"][l]).then_inc(raw_in, 16)
                sp.dma_start(raw1[:], ins["L1_ffn_w1"][l]).then_inc(raw_in, 16)
            sp.wait_ge(rest2_in, 32)

        @block.vector
        def _(dve):
            n = 0
            dve.memset(m.ps[:, 0:2, :2 * MC], 0.0).then_inc(cleared, 1)
            dve.wait_ge(rest_in, REST)
            for l, w in enumerate(ws):
                dve.wait_ge(raw_in, 32 * (l + 1))
                sw = lambda t: t.rearrange("p (h s j) -> p h s j", s=2, j=DH // 2)
                pairs = [(raw[:, 2 * T:], w.vh[:], w.vl[:])]
                for i in range(2):
                    src = raw[:, i * T:(i + 1) * T]
                    pairs.append((src, w.qkh[:, 2 * i, :], w.qkl[:, 2 * i, :]))
                    for half in range(2):
                        pairs.append((sw(src)[:, :, 1 - half, :], sw(w.qkh[:, 2 * i + 1, :])[:, :, half, :],
                                      sw(w.qkl[:, 2 * i + 1, :])[:, :, half, :]))
                n = split_weights(dve, pairs, steps, n)
                for k in range(4):
                    dve.tensor_scalar(w.tables[:, k, :], w.tables[:, k, :], scales[:, l, k:k + 1], None,
                                      ALU.mult).then_inc(steps, 1)
                    n += 1
                dve.wait_ge(biased, l + 1)
                dve.tensor_tensor(w.bias[:], m.ps[:, l, :2 * MC], b1[:, l, :], ALU.add).then_inc(steps, 1)
                dve.tensor_scalar(raw1[:], raw1[:], lnw[:, l, 0:1], None, ALU.mult).then_inc(steps, 1)
                n += 2
                dve.wait_ge(steps, n)
                n = split_weights(dve, [(raw1[:], w.w1h[:], w.w1l[:])], steps, n)
                assert n == (l + 1) * LAYER_STEPS

        @block.tensor
        def _(pe):
            pe.wait_ge(rest_in, REST)
            pe.wait_ge(cleared, 1)
            for l in range(2):
                pe.wait_ge(raw_in, 32 * (l + 1))
                for i in range(2 * MC):
                    lo = (i // MC) * HID + (i % MC) * MW
                    n = min(MW, HID - (i % MC) * MW)
                    mm = pe.matmul(m.ps[:n, l, i:i + 1], raw1[:, lo:lo + n], lnw[:, l, 1:2], start=True, stop=True)
                mm.then_inc(biased, 1)
    return ws


def attention_phase(nc, m, app, l, w):
    Q, QR, K, KR, S, PT, O = 0, 1, 2, 3, 4, 6, 7
    HW = NW // 2
    NT = T // P
    ORDER = [1, 0, 3, 2]
    V_ORDER = [0, 2, 1, 3]
    V_BANK = [0, 1, 0, 0]
    V_TILES = [[t for t in V_ORDER if V_BANK[t] == k] for k in range(2)]
    with Phase(nc) as c:
        name = f"att{app}{l}"
        sb = lambda n, s, d=F32: c.enter_context(nc.sbuf_tensor(f"{name}_{n}", s, d))
        sem = lambda n: c.sem(f"{name}_{n}")
        hs = sb("hs", [P, T])
        hh, hl = sb("hh", [P, T], F32R), sb("hl", [P, T], F32R)
        v, v_even = sb("v", [P, NT, T]), sb("v_even", [P, NT, T])
        turned = sb("turned", [P, 4, T])
        sums = sb("sums", [P, 2, T])
        squares = sb("squares", [P, 2, T])
        rn = sb("rn", [P, 2, T])
        qn, kn = sb("qn", [P, 2, T]), sb("kn", [P, 2, 2 * (NT + 1), WIN])
        probs = sb("probs", [P, 2, NW, P])
        nmax, psum_, rsum = sb("nmax", [P, 2, NW]), sb("psum", [P, 2, NW]), sb("rsum", [P, 2, NW])
        pts = sb("pts", [P, 2, T])
        o = sb("o", [P, HP, T])
        zeroed, taken, hi_done, split = sem("zeroed"), sem("taken"), sem("hi_done"), sem("split")
        projected, rotated, squared, added = sem("projected"), sem("rotated"), sem("squared"), sem("added")
        ss_done, ss_logged, rn_done, qk_done = sem("ss_done"), sem("ss_logged"), sem("rn_done"), sem("qk_done")
        sim_done, maxed, exped, recip, normed = sem("sim_done"), sem("maxed"), sem("exped"), sem("recip"), sem("normed")
        pt_done, pt_kept0, pt_kept1, pv_done = sem("pt_done"), sem("pt_kept0"), sem("pt_kept1"), sem("pv_done")
        zeroed2 = sem("zeroed2")
        o_kept, wo_done, u_done = sem("o_kept"), sem("wo_done"), sem("u_done")
        v_done, v_kept0, v_kept1, v_copied = sem("v_done"), sem("v_kept0"), sem("v_kept1"), sem("v_copied")
        block = c.block()
        pt_kept = [pt_kept0, pt_kept1]
        v_kept = [v_kept0, v_kept1]

        @block.tensor
        def _(pe):
            def project(n, j, kinds):
                cols = slice(j * P, (j + 1) * P)
                for k in kinds:
                    if k % 2 == 0:
                        pe.wait_ge(ss_logged, START + 2 * n + k // 2 + 1)
                    else:
                        pe.wait_ge(rotated, START + 4 * n + k)
                    mm3(pe, m.ps[:, Q + k, :], (w.qkh[:, k, cols], w.qkl[:, k, cols]),
                        (hh[:], hl[:])).then_inc(projected, 1)

            def norms(n, i):
                pe.wait_ge(squared, START + 2 * n + i + 1)
                pe.wait_ge(rotated, START + 4 * n + 2 * i + 2 + 4)
                pe.matmul(m.ps[:, Q + 2 * i, :], m.per_head[:], squares[:, i, :], start=True, stop=True).then_inc(ss_done, 1)

            def sims(n, j):
                for half in range(2):
                    if half == 0:
                        pe.wait_ge(qk_done, START + 2 * n + 2)
                    pe.wait_ge(exped, START + NW * n + HW * (half + 1))
                    pe.matmul(m.ps[:, S + half, :], m.ident_bf[:], m.masks[:, half, :], start=True, stop=True)
                    for i in range(HW):
                        win = half * HW + i
                        even, apart = win // 2, NT + win % 2
                        for h in range(2):
                            r = slice(DH * h, DH * h + DH)
                            mm = pe.matmul(m.ps[r, S + half, i * P:(i + 1) * P], qn[r, j % 2, win * WIN:(win + 1) * WIN],
                                           kn[r, j % 2, even:even + apart + 1:apart, :], start=False,
                                           stop=True, skip_group_check=True)
                    mm.then_inc(sim_done, 1)

            def turn(n, j, half):
                pe.wait_ge(normed, START + 2 * n + half + 1)
                if half == 0:
                    pe.wait_ge(pt_kept[1], START + n + 1)
                else:
                    pe.wait_ge(pt_kept[0], START + n + 1 + 1)
                for i in range(HW):
                    tr = pe.transpose(m.ps[:, PT, i * P:(i + 1) * P], probs[:, j % 2, half * HW + i, :], m.ident[:])
                tr.then_inc(pt_done, 1)

            def values(n, j, half):
                pe.wait_ge(pt_kept[half], START + n + 1 + 1)
                if half == 0:
                    pe.wait_ge(o_kept, START + n + 1)
                for i in range(HW):
                    win = half * HW + i
                    for h in range(2):
                        mm = pe.matmul(m.ps[DH * h:DH * h + DH, O, win * WIN:(win + 1) * WIN],
                                       (v_even, v)[win % 2][:, win // 2, j * P + DH * h:j * P + DH * h + DH],
                                       pts[:, half, i * P + DH * h:i * P + DH * h + DH], start=True, stop=True)
                mm.then_inc(pv_done, 1)

            def make_values(b, tiles):
                for t in tiles:
                    k = V_BANK[t]
                    kept = V_TILES[k].index(t)
                    if kept == 0:
                        pe.wait_ge((pt_kept[1], u_done)[k], START + (HP * b + 1, b)[k])
                    else:
                        pe.wait_ge(v_kept[k], START + len(V_TILES[k]) * b + kept)
                    mm3(pe, m.ps[:, (PT, O)[k], :], (hh[:, t * P:(t + 1) * P], hl[:, t * P:(t + 1) * P]),
                        (w.vh[:], w.vl[:])).then_inc(v_done, 1)

            def output(b):
                pe.wait_ge(o_kept, START + HP * (b + 1) + 1)
                for j in range(HP):
                    mm = pe.matmul(m.ps[:, O, :], w.wo[:, j, :], o[:, j, :], start=(j == 0), stop=(j == HP - 1))
                mm.then_inc(wo_done, 1)

            def unit(b, j, first=False):
                n = b * HP + j
                before = (j - 1) % HP
                if j == HP - 1:
                    pe.wait_ge(split, START + b + 2)
                project(n + 1, (j + 1) % HP, ORDER)
                sims(n, j)
                if j == 1:
                    for k in range(2):
                        pe.wait_ge(v_kept[k], START + len(V_TILES[k]) * (b + 1))
                    pe.wait_ge(v_copied, START + 32 * (b + 1))
                if not first:
                    turn(n - 1, before, 0)
                for i in range(2):
                    norms(n + 1, i)
                if not first:
                    turn(n - 1, before, 1)
                    for half in range(2):
                        values(n - 1, before, half)
                if j == 0:
                    make_values(b, V_ORDER[:1])
                    if not first:
                        output(b - 1)
                    make_values(b, V_ORDER[1:])

            pe.sem_inc(pt_done, 2)
            pe.wait_ge(split, START + 1)
            project(0, 0, ORDER)
            norms(0, 0)
            norms(0, 1)
            unit(0, 0, first=True)
            with pe.Fori(0, NB) as b:
                for j in range(1, HP):
                    unit(b, j)
                unit(b + 1, 0)

        @block.scalar
        def _(act):
            def square(n, i):
                act.wait_ge(projected, START + 4 * n + ORDER.index(2 * i) + 1)
                act.wait_ge(ss_done, START + 2 * n)
                act.activation(squares[:, i, :], m.ps[:, Q + 2 * i, :], ACT.Square).then_inc(squared, 1)

            def scale(n, i):
                act.wait_ge(ss_done, START + 2 * n + i + 1)
                act.wait_ge(qk_done, START + 2 * n)
                act.activation(rn[:, i, :], m.ps[:, Q + 2 * i, :], ACT.Ln, bias=m.tiny[:, 0:1],
                               scale=SS_SCALE).then_inc(ss_logged, 1)
                act.wait_ge(ss_logged, START + 2 * n + i + 1 + 2)
                act.activation(rn[:, i, :], rn[:, i, :], ACT.Exp, scale=-0.5,
                               bias=m.unscale[:, i:i + 1]).then_inc(rn_done, 1)

            def exps(n, j, half):
                for win in range(half * HW, (half + 1) * HW):
                    if win % HW == 0:
                        act.wait_ge(maxed, START + 2 * n + win // HW + 1)
                        act.wait_ge(pt_done, START + 2 * n)
                    act.activation(probs[:, j % 2, win, :], m.ps[:, S + win // HW, (win % HW) * P:(win % HW + 1) * P],
                                   ACT.Exp, bias=nmax[:, j % 2, win:win + 1],
                                   accum_out=psum_[:, j % 2, win:win + 1]).then_inc(exped, 1)

            def keep_turned(n):
                act.wait_ge(pt_done, START + 2 * n + 1 + 2)
                act.wait_ge(pv_done, START + 2 * n)
                act.activation(pts[:, 0, :], m.ps[:, PT, :], ACT.Copy).then_inc(pt_kept[0], 1)

            def unit(b, j, first=False):
                n = b * HP + j
                for i in range(2):
                    square(n + 1, i)
                if not first:
                    keep_turned(n - 1)
                exps(n, j, 0)
                for i in range(2):
                    scale(n + 1, i)
                exps(n, j, 1)
                if j == 0:
                    act.wait_ge(v_copied, START + 32 * b)
                    for t in V_TILES[0]:
                        act.wait_ge(v_done, START + NT * b + V_ORDER.index(t) + 1)
                        act.activation(v[:, t, :], m.ps[:, PT, :], ACT.Copy).then_inc(v_kept[0], 1)
                    act.wait_ge(v_kept[1], START + len(V_TILES[1]) * (b + 1))
                    act.wait_ge(v_kept[0], START + len(V_TILES[0]) * (b + 1))
                    act.dma_start(v_even[:P // 2, :, :], v[:P // 2, :, :]).then_inc(v_copied, 16)
                    act.dma_start(v_even[P // 2:, 1:, :], v[P // 2:, :NT - 1, :]).then_inc(v_copied, 16)

            act.preload_act_table_set(EXP_LN)
            act.sem_inc(ss_logged, 2)
            act.sem_inc(exped, NW)
            act.sem_inc(pt_kept[0], 1)
            for i in range(2):
                square(0, i)
            for i in range(2):
                scale(0, i)
            unit(0, 0, first=True)
            with act.Fori(0, NB) as b:
                for j in range(1, HP):
                    unit(b, j)
                unit(b + 1, 0)
            act.wait_ge(v_copied, START + 32 * (NB + 1))

        @block.vector
        def _(dve):
            def halves(b):
                dve.wait_ge(taken, START + 2 * (b + 1))
                dve.wait_ge(projected, START + 4 * HP * b)
                dve.wait_ge(v_done, START + NT * b)
                dve.tensor_copy(hh[:], hs[:]).then_inc(hi_done, 1)
                dve.wait_ge(hi_done, START + b + 1)
                dve.tensor_tensor(hl[:], hs[:], hh[:], ALU.subtract).then_inc(split, 1)

            def rotate(n):
                for k in ORDER:
                    dve.wait_ge(projected, START + 4 * n + ORDER.index(k) + 1)
                    if k % 2 == 0:
                        dve.wait_ge(squared, START + 2 * n + k // 2 + 1)
                    dve.wait_ge(added, START + 2 * n)
                    dve.tensor_tensor(turned[:, k, :], m.ps[:, Q + k, :], w.tables[:, k, :], ALU.mult).then_inc(rotated, 1)

            def maxima(n, j):
                for half in range(2):
                    dve.wait_ge(sim_done, START + 2 * n + half + 1)
                    dve.wait_ge(exped, START + NW * n + HW * (half + 1))
                    dve.tensor_reduce(nmax[:, j % 2, half * HW:(half + 1) * HW],
                                      m.ps[:, S + half, :].rearrange("p (w k) -> p w k", k=P), AX.X, ALU.max,
                                      negate=True).then_inc(maxed, 1)

            def scale_qk(n, j):
                dve.wait_ge(sim_done, START + 2 * n)
                dve.wait_ge(rn_done, START + 2 * n + 1)
                dve.wait_ge(added, START + 2 * n + 1)
                dve.scalar_tensor_tensor(out=qn[:, j % 2, :], in0=rn[:, 0, :], scalar=8e12, in1=sums[:, 0, :], op0=ALU.min,
                                         op1=ALU.mult).then_inc(qk_done, 1)
                dve.wait_ge(rn_done, START + 2 * n + 2)
                dve.wait_ge(added, START + 2 * n + 2)
                blocks = lambda t: t.rearrange("p (t k c) -> p t k c", k=2, c=WIN)
                for k in range(2):
                    half = dve.scalar_tensor_tensor(out=kn[:, j % 2, k * (NT + 1):k * (NT + 1) + NT, :],
                                                    in0=blocks(rn[:, 1, :])[:, :, k, :], scalar=1e12,
                                                    in1=blocks(sums[:, 1, :])[:, :, k, :], op0=ALU.min, op1=ALU.mult)
                half.then_inc(qk_done, 1)

            def reciprocals(n, j):
                dve.wait_ge(exped, START + NW * (n + 2))
                dve.wait_ge(normed, START + 2 * n)
                dve.reciprocal(rsum[:, j % 2, :], psum_[:, j % 2, :]).then_inc(recip, 1)

            def keep_turned(n):
                dve.wait_ge(pt_done, START + 2 * n + 2 + 2)
                dve.wait_ge(pv_done, START + 2 * n)
                dve.tensor_copy(pts[:, 1, :], m.ps[:, PT, :]).then_inc(pt_kept[1], 1)

            def keep_out(n, j, b):
                dve.wait_ge(pv_done, START + 2 * n + 2)
                dve.wait_ge(wo_done, START + b)
                dve.tensor_copy(o[:, j, :], m.ps[:, O, :]).then_inc(o_kept, 1)

            def unit(b, j, first=False):
                n = b * HP + j
                rotate(n + 1)
                maxima(n, j)
                if j == HP - 2:
                    halves(b + 1)
                if not first:
                    keep_turned(n - 1)
                    keep_out(n - 1, (j - 1) % HP, b if j else b - 1)
                scale_qk(n + 1, (j + 1) % HP)
                reciprocals(n, j)
                if j == 0:
                    if not first:
                        dve.wait_ge(wo_done, START + b)
                        dve.tensor_tensor(seq(m.u, b - 1), m.ps[:, O, :], seq(m.u, b - 1), ALU.add).then_inc(u_done, 1)
                    dve.wait_ge(v_copied, START + 32 * b)
                    for t in V_TILES[1]:
                        dve.wait_ge(v_done, START + NT * b + V_ORDER.index(t) + 1)
                        dve.tensor_copy(v[:, t, :], m.ps[:, O, :]).then_inc(v_kept[1], 1)

            dve.sem_inc(rotated, 4)
            dve.sem_inc(pt_kept[1], 1)
            dve.sem_inc(o_kept, 1)
            dve.memset(v_even[P // 2:, 0, :], 0.0).then_inc(zeroed, 1)
            for k in range(2):
                dve.memset(kn[:, k, NT, :], 0.0).then_inc(zeroed, 1)
            halves(0)
            rotate(0)
            scale_qk(0, 0)
            unit(0, 0, first=True)
            with dve.Fori(0, NB) as b:
                for j in range(1, HP):
                    unit(b, j)
                unit(b + 1, 0)

        @block.gpsimd
        def _(pool):
            def take(b):
                pool.wait_ge(split, START + b)
                pool.tensor_copy(hs[:P // 2, :], m.u[:P // 2, bass.ds(b * T, T)]).then_inc(taken, 1)
                pool.tensor_copy(hs[P // 2:, 1:], m.u[P // 2:, bass.ds(b * T, T - 1)]).then_inc(taken, 1)
                pool.wait_ge(taken, START + 2 * b + 2)

            def add(n):
                for i in range(2):
                    pool.wait_ge(rotated, START + 4 * n + 2 * i + 2 + 4)
                    pool.wait_ge(qk_done, START + 2 * n)
                    pool.tensor_tensor(sums[:, i, :], turned[:, 2 * i, :], turned[:, 2 * i + 1, :], ALU.add).then_inc(added, 1)

            def norm(n, j):
                pool.wait_ge(recip, START + n + 1)
                for half in range(2):
                    ws = slice(half * HW, (half + 1) * HW)
                    pool.tensor_tensor(probs[:, j % 2, ws, :], probs[:, j % 2, ws, :],
                                       rsum[:, j % 2, ws].unsqueeze(2).to_broadcast([P, HW, P]),
                                       ALU.mult).then_inc(normed, 1)

            pool.memset(hs[P // 2:, 0:1], 0.0).then_inc(zeroed2, 1)
            pool.wait_ge(zeroed2, START + 1)
            take(0)
            add(0)
            pool.wait_ge(added, START + 2)
            add(1)
            norm(0, 0)
            with pool.Fori(0, NB) as b:
                pool.wait_ge(normed, START + 2 * (HP * b + 1))
                take(b + 1)
                for j in range(1, HP + 1):
                    n = b * HP + j
                    add(n + 1)
                    norm(n, j % HP)


def gated_phase(nc, m, app, l, w, last):
    A, G, Y = [2, 3, 2], [4, 5, 4], 6
    with Phase(nc) as c:
        name = f"ff{app}{l}"
        sb = lambda n, s, d=F32: c.enter_context(nc.sbuf_tensor(f"{name}_{n}", s, d))
        sem = lambda n: c.sem(f"{name}_{n}")
        ln = Norm(nc, c, m, name + "_ln", 0, 1, shift=True)
        xh, xl = sb("xh", [P, T], F32R), sb("xl", [P, T], F32R)
        gate, prod = sb("gate", [P, MC, T]), sb("prod", [P, MC, T])
        hi_done, split, up_done, gelued, gated = sem("hi_done"), sem("split"), sem("up_done"), sem("gelued"), sem("gated")
        down_done, u_done, x_done = sem("down_done"), sem("u_done"), sem("x_done")
        block = c.block()
        width = [MW, MW, HID - 2 * MW]

        @block.gpsimd
        def _(pool):
            ln.start(pool)
            ln.take(pool, 0, m.u, 0)
            ln.take(pool, 1, m.u, 1)
            with pool.Fori(0, NB) as b:
                ln.take(pool, b + 2, m.u, b + 2)

        @block.tensor
        def _(pe):
            def up(b, i):
                pe.wait_ge(gated, START + MC * b + (i == 2))
                for k, bank in ((1, G[i]), (0, A[i])):
                    cols = slice(k * HID + i * MW, k * HID + i * MW + width[i])
                    mm3(pe, m.ps[:width[i], bank, :], (w.w1h[:, cols], w.w1l[:, cols]), (xh[:], xl[:])).then_inc(up_done, 1)

            def down(b, i):
                pe.wait_ge(gated, START + MC * b + i + 1)
                if i == 0:
                    pe.wait_ge(u_done, START + b)
                pe.matmul(m.ps[:, Y, :], w.w2[:width[i], i, :], prod[:width[i], i, :], start=(i == 0),
                          stop=(i == MC - 1)).then_inc(down_done, 1)

            ln.centre(pe, 0)
            ln.variance(pe, 0)
            ln.centre(pe, 1)
            with pe.Fori(0, NB) as b:
                pe.wait_ge(split, START + b + 1)
                up(b, 0)
                up(b, 1)
                ln.variance(pe, b + 1)
                up(b, 2)
                for i in range(MC):
                    down(b, i)
                ln.centre(pe, b + 2)

        @block.scalar
        def _(act):
            def gelu(b, i):
                act.wait_ge(up_done, START + 2 * (MC * b + i) + 1)
                act.wait_ge(gated, START + MC * b)
                act.activation(gate[:width[i], i, :], m.ps[:width[i], G[i], :], ACT.Gelu,
                               bias=w.bias[:width[i], MC + i:MC + i + 1]).then_inc(gelued, 1)

            ln.square(act, 0)
            ln.scale(act, 0)
            with act.Fori(0, NB) as b:
                for i in range(MC):
                    gelu(b, i)
                    if i == 0:
                        ln.square(act, b + 1)
                ln.scale(act, b + 1)

        @block.vector
        def _(dve):
            def halves(n):
                dve.wait_ge(up_done, START + 2 * MC * n)
                dve.wait_ge(ln.normed, START + n + 1)
                dve.tensor_copy(xh[:], ln.out[:]).then_inc(hi_done, 1)
                dve.wait_ge(hi_done, START + n + 1)
                dve.tensor_tensor(xl[:], ln.out[:], xh[:], ALU.subtract).then_inc(split, 1)

            ln.norm(dve, 0)
            halves(0)
            with dve.Fori(0, NB) as b:
                for i in range(MC):
                    dve.wait_ge(up_done, START + 2 * (MC * b + i) + 2)
                    dve.wait_ge(gelued, START + MC * b + i + 1)
                    dve.wait_ge(down_done, START + MC * b)
                    dve.scalar_tensor_tensor(out=prod[:width[i], i, :], in0=m.ps[:width[i], A[i], :],
                                             scalar=w.bias[:width[i], i:i + 1], in1=gate[:width[i], i, :],
                                             op0=ALU.add, op1=ALU.mult).then_inc(gated, 1)
                ln.norm(dve, b + 1)
                halves(b + 1)
                dve.wait_ge(down_done, START + MC * (b + 1))
                dve.scalar_tensor_tensor(out=seq(m.u, b), in0=m.ps[:, Y, :], scalar=w.b2[:, 0:1], in1=seq(m.u, b),
                                         op0=ALU.add, op1=ALU.add).then_inc(u_done, 1)
                if last:
                    dve.wait_ge(u_done, START + b + 1)
                    dve.scalar_tensor_tensor(out=seq(m.x, b), in0=seq(m.u, b), scalar=0.5, in1=seq(m.x, b),
                                             op0=ALU.mult, op1=ALU.add).then_inc(x_done, 1)


def global_phase(nc, m, ins):
    with Phase(nc) as c:
        sb = lambda n, s, d=F32: c.enter_context(nc.sbuf_tensor(f"glob_{n}", s, d))
        sem = lambda n: c.sem(f"glob_{n}")
        ln = Norm(nc, c, m, "glob_ln", 0, 1)
        raw = sb("raw", [P, 3, P])
        wh, wl = sb("wh", [P, 3, P], F32R), sb("wl", [P, 3, P], F32R)
        xh, xl = sb("xh", [P, T], F32R), sb("xl", [P, T], F32R)
        ones = sb("ones", [P, P])
        squares, rn, v = sb("squares", [P, 2, T]), sb("rn", [P, 2, T]), sb("v", [P, T])
        kn, kv, qn, feat = sb("kn", [P, T]), sb("kv", [P, T]), sb("qn", [P, T]), sb("feat", [P, 1])
        w_in, steps, hi_done, split, projected = sem("w_in"), sem("steps"), sem("hi_done"), sem("split"), sem("projected")
        squared, v_kept, ss_done, ss_logged, rn_done = sem("squared"), sem("v_kept"), sem("ss_done"), sem("ss_logged"), sem("rn_done")
        k_scaled, q_scaled, feated, x_done = sem("k_scaled"), sem("q_scaled"), sem("feated"), sem("x_done")
        block = c.block()
        Q, K, V, SS = 2, 3, 4, 5

        @block.sync
        def _(sp):
            sp.dma_start(raw[:], ins["qkv_global"]).then_inc(w_in, 16)

        @block.gpsimd
        def _(pool):
            ln.take(pool, 0, m.x, 0)
            ln.take(pool, 1, m.x, 1)
            with pool.Fori(0, NB) as b:
                ln.take(pool, b + 2, m.x, b + 2)

        @block.tensor
        def _(pe):
            ln.centre(pe, 0)
            ln.variance(pe, 0)
            ln.centre(pe, 1)
            with pe.Fori(0, NB) as b:
                pe.wait_ge(split, START + b + 1)
                for k in (1, 0, 2):
                    if k == Q - 2:
                        pe.wait_ge(q_scaled, START + b)
                    if k == K - 2:
                        pe.wait_ge(k_scaled, START + b)
                    if k == V - 2:
                        pe.wait_ge(v_kept, START + b)
                    mm3(pe, m.ps[:, Q + k, :], (wh[:, k, :], wl[:, k, :]), (xh[:], xl[:])).then_inc(projected, 1)
                ln.variance(pe, b + 1)
                for i in (1, 0):
                    pe.wait_ge(squared, START + 2 * b + 2 - i)
                    pe.wait_ge(ss_logged, START + 2 * b)
                    pe.matmul(m.ps[:, SS + i, :], ones[:], squares[:, i, :], start=True, stop=True).then_inc(ss_done, 1)
                ln.centre(pe, b + 2)

        @block.scalar
        def _(act):
            act.preload_act_table_set(EXP_LN)
            ln.square(act, 0)
            ln.scale(act, 0)
            ln.square(act, 1)
            with act.Fori(0, NB) as b:
                for i in (1, 0):
                    act.wait_ge(projected, START + 3 * b + 2 - i)
                    act.wait_ge(ss_done, START + 2 * b)
                    act.activation(squares[:, i, :], m.ps[:, Q + i, :], ACT.Square).then_inc(squared, 1)
                act.wait_ge(projected, START + 3 * b + 3)
                act.wait_ge(feated, START + b)
                act.activation(v[:], m.ps[:, V, :], ACT.Copy).then_inc(v_kept, 1)
                for i in (1, 0):
                    act.wait_ge(ss_done, START + 2 * b + 2 - i)
                    act.wait_ge(k_scaled, START + b)
                    act.wait_ge(q_scaled, START + b)
                    act.activation(rn[:, i, :], m.ps[:, SS + i, :], ACT.Ln, bias=m.tiny[:, 0:1],
                                   scale=SS_SCALE).then_inc(ss_logged, 1)
                    act.wait_ge(ss_logged, START + 2 * b + 2 - i)
                    act.activation(rn[:, i, :], rn[:, i, :], ACT.Exp, scale=-0.5,
                                   bias=m.unscale[:, 1:2]).then_inc(rn_done, 1)
                    if i == 1:
                        ln.scale(act, b + 1)
                ln.square(act, b + 2)

        @block.vector
        def _(dve):
            def halves(n):
                dve.wait_ge(projected, START + 3 * n)
                dve.wait_ge(ln.normed, START + n + 1)
                dve.tensor_copy(xh[:], ln.out[:]).then_inc(hi_done, 1)
                dve.wait_ge(hi_done, START + n + 1)
                dve.tensor_tensor(xl[:], ln.out[:], xh[:], ALU.subtract).then_inc(split, 1)

            dve.memset(ones[:], 1.0)
            dve.wait_ge(w_in, START + 16)
            split_weights(dve, [(raw[:], wh[:], wl[:])], steps, START)
            ln.norm(dve, 0)
            halves(0)
            with dve.Fori(0, NB) as b:
                dve.wait_ge(rn_done, START + 2 * b + 1)
                dve.scalar_tensor_tensor(out=kn[:], in0=rn[:, 1, :], scalar=1e12, in1=m.ps[:, K, :], op0=ALU.min,
                                         op1=ALU.mult).then_inc(k_scaled, 1)
                dve.wait_ge(v_kept, START + b + 1)
                dve.wait_ge(k_scaled, START + b + 1)
                dve.tensor_tensor_reduce(out=kv[:], in0=kn[:], in1=v[:], scale=1.0 / T, scalar=0.0, op0=ALU.mult,
                                         op1=ALU.add, accum_out=feat[:]).then_inc(feated, 1)
                ln.norm(dve, b + 1)
                halves(b + 1)
                dve.wait_ge(x_done, START + b)
                dve.wait_ge(rn_done, START + 2 * b + 2)
                dve.scalar_tensor_tensor(out=qn[:], in0=rn[:, 0, :], scalar=1e12, in1=m.ps[:, Q, :], op0=ALU.min,
                                         op1=ALU.mult).then_inc(q_scaled, 1)
                dve.wait_ge(feated, START + b + 1)
                dve.wait_ge(q_scaled, START + b + 1)
                dve.scalar_tensor_tensor(out=seq(m.x, b), in0=qn[:], scalar=feat[:, 0:1], in1=seq(m.x, b),
                                         op0=ALU.mult, op1=ALU.add).then_inc(x_done, 1)


IDENT = np.eye(P, dtype=np.float32)


def constants():
    k = {"ident": IDENT, "center": IDENT - np.float32(1.0 / P)}
    e = np.arange(NE)
    k["before"] = np.tile((e[None, :] < e[:, None]).astype(np.float32), (P, 1, 1))
    r = np.arange(P)
    sp = np.zeros((P, NS, P), np.float32)
    sh = np.zeros((P, NB, P), np.float32)
    for p in range(NS):
        for q in r:
            sp[(q // NS) * NS + p, p, q] = 1.0
    for b in range(NB):
        for q in r:
            sh[b * NH + q // NS, b, q] = 1.0
    k["spread_p"], k["spread_h"] = sp, sh
    k["gather_p"] = np.ascontiguousarray(sp.transpose(2, 1, 0))
    cm = np.ones((P, T), np.float32)
    cm[:, ::CHUNK] = 0.0
    k["chunk_mask"] = cm
    k["per_head"] = np.kron(np.eye(2), np.ones((DH, DH))).astype(np.float32)
    q, key = np.arange(WIN)[:, None], np.arange(2 * WIN)[None, :]
    seen = (key <= q + WIN) & (key >= q)
    later = np.where(seen, 0.0, MASKED)
    first = np.where(seen & (key >= WIN), 0.0, MASKED)
    own_first = lambda z: np.roll(z, WIN, axis=1)
    rows = np.stack([np.concatenate([own_first(w0), later, own_first(later), later], 1) for w0 in (first, later)], 1)
    k["masks"] = np.tile(rows, (2, 1, 1)).astype(np.float32)
    f32 = np.float32
    half = np.arange(0, DH, 2, dtype=f32)
    inv = (1.0 / (f32(10000.0) ** (half / f32(DH)))).astype(f32)
    t = np.arange(T, dtype=f32)
    freqs = (t[:, None] * inv[None, :]).astype(f32)
    base = (half + f32(0.4 * DH)) / f32(1.4 * DH)
    power = (t - T // 2) / f32(WIN // 2)
    scale = (base[None, :] ** power[:, None]).astype(f32)
    cos, sin = np.cos(freqs), np.sin(freqs)
    tab = []
    for sc in (scale, 1.0 / scale):
        cc, ss = (cos * sc).T, (sin * sc).T
        tab += [np.concatenate([cc, cc] * 2), np.concatenate([-ss, ss] * 2)]
    k["rotary"] = np.ascontiguousarray(np.stack(tab, 1).astype(f32))
    return k


def build(nc, ins, out, upto="s6"):
    with ExitStack() as c:
        m = Mem()
        sb = lambda n, s, d=F32: c.enter_context(nc.sbuf_tensor(n, s, d))
        m.x = sb("x", [P, (NB + 2) * T])
        m.ident, m.center, m.mean_of = sb("ident", [P, P]), sb("center", [P, P]), sb("mean_of", [P, P])
        m.eps, m.before = sb("eps", [P, 1]), sb("before", [P, NE, NE])
        m.ps = c.enter_context(nc.psum_tensor("banks", [P, 8, T], F32))
        cw_dram = nc.dram_tensor("cw_dram", [NE, T], F32)
        load_phase(nc, m, ins["L0_attn_x"], ins)
        with ExitStack() as moe:
            w = moe_weights(nc, moe, m, ins)
            moe_phase(nc, m, 0, w, cw_dram.ap())
            if upto >= "s2":
                ssm_phase(nc, m, ins)
            if upto >= "s3":
                moe_phase(nc, m, 1, w, cw_dram.ap())
        with ExitStack() as gated:
            if upto >= "s4":
                m.u = gated.enter_context(nc.sbuf_tensor("u", [P, (NB + 2) * T], F32))
                extras_phase(nc, gated, m, ins)
                ws = gated_weights(nc, gated, m, ins)
            for app in range(2):
                if upto >= ("s4", "s6")[app]:
                    entry_phase(nc, m, app)
                    for l in range(2):
                        attention_phase(nc, m, app, l, ws[l])
                        gated_phase(nc, m, app, l, ws[l], last=(l == 1))
                if app == 0 and upto >= "s5":
                    global_phase(nc, m, ins)
        store_phase(nc, m, out)


def arrays(inp):
    import numpy as np
    a = {n: np.ascontiguousarray(np.asarray(v)) for n, v in inp.items()}
    t = np.ascontiguousarray
    a.update(constants())
    a["gate_t"] = t(a["L0_ffn_w_gate"].T)
    a["b1_t"] = t(a["L0_ffn_b1"].reshape(NE * HC, P).T)
    a["b2_t"] = t(a["L0_ffn_b2"].T)
    w_in = a["L0_attn_W_in"]
    a["ssm_w_in"] = t(w_in[:3 * P].T)
    a["ssm_w_dt"] = t(w_in[3 * P:].T)
    a["ssm_w_dtx"] = t(np.repeat(w_in[3 * P:], NS, axis=0).T)
    a["ssm_w_out"] = t(a["L0_attn_W_out"].T)
    a["ssm_conv_w"] = t(a["L0_attn_conv_w"].reshape(3, P, 4).transpose(1, 0, 2))
    a["ssm_conv_b"] = t(a["L0_attn_conv_b"].reshape(3, P).T)
    a["ssm_a"] = t(np.stack([np.tile(a["L0_attn_A_param"], NB), np.repeat(a["L0_attn_A_param"], NS)], 1))
    a["ssm_dt_b"] = t(np.stack([np.tile(a["L0_attn_dt_bias"], NB), np.repeat(a["L0_attn_dt_bias"], NS)], 1))
    a["b2_gated"] = t(a["L1_ffn_b2"][:, :, None])
    other = np.roll(np.arange(DH), DH // 2)
    qs, ks = a["L1_ffn_q_scale"], a["L1_ffn_k_scale"]
    a["qk_scales"] = t(np.stack([np.tile(z, (1, 2)) for z in (qs, qs[:, other], ks, ks[:, other])], 2).transpose(1, 0, 2))
    a["ln_w"] = t(np.stack([a["L1_ffn_ln_g"], a["L1_ffn_ln_b"]], 2).transpose(1, 0, 2))
    b1 = np.zeros((P, 2, 2 * MC), np.float32)
    for i in range(2 * MC):
        n = min(MW, HID - (i % MC) * MW)
        lo = (i // MC) * HID + (i % MC) * MW
        b1[:n, :, i] = a["L1_ffn_b1"][:, lo:lo + n].T
    a["b1_gated"] = b1
    a["qkv_global"] = t(np.stack([a[f"L1_attn_W_{n}"].T for n in "qkv"], 1))
    return a


USED = ["L0_attn_x", "L0_ffn_W1", "L0_ffn_W2", "gate_t", "b1_t", "b2_t", "before", "ident", "center",
        "ssm_w_in", "ssm_w_dt", "ssm_w_dtx", "ssm_w_out", "ssm_conv_w", "ssm_conv_b", "ssm_a", "ssm_dt_b",
        "spread_p", "gather_p", "spread_h", "chunk_mask", "per_head", "masks", "rotary", "b2_gated", "qk_scales", "ln_w", "b1_gated", "qkv_global",
        "L1_ffn_wqkv", "L1_ffn_wo", "L1_ffn_w1", "L1_ffn_w2"]


def kernel(**inputs):
    import numpy as np
    import concourse.bacc as bacc
    from concourse.bass_utils import run_bass_kernel_spmd

    nc = bacc.Bacc("TRN2", target_bir_lowering=False, num_devices=1)
    a = arrays(inputs)
    fed = {f"in_{n}": a[n] for n in USED}
    ins = {n: nc.dram_tensor(f"in_{n}", a[n].shape, mybir.dt.from_np(a[n].dtype), kind="ExternalInput").ap() for n in USED}
    out = nc.dram_tensor("out_0", (NB, T, P), F32, kind="ExternalOutput").ap()
    build(nc, ins, out)
    r = run_bass_kernel_spmd(nc, [fed], core_ids=[0])
    return r.results[0]["out_0"]
```

```python
import math
from contextlib import ExitStack

import numpy as np
import concourse.bass as bass
from concourse import mybir

F32 = mybir.dt.float32
F32R = mybir.dt.float32r
BF16 = mybir.dt.bfloat16
ALU = mybir.AluOpType
ACT = mybir.ActivationFunctionType
AX = mybir.AxisListType

P = 128
NB = 8
T = 512
TT = T // P
NE = 8
HC = 4
NH = 16
NS = 8
CHUNK = 64
WIN = 64
NW = T // WIN
HP = 4
DH = 64
HID = 341
MC = 3
MW = 114
LN_EPS = 1e-5
MASKED = -1e30
SS_SCALE = 65536.0


def mm3(pe, out, w, x, start=True, stop=True):
    (wh, wl), (xh, xl) = w, x
    pe.matmul(out, wh, xh, start=start, stop=False)
    pe.matmul(out, wl, xh, start=False, stop=False)
    return pe.matmul(out, wh, xl, start=False, stop=stop)


START = 1


class Phase(ExitStack):

    def __init__(self, nc):
        super().__init__()
        self.nc, self.sems = nc, []
        self.callback(self.clear)

    def sem(self, name):
        self.sems.append(self.nc.alloc_semaphore(name=name))
        return self.sems[-1]

    def block(self):
        engines = (self.nc.tensor, self.nc.scalar, self.nc.vector, self.nc.gpsimd)
        for i, s in enumerate(self.sems):
            engines[i % len(engines)].sem_inc(s, START)
        self.nc.all_engine_barrier()
        return self.enter_context(self.nc.Block())

    def clear(self):
        if self.sems:
            self.nc.clear_and_free_semaphores(self.sems)
            self.nc.all_engine_barrier()


class Mem:
    pass


def seq(t, b):
    return t[:, bass.ds(b * T, T)]


def split_weights(dve, pairs, sem, count):
    for raw, hi, lo in pairs:
        dve.tensor_copy(hi, raw).then_inc(sem, 1)
        count += 1
        dve.wait_ge(sem, count)
        dve.tensor_tensor(lo, raw, hi, ALU.subtract).then_inc(sem, 1)
        count += 1
    return count


def load_phase(nc, m, w, x_in, consts):
    with Phase(nc) as c:
        PART = 2
        raw1 = c.enter_context(nc.sbuf_tensor("raw_w1", [P, NE, T], F32))
        raw2 = c.enter_context(nc.sbuf_tensor("raw_w2", [P, NE, HC, P], F32))
        parts = [slice(e, e + PART) for e in range(0, NE, PART)]
        w1_in = [c.sem(f"w1_in{i}") for i in range(len(parts))]
        w2_in = [c.sem(f"w2_in{i}") for i in range(len(parts))]
        rest_in, steps = c.sem("moe_rest_in"), c.sem("moe_split_steps")
        xin = c.enter_context(nc.sbuf_tensor("x_tokens", [P, NB * TT, P], F32))
        consts_in = c.sem("consts_in")
        x_tokens_in = c.sem("x_tokens_in")
        turned = c.sem("x_turned")
        stored = c.sem("x_stored")
        made = c.sem("load_made")
        block = c.enter_context(nc.Block())

        @block.sync
        def _(sp):
            sp.dma_start(m.ident[:], consts["ident"]).then_inc(consts_in, 16)
            sp.dma_start(xin[:], x_in.rearrange("b (t p) d -> p (b t) d", p=P)).then_inc(x_tokens_in, 16)
            sp.dma_start(m.center[:], consts["center"]).then_inc(consts_in, 16)
            sp.dma_start(w.gate[:], consts["gate_t"]).then_inc(rest_in, 16)
            sp.dma_start(w.b1[:], consts["b1_t"]).then_inc(rest_in, 16)
            sp.dma_start(w.b2[:], consts["b2_t"]).then_inc(rest_in, 16)
            sp.dma_start(m.before[:], consts["before"]).then_inc(rest_in, 16)
            sp.wait_ge(consts_in, 32)
            sp.wait_ge(rest_in, 64)

        @block.gpsimd
        def _(pool):
            for i, e in enumerate(parts):
                pool.dma_start(raw1[:, e, :], consts["L0_ffn_W1"][e].rearrange("e d h -> d e h")).then_inc(w1_in[i], 16)
                for k in range(e.start, e.stop):
                    pool.dma_start(raw2[:, k, :, :], consts["L0_ffn_W2"][k].rearrange("(k p) d -> p k d", p=P)).then_inc(w2_in[i], 16)

        @block.vector
        def _(dve):
            dve.memset(m.x[:, NB * T:], 0.0)
            dve.memset(m.mean_of[:], 1.0 / P)
            dve.memset(m.eps[:], LN_EPS)
            n = 0
            for i, e in enumerate(parts):
                dve.wait_ge(w1_in[i], 16)
                n = split_weights(dve, [(raw1[:, e], w.w1h[:, e], w.w1l[:, e])], steps, n)
                dve.wait_ge(w2_in[i], 16 * PART)
                n = split_weights(dve, [(raw2[:, e], w.w2h[:, e], w.w2l[:, e])], steps, n)

        @block.tensor
        def _(pe):
            pe.wait_ge(consts_in, 32)
            pe.wait_ge(x_tokens_in, 16)
            for b in range(NB):
                if b >= 2:
                    pe.wait_ge(stored, b - 1)
                for t in range(TT):
                    tr = pe.transpose(m.ps[:, b % 2, t * P:(t + 1) * P], xin[:, b * TT + t, :], m.ident[:])
                tr.then_inc(turned, 1)

        @block.scalar
        def _(act):
            for b in range(NB):
                act.wait_ge(turned, b + 1)
                act.activation(m.x[:, b * T:(b + 1) * T], m.ps[:, b % 2, :], ACT.Copy).then_inc(stored, 1)


def store_phase(nc, m, out):
    with Phase(nc) as c:
        xout = c.enter_context(nc.sbuf_tensor("out_tokens", [P, NB * TT, P], F32))
        turned = c.sem("out_turned")
        ready = c.sem("out_ready")
        written = c.sem("out_written")
        block = c.enter_context(nc.Block())
        dst = out.rearrange("b (t p) d -> p (b t) d", p=P)

        @block.tensor
        def _(pe):
            for b in range(NB):
                if b >= 2:
                    pe.wait_ge(ready, b - 1)
                for t in range(TT):
                    col = b * T + t * P
                    tr = pe.transpose(m.ps[:, b % 2, t * P:(t + 1) * P], m.x[:, col:col + P], m.ident[:])
                tr.then_inc(turned, 1)

        @block.scalar
        def _(act):
            for b in range(NB):
                act.wait_ge(turned, b + 1)
                act.activation(xout[:, b * TT:(b + 1) * TT, :].rearrange("p t d -> p (t d)"),
                               m.ps[:, b % 2, :], ACT.Copy).then_inc(ready, 1)

        @block.sync
        def _(sp):
            for b in range(NB):
                sp.wait_ge(ready, b + 1)
                sp.dma_start(dst[:, b * TT:(b + 1) * TT, :], xout[:, b * TT:(b + 1) * TT, :]).then_inc(written, 16)
            sp.wait_ge(written, 16 * NB)


class Norm:

    def __init__(self, nc, c, m, name, cb, vb, shift=False, switch=False):
        self.m, self.cb, self.vb, self.shift, self.switch = m, cb, vb, shift, switch
        sb = lambda n: c.enter_context(nc.sbuf_tensor(f"{name}_{n}", [P, T], F32))
        self.xs, self.sq, self.rstd, self.out = sb("xs"), sb("sq"), sb("rstd"), sb("xn")
        sem = lambda n: c.sem(f"{name}_{n}")
        self.taken, self.centred, self.squared = sem("taken"), sem("centred"), sem("squared")
        self.varied, self.logged, self.scaled, self.normed = sem("varied"), sem("logged"), sem("scaled"), sem("normed")
        self.zeroed = sem("zeroed")

    def start(self, eng):
        if self.shift:
            eng.memset(self.xs[P // 2:, 0:1], 0.0).then_inc(self.zeroed, 1)
            eng.wait_ge(self.zeroed, START + 1)

    def take(self, eng, n, src, b, after=None):
        eng.wait_ge(self.centred, START + n)
        if self.shift:
            eng.tensor_copy(self.xs[:P // 2, :], src[:P // 2, bass.ds(b * T, T)]).then_inc(self.taken, 1)
            eng.tensor_copy(self.xs[P // 2:, 1:], src[P // 2:, bass.ds(b * T, T - 1)]).then_inc(self.taken, 1)
        else:
            eng.tensor_copy(self.xs[:], seq(src, b)).then_inc(self.taken, 1)

    def centre(self, pe, n, src=None):
        if src is None:
            pe.wait_ge(self.taken, START + (n + 1) * (1 + self.shift))
        pe.wait_ge(self.normed, START + n)
        pe.matmul(self.m.ps[:, self.cb, :], self.m.center[:], self.xs[:] if src is None else src, start=True,
                  stop=True).then_inc(self.centred, 1)

    def square(self, act, n):
        act.wait_ge(self.centred, START + n + 1)
        act.wait_ge(self.varied, START + n)
        act.activation(self.sq[:], self.m.ps[:, self.cb, :], ACT.Square).then_inc(self.squared, 1)

    def variance(self, pe, n):
        pe.wait_ge(self.squared, START + n + 1)
        pe.wait_ge(self.logged, START + n)
        pe.matmul(self.m.ps[:, self.vb, :], self.m.mean_of[:], self.sq[:], start=True, stop=True).then_inc(self.varied, 1)

    def scale(self, act, n):
        if self.switch:
            act.preload_act_table_set(EXP_LN)
        act.wait_ge(self.varied, START + n + 1)
        act.wait_ge(self.normed, START + n)
        act.activation(self.rstd[:], self.m.ps[:, self.vb, :], ACT.Ln, bias=self.m.eps[:, 0:1]).then_inc(self.logged, 1)
        act.wait_ge(self.logged, START + n + 1)
        act.activation(self.rstd[:], self.rstd[:], ACT.Exp, scale=-0.5).then_inc(self.scaled, 1)

    def norm(self, dve, n, out=None):
        dve.wait_ge(self.scaled, START + n + 1)
        dve.tensor_tensor(self.out[:] if out is None else out, self.m.ps[:, self.cb, :], self.rstd[:],
                          ALU.mult).then_inc(self.normed, 1)


def moe_phase(nc, m, app, w, cw_dram):
    NC = NE * HC
    UP = [1, 2, 3, 4]
    YB = [5, 6]
    GB = 7
    SLOTS = 4
    TAKE = 6
    LOOK = 3
    AT_CENTRE, AT_SCALE, AT_NORM, AT_LOGITS, AT_PEAK, AT_WEIGHTS, AT_TURN, AT_KEEP = 5, 6, 9, 13, 13, 20, 26, 26
    by_dve = lambda i: i % 2 == 0
    ROUNDED = [sum(by_dve(j) == k for j in range(NC)) for k in (False, True)]
    nth = lambda i: sum(by_dve(j) == by_dve(i) for j in range(i))
    with Phase(nc) as c:
        name = f"moe{app}"
        sb = lambda n, s, d=F32: c.enter_context(nc.sbuf_tensor(f"{name}_{n}", s, d))
        sem = lambda n: c.sem(f"{name}_{n}")
        ln = Norm(nc, c, m, name + "_ln", 0, GB, switch=True)
        xh, xl = sb("xh", [P, T], F32R), sb("xl", [P, T], F32R)
        g32 = sb("g32", [P, SLOTS, T])
        gh, gl = sb("gh", [P, SLOTS, T], F32R), sb("gl", [P, SLOTS, T], F32R)
        cwb = sb("cwb", [P, NE, T])
        part, acc = sb("part", [P, 2, T]), sb("acc", [P, T])
        peak, total, rtotal = sb("peak", [P, TT]), sb("total", [P, TT]), sb("rtotal", [P, TT])
        gate = sb("gate", [P, TT, NE])
        more, ties = sb("more", [P, TT, NE, NE]), sb("ties", [P, TT, NE, NE])
        rank, cw = sb("rank", [P, TT, NE]), sb("cw", [P, TT, NE])
        cwt = sb("cwt", [NE, T])
        split, up_done, gelu_done, rounded, lo_done = sem("split"), sem("up_done"), sem("gelu_done"), sem("rounded"), sem("lo_done")
        copied = sem("copied")
        down_done, part_done, summed, x_done = sem("down_done"), sem("part_done"), sem("summed"), sem("x_done")
        logits_done, peeled, exped, gated, turned = sem("logits"), sem("peeled"), sem("exped"), sem("gated"), sem("turned")
        cwt_done, cw_out, gchain, xh_done = sem("cwt_done"), sem("cw_out"), sem("gchain"), sem("xh_done")
        wchain = sem("wchain")
        cw_in = [sem(f"cw_in{e}") for e in range(NE)]
        GSTEPS = 8
        block = c.block()

        @block.tensor
        def _(pe):
            def logits(n):
                pe.wait_ge(ln.normed, START + n + 1)
                pe.wait_ge(cwt_done, START + n)
                for t in range(TT):
                    mm = pe.matmul(m.ps[:, GB, t * NE:(t + 1) * NE], ln.out[:, t * P:(t + 1) * P], w.gate[:],
                                   start=True, stop=True)
                mm.then_inc(logits_done, 1)

            def turn(n):
                pe.wait_ge(gated, START + n + 1)
                for t in range(TT):
                    tr = pe.transpose(m.ps[:NE, GB, t * P:(t + 1) * P], cw[:, t, :], m.ident[:])
                tr.then_inc(turned, 1)

            def up(b, i):
                if i >= len(UP):
                    j = i - len(UP)
                    if by_dve(j):
                        pe.wait_ge(gelu_done, START + b * NC + j + 1)
                    else:
                        pe.wait_ge(rounded, START + b * ROUNDED[0] + nth(j) + 1)
                cols = slice((i % HC) * P, (i % HC + 1) * P)
                mm3(pe, m.ps[:, UP[i % len(UP)], :], (w.w1h[:, i // HC, cols], w.w1l[:, i // HC, cols]),
                    (xh[:], xl[:])).then_inc(up_done, 1)

            def down(b, i):
                e, k = i // HC, i % HC
                pe.wait_ge(lo_done, START + b * NC + i + 1 + SLOTS)
                if k == 0:
                    pe.wait_ge(part_done, START + b * NE + e + 1)
                s = i % SLOTS
                mm3(pe, m.ps[:, YB[e % 2], :], (w.w2h[:, e, k, :], w.w2l[:, e, k, :]), (gh[:, s, :], gl[:, s, :]),
                    start=(k == 0), stop=(k == HC - 1)).then_inc(down_done, 1)

            ln.centre(pe, 0)
            ln.variance(pe, 0)
            logits(0)
            turn(0)
            with pe.Fori(0, NB) as b:
                pe.wait_ge(split, START + b + 1)
                for i in range(NC + LOOK):
                    if i < NC:
                        up(b, i)
                    if i >= LOOK:
                        down(b, i - LOOK)
                    if i == AT_CENTRE:
                        ln.centre(pe, b + 1)
                    if i == AT_SCALE:
                        pe.wait_ge(cwt_done, START + b + 1)
                        ln.variance(pe, b + 1)
                    if i == AT_LOGITS:
                        logits(b + 1)
                    if i == AT_TURN:
                        turn(b + 1)

        @block.scalar
        def _(act):
            def exps(n):
                act.wait_ge(peeled, START + n + 1)
                act.wait_ge(gated, START + n)
                act.activation(gate[:], gate[:], ACT.Exp).then_inc(exped, 1)

            ln.square(act, 0)
            ln.scale(act, 0)
            exps(0)
            act.preload_act_table_set(GELU)
            with act.Fori(0, NB) as b:
                for i in range(NC):
                    s = i % SLOTS
                    e, k = i // HC, i % HC
                    act.wait_ge(up_done, START + b * NC + i + 1)
                    act.wait_ge(lo_done, START + b * NC + i + 1)
                    act.activation(g32[:, s, :], m.ps[:, UP[i % len(UP)], :], ACT.Gelu,
                                   bias=w.b1[:, i:i + 1]).then_inc(gelu_done, 1)
                    if not by_dve(i):
                        act.wait_ge(down_done, START + b * NC + i + 1)
                        act.activation(gh[:, s, :], m.ps[:, UP[i % len(UP)], :], ACT.Gelu,
                                       bias=w.b1[:, i:i + 1]).then_inc(rounded, 1)
                    if i == AT_CENTRE:
                        ln.square(act, b + 1)
                    if i == AT_SCALE:
                        ln.scale(act, b + 1)
                    if i == AT_PEAK + 1:
                        exps(b + 1)

        @block.vector
        def _(dve):
            def gates(n):
                l3 = m.ps[:, GB, :TT * NE].rearrange("p (t e) -> p t e", e=NE)
                dve.wait_ge(logits_done, START + n + 1)
                dve.tensor_reduce(peak[:], l3, AX.X, ALU.max).then_inc(gchain, 1)
                dve.wait_ge(gchain, START + n * GSTEPS + 1)
                dve.tensor_tensor(gate[:], l3, peak[:].unsqueeze(2).to_broadcast([P, TT, NE]),
                                  ALU.subtract).then_inc(peeled, 1)

            def weights(n, step):
                a = gate[:].unsqueeze(2).to_broadcast([P, TT, NE, NE])
                z = gate[:].unsqueeze(3).to_broadcast([P, TT, NE, NE])
                if step == 0:
                    dve.wait_ge(exped, START + n + 1)
                    dve.tensor_reduce(total[:], gate[:], AX.X, ALU.add).then_inc(gchain, 1)
                    dve.tensor_tensor(more[:], a, z, ALU.is_gt).then_inc(gchain, 1)
                    dve.tensor_tensor(ties[:], a, z, ALU.is_ge).then_inc(gchain, 1)
                elif step == 1:
                    dve.wait_ge(gchain, START + n * GSTEPS + 4)
                    dve.reciprocal(rtotal[:], total[:]).then_inc(gchain, 1)
                    dve.tensor_tensor(ties[:], ties[:], m.before[:].unsqueeze(1).to_broadcast([P, TT, NE, NE]),
                                      ALU.mult).then_inc(gchain, 1)
                elif step == 2:
                    dve.wait_ge(gchain, START + n * GSTEPS + 6)
                    dve.tensor_tensor(more[:], more[:], ties[:], ALU.max).then_inc(gchain, 1)
                elif step == 3:
                    dve.wait_ge(gchain, START + n * GSTEPS + 7)
                    dve.tensor_reduce(rank[:], more[:], AX.X, ALU.add).then_inc(gchain, 1)
                    dve.wait_ge(gchain, START + n * GSTEPS + 8)
                    dve.wait_ge(turned, START + n)
                    dve.scalar_tensor_tensor(out=cw[:], in0=rank[:], scalar=2.0, in1=gate[:], op0=ALU.is_lt,
                                             op1=ALU.mult).then_inc(wchain, 1)
                    dve.wait_ge(wchain, START + n + 1)
                    dve.scalar_tensor_tensor(out=cw[:], in0=cw[:], scalar=0.5, in1=rtotal[:].unsqueeze(2).to_broadcast([P, TT, NE]),
                                             op0=ALU.mult, op1=ALU.mult).then_inc(gated, 1)

            def keep_cwt(n):
                dve.wait_ge(turned, START + n + 1)
                dve.wait_ge(cw_out, START + 16 * n)
                dve.tensor_copy(cwt[:], m.ps[:NE, GB, :]).then_inc(cwt_done, 1)

            def halves(n):
                dve.wait_ge(up_done, START + n * NC)
                dve.wait_ge(ln.normed, START + n + 1)
                dve.tensor_copy(xh[:], ln.out[:]).then_inc(xh_done, 1)
                dve.wait_ge(xh_done, START + n + 1)
                dve.tensor_tensor(xl[:], ln.out[:], xh[:], ALU.subtract).then_inc(split, 1)

            def take_part(b, e):
                dve.wait_ge(down_done, START + b * NC + HC * (e + 1) + SLOTS)
                dve.wait_ge(cw_in[e], START + 16 * (b + 1))
                if e >= 2:
                    dve.wait_ge(summed, START + b * (NE - 1) + e - 1)
                else:
                    dve.wait_ge(summed, START + b * (NE - 1))
                dve.scalar_tensor_tensor(out=part[:, e % 2, :], in0=m.ps[:, YB[e % 2], :], scalar=w.b2[:, e:e + 1],
                                         in1=cwb[:, e, :], op0=ALU.add, op1=ALU.mult).then_inc(part_done, 1)

            dve.sem_inc(lo_done, SLOTS)
            dve.sem_inc(down_done, SLOTS)
            dve.sem_inc(part_done, 2)
            ln.norm(dve, 0)
            gates(0)
            for step in range(4):
                weights(0, step)
            keep_cwt(0)
            halves(0)
            with dve.Fori(0, NB) as b:
                for i in range(NC - HC + TAKE + 1):
                    if i < NC:
                        s = i % SLOTS
                        if by_dve(i):
                            dve.wait_ge(down_done, START + b * NC + i + 1)
                            dve.wait_ge(gelu_done, START + b * NC + i + 1)
                            dve.tensor_copy(gh[:, s, :], g32[:, s, :]).then_inc(copied, 1)
                            dve.wait_ge(copied, START + b * ROUNDED[1] + nth(i) + 1)
                        else:
                            dve.wait_ge(rounded, START + b * ROUNDED[0] + nth(i) + 1)
                        dve.tensor_tensor(gl[:, s, :], g32[:, s, :], gh[:, s, :], ALU.subtract).then_inc(lo_done, 1)
                    if i >= TAKE and (i - TAKE) % HC == 0 and (i - TAKE) // HC < NE:
                        take_part(b, (i - TAKE) // HC)
                    if i == AT_NORM:
                        ln.norm(dve, b + 1)
                    if i == AT_PEAK:
                        gates(b + 1)
                    if 0 <= i - AT_WEIGHTS < 4:
                        weights(b + 1, i - AT_WEIGHTS)
                    if i == AT_KEEP:
                        keep_cwt(b + 1)
                    if i == NC:
                        halves(b + 1)

        @block.gpsimd
        def _(pool):
            ln.take(pool, 0, m.x, 0)
            with pool.Fori(0, NB) as b:
                ln.take(pool, b + 1, m.x, b + 1)
                for e in range(1, NE):
                    pool.wait_ge(part_done, START + b * NE + e + 1 + 2)
                    if e == 1:
                        pool.wait_ge(x_done, START + b)
                        pool.tensor_tensor(acc[:], part[:, 0, :], part[:, 1, :], ALU.add).then_inc(summed, 1)
                    else:
                        pool.wait_ge(summed, START + b * (NE - 1) + e - 1)
                        pool.tensor_tensor(acc[:], acc[:], part[:, e % 2, :], ALU.add).then_inc(summed, 1)
                pool.wait_ge(summed, START + (b + 1) * (NE - 1))
                pool.tensor_tensor(seq(m.x, b), acc[:], seq(m.x, b), ALU.add).then_inc(x_done, 1)

        @block.sync
        def _(sp):
            def spread(n, used=None):
                sp.wait_ge(cwt_done, START + n + 1)
                if used is not None:
                    for e in range(NE):
                        sp.wait_ge(cw_in[e], START + 16 * used + 16)
                sp.dma_start(cw_dram[:], cwt[:]).then_inc(cw_out, 16)
                sp.wait_ge(cw_out, START + 16 * (n + 1))
                for e in range(NE):
                    if used is not None:
                        sp.wait_ge(part_done, START + used * NE + e + 1 + 2)
                    sp.dma_start(cwb[:, e, :], cw_dram[e:e + 1, :].to_broadcast([P, T])).then_inc(cw_in[e], 16)

            spread(0)
            with sp.Fori(0, NB) as b:
                spread(b + 1, used=b)
            for e in range(NE):
                sp.wait_ge(cw_in[e], START + 16 * (NB + 1))


def moe_weights(nc, c):
    w = Mem()
    sb = lambda n, s, d=F32: c.enter_context(nc.sbuf_tensor(n, s, d))
    w.w1h, w.w1l = sb("w1h", [P, NE, T], F32R), sb("w1l", [P, NE, T], F32R)
    w.w2h, w.w2l = sb("w2h", [P, NE, HC, P], F32R), sb("w2l", [P, NE, HC, P], F32R)
    w.b1, w.b2, w.gate = sb("b1", [P, NE * HC]), sb("b2", [P, NE]), sb("w_gate", [P, NE])
    return w


def ssm_phase(nc, m, ins):
    with Phase(nc) as c:
        sb = lambda n, s, d=F32: c.enter_context(nc.sbuf_tensor(f"ssm_{n}", s, d))
        sem = lambda n: c.sem(f"ssm_{n}")
        ln = Norm(nc, c, m, "ssm_ln", 0, 1)
        DTB, ZB = 2, 3
        CONV = 4
        XB = [4, 5]
        XSTART, XRATE = 4, 2
        w_in = sb("w_in", [P, 3 * P])
        w_dt, w_dtx = sb("w_dt", [P, 2 * P - NH]), sb("w_dtx", [P, P])
        w_out = sb("w_out", [P, P])
        conv_w, conv_b = sb("conv_w", [P, 3, 4]), sb("conv_b", [P, 3])
        a_par, dt_b = sb("a_par", [P, 2]), sb("dt_b", [P, 2])
        spread_p, gather_p = sb("spread_p", [P, NS, P]), sb("gather_p", [P, NS, P])
        spread_h = sb("spread_h", [P, NB, P])
        chunk_mask = sb("chunk_mask", [P, T])
        raw = sb("raw", [P, 3, T + 3])
        cbx = sb("cbx", [P, 3, T])
        z, az, ez, lz = (sb(n, [P, 2, T]) for n in ("z", "az", "ez", "lz"))
        cum, grow, fall = (sb(n, [P, 2, T]) for n in ("cum", "grow", "fall"))
        carry = sb("carry", [P, 2, T])
        state, rnorm = sb("state", [P, T]), sb("rnorm", [P, T])
        be, ce = sb("be", [P, T]), sb("ce", [P, T])
        d1, g, cg = sb("d1", [P, 2, T]), sb("g", [P, 2, T]), sb("cg", [P, 2, T])
        y, yb = sb("y", [P, T]), sb("yb", [P, 2, T])
        late_in = sem("late_in")
        ins_in, zeroed, stepped, conved = sem("ins_in"), sem("zeroed"), sem("stepped"), sem("conv_in")
        chain, absd, exped, logged, curves = sem("chain"), sem("absd"), sem("exped"), sem("logged"), sem("curves")
        xrep, cg_done, y_done, d1_done = sem("xrep"), sem("cg_done"), sem("y_done"), sem("d1_done")
        rn_ready, yb_done, out_done, x_done, y_kept = sem("rn_ready"), sem("yb_done"), sem("out_done"), sem("x_done"), sem("y_kept")
        rnormed, raw_done, cx_done, cum_done = sem("rnormed"), sem("raw_done"), sem("cx_done"), sem("cum_done")
        block = c.block()
        LOADS = [(w_in, "ssm_w_in"), (w_dtx, "ssm_w_dtx"), (conv_w, "ssm_conv_w"), (conv_b, "ssm_conv_b"),
                 (a_par, "ssm_a"), (dt_b, "ssm_dt_b")]
        LATE_LOADS = [(chunk_mask, "chunk_mask"), (spread_p, "spread_p"), (gather_p, "gather_p"),
                      (spread_h, "spread_h"), (w_out, "ssm_w_out")]

        @block.sync
        def _(sp):
            for t, n in LOADS:
                sp.dma_start(t[:], ins[n]).then_inc(ins_in, 16)
            sp.wait_ge(zeroed, START + 1)
            sp.dma_start(w_dt[:, P - NH:P], ins["ssm_w_dt"]).then_inc(ins_in, 16)
            for t, n in LATE_LOADS:
                sp.dma_start(t[:], ins[n]).then_inc(late_in, 16)

        ALL_IN = 16 * (len(LOADS) + 1)

        @block.gpsimd
        def _(pool):
            pool.memset(w_dt[:], 0.0).then_inc(zeroed, 1)
            pool.memset(raw[:, :, 0:3], 0.0).then_inc(zeroed, 1)

        @block.tensor
        def _(pe):
            def heads_x(p):
                if p >= 2:
                    pe.wait_ge(d1_done, START + p - 1)
                pe.matmul(m.ps[:, XB[p % 2], :], spread_p[:, p, :], cbx[:, 2, :], start=True, stop=True).then_inc(xrep, 1)

            def heads_y(p):
                pe.wait_ge(cg_done, START + p + 1)
                pe.matmul(m.ps[:, 7, :], gather_p[:, p, :], cg[:, p % 2, :], start=(p == 0),
                          stop=(p == NS - 1)).then_inc(y_done, 1)

            ln.centre(pe, 0, m.x[:, :T])
            ln.variance(pe, 0)
            pe.wait_ge(ins_in, START + ALL_IN)
            for b in range(NB):
                if b + 1 < NB:
                    ln.centre(pe, b + 1, m.x[:, (b + 1) * T:(b + 2) * T])
                if b == NB - 1:
                    pe.wait_ge(ln.normed, START + NB)
                lo = P - NH - NH * b
                pe.matmul(m.ps[:, DTB, :], w_dt[:, lo:lo + P], ln.out[:], start=(b == 0), stop=(b == NB - 1)).then_inc(stepped, 1)
                if b == 0:
                    for k in range(3):
                        pe.matmul(m.ps[:, CONV + k, :], w_in[:, k * P:(k + 1) * P], ln.out[:], start=True,
                                  stop=True).then_inc(conved, 1)
                    pe.matmul(m.ps[:, ZB, :], w_dtx[:], ln.out[:], start=True, stop=True).then_inc(conved, 1)
                if b + 1 < NB:
                    ln.variance(pe, b + 1)
                if b >= XSTART:
                    if b == XSTART:
                        pe.wait_ge(cx_done, START + 1)
                        pe.wait_ge(late_in, START + 16 * len(LATE_LOADS))
                        heads_x(0)
                    for p in range((b - XSTART) * XRATE, (b - XSTART + 1) * XRATE):
                        if p + 1 < NS:
                            heads_x(p + 1)
                        if p < NS:
                            heads_y(p)
            pe.wait_ge(rnormed, START + 1)
            for b in range(NB + 1):
                if b < NB:
                    if b >= 2:
                        pe.wait_ge(yb_done, START + b - 1)
                    pe.matmul(m.ps[:, b % 2, :], spread_h[:, b, :], rnorm[:], start=True, stop=True).then_inc(rn_ready, 1)
                if b > 0:
                    pe.wait_ge(yb_done, START + b)
                    if b > 2:
                        pe.wait_ge(x_done, START + b - 2)
                    pe.matmul(m.ps[:, 2 + b % 2, :], w_out[:], yb[:, (b - 1) % 2, :], start=True, stop=True).then_inc(out_done, 1)

        @block.scalar
        def _(act):
            def softplus(i):
                act.wait_ge(absd, START + 2 - i)
                act.activation(ez[:, i, :], az[:, i, :], ACT.Exp, scale=-1.0).then_inc(exped, 1)
                act.wait_ge(exped, START + 2 - i)
                act.activation(lz[:, i, :], ez[:, i, :], ACT.Ln, bias=1.0).then_inc(logged, 1)

            def decays(i):
                act.wait_ge(cum_done, START + 2 - i)
                act.activation(fall[:, i, :], cum[:, i, :], ACT.Exp, scale=-1.0).then_inc(curves, 1)
                act.activation(grow[:, i, :], cum[:, i, :], ACT.Exp).then_inc(curves, 1)

            act.preload_act_table_set(EXP_LN)
            for b in range(NB):
                ln.square(act, b)
                ln.scale(act, b)
                if b == 0:
                    act.wait_ge(conved, START + 3)
                    act.wait_ge(zeroed, START + 2)
                    for k in range(3):
                        act.activation(raw[:, k, 3:], m.ps[:, CONV + k, :], ACT.Copy).then_inc(raw_done, 1)
                if b == 1:
                    softplus(1)
                if b == 2:
                    decays(1)
            softplus(0)
            decays(0)

        @block.vector
        def _(dve):
            count = [0]

            def step(ins_):
                ins_.then_inc(chain, 1)
                count[0] += 1
                dve.wait_ge(chain, START + count[0])

            def convolve(k):
                dve.wait_ge(raw_done, START + 3)
                step(dve.tensor_scalar(cbx[:, k, :], raw[:, k, 0:T], conv_w[:, k, 0:1], conv_b[:, k:k + 1], ALU.mult, ALU.add))
                for j in range(1, 4):
                    step(dve.scalar_tensor_tensor(out=cbx[:, k, :], in0=raw[:, k, j:j + T], scalar=conv_w[:, k, j:j + 1],
                                                  in1=cbx[:, k, :], op0=ALU.mult, op1=ALU.add))

            def absolute(i):
                step(dve.tensor_scalar(z[:, i, :], m.ps[:, DTB + i, :], dt_b[:, i:i + 1], None, ALU.add))
                step(dve.tensor_scalar(az[:, i, :], z[:, i, :], -1.0, None, ALU.mult))
                dve.tensor_tensor(az[:, i, :], az[:, i, :], z[:, i, :], ALU.max).then_inc(absd, 1)

            def decay(i):
                dve.wait_ge(logged, START + 2 - i)
                step(dve.scalar_tensor_tensor(out=z[:, i, :], in0=z[:, i, :], scalar=0.0, in1=lz[:, i, :], op0=ALU.max, op1=ALU.add))
                step(dve.tensor_scalar(z[:, i, :], z[:, i, :], a_par[:, i:i + 1], None, ALU.mult))
                dve.tensor_tensor_scan(cum[:, i, :], chunk_mask[:], z[:, i, :], 0.0, ALU.mult, ALU.add).then_inc(cum_done, 1)

            def carries(i):
                dve.wait_ge(curves, START + 2 * (2 - i))
                step(dve.memset(carry[:, i, :], 1.0))
                step(dve.tensor_copy(carry[:, i, CHUNK::CHUNK], grow[:, i, CHUNK - 1:T - 1:CHUNK]))

            def head_states(p):
                s = p % 2
                dve.wait_ge(xrep, START + p + 1)
                dve.tensor_tensor(d1[:, s, :], m.ps[:, XB[s], :], be[:], ALU.mult).then_inc(d1_done, 1)
                dve.wait_ge(d1_done, START + p + 1)
                step(dve.tensor_tensor_scan(g[:, s, :], carry[:, 1, :], d1[:, s, :], 0.0, ALU.mult, ALU.add))
                if p >= 2:
                    dve.wait_ge(y_done, START + p - 1)
                dve.tensor_tensor(cg[:, s, :], g[:, s, :], ce[:], ALU.mult).then_inc(cg_done, 1)

            for b in range(NB):
                if b >= 1:
                    dve.wait_ge(stepped, START + b)
                    if b == 1:
                        dve.wait_ge(conved, START + 4)
                ln.norm(dve, b)
                if b == 0:
                    dve.wait_ge(ins_in, START + ALL_IN)
                if b == 1:
                    dve.wait_ge(late_in, START + 16 * len(LATE_LOADS))
                    absolute(1)
                    convolve(2)
                if b == 2:
                    decay(1)
                    convolve(1)
                if b == 3:
                    carries(1)
                    step(dve.tensor_tensor(be[:], cbx[:, 1, :], fall[:, 1, :], ALU.mult))
                    convolve(0)
                    step(dve.tensor_tensor(ce[:], cbx[:, 0, :], grow[:, 1, :], ALU.mult))
                    dve.sem_inc(cx_done, 1)
                if b >= XSTART:
                    for p in range((b - XSTART) * XRATE, min((b - XSTART + 1) * XRATE, NS)):
                        head_states(p)
            dve.wait_ge(stepped, START + NB)
            absolute(0)
            decay(0)
            carries(0)
            step(dve.tensor_tensor_scan(state[:], carry[:, 0, :], fall[:, 0, :], 0.0, ALU.mult, ALU.add))
            step(dve.tensor_tensor(state[:], state[:], grow[:, 0, :], ALU.mult))
            dve.reciprocal(rnorm[:], state[:]).then_inc(rnormed, 1)
            dve.wait_ge(y_done, START + NS)
            dve.tensor_copy(y[:], m.ps[:, 7, :]).then_inc(y_kept, 1)
            dve.wait_ge(y_kept, START + 1)
            for b in range(NB + 1):
                if b < NB:
                    dve.wait_ge(rn_ready, START + b + 1)
                    if b >= 2:
                        dve.wait_ge(out_done, START + b - 1)
                    dve.tensor_tensor(yb[:, b % 2, :], m.ps[:, b % 2, :], y[:], ALU.mult).then_inc(yb_done, 1)
                if b > 0:
                    dve.wait_ge(out_done, START + b)
                    xb = m.x[:, (b - 1) * T:b * T]
                    dve.tensor_tensor(xb, m.ps[:, 2 + b % 2, :], xb, ALU.add).then_inc(x_done, 1)


EXP_LN = "natural_log_exp_and_others"
GELU = "gelu_and_others"


def entry_phase(nc, m, app):
    with Phase(nc) as c:
        WAYS = 4
        lns = [Norm(nc, c, m, f"entry{app}_{i}", 2 * i, 2 * i + 1) for i in range(WAYS)]
        block = c.block()

        @block.tensor
        def _(pe):
            for b in range(NB + 2):
                if b < NB:
                    lns[b % WAYS].centre(pe, b // WAYS, m.x[:, b * T:(b + 1) * T])
                if b >= 2:
                    lns[(b - 2) % WAYS].variance(pe, (b - 2) // WAYS)

        @block.scalar
        def _(act):
            act.preload_act_table_set(EXP_LN)
            for b in range(NB + 2):
                if b < NB:
                    lns[b % WAYS].square(act, b // WAYS)
                if b >= 2:
                    lns[(b - 2) % WAYS].scale(act, (b - 2) // WAYS)

        @block.vector
        def _(dve):
            for b in range(NB):
                lns[b % WAYS].norm(dve, b // WAYS, m.u[:, b * T:(b + 1) * T])


def gated_weights(nc, c, m, ins):
    ws = []
    sb = lambda n, s, d=F32: c.enter_context(nc.sbuf_tensor(n, s, d))
    m.per_head, m.ident_bf, m.masks = sb("per_head", [P, P]), sb("ident_bf", [P, P], BF16), sb("masks_bf", [P, 2, T], BF16)
    m.tiny, m.unscale = sb("tiny", [P, 1]), sb("unscale", [P, 2])
    for l in range(2):
        w = Mem()
        w.qkh, w.qkl = sb(f"wqk_h{l}", [P, 4, T], F32R), sb(f"wqk_l{l}", [P, 4, T], F32R)
        w.vh, w.vl = sb(f"wv_h{l}", [P, T], F32R), sb(f"wv_l{l}", [P, T], F32R)
        w.wo = sb(f"wo{l}", [P, HP, P])
        w.w1h, w.w1l = sb(f"w1_h{l}", [P, 2 * HID], F32R), sb(f"w1_l{l}", [P, 2 * HID], F32R)
        w.w2 = sb(f"w2_{l}", [P, MC, P])
        w.bias, w.b2 = sb(f"w1_bias{l}", [P, 2 * MC]), sb(f"b2_{l}", [P, 1])
        w.tables = sb(f"tables{l}", [P, 4, T])
        ws.append(w)
    with Phase(nc) as s:
        tb = lambda n, sh, d=F32: s.enter_context(nc.sbuf_tensor(n, sh, d))
        raws, raw1s = tb("raw_qkv", [P, 2, 3 * T]), tb("raw_gated_w1", [P, 2, 2 * HID])
        raw_masks = tb("raw_masks", [P, 2, T])
        scales, lnw, b1 = tb("qk_scales", [P, 2, 4]), tb("ln_w", [P, 2, 2]), tb("b1_raw", [P, 2, 2 * MC])
        raw_in = [s.sem(f"gw_raw{l}") for l in range(2)]
        rest_in, biased, steps, extras_in = (s.sem(n) for n in ("gw_rest", "gw_biased", "gw_steps", "extras_in"))
        rest2_in, cleared = s.sem("gw_rest2"), s.sem("gw_cleared")
        block = s.enter_context(nc.Block())
        REST = 16 * (3 + 2 * 4)

        @block.sync
        def _(sp):
            for l in range(2):
                sp.dma_start(raws[:, l, :], ins["L1_ffn_wqkv"][l]).then_inc(raw_in[l], 16)
                sp.dma_start(raw1s[:, l, :], ins["L1_ffn_w1"][l]).then_inc(raw_in[l], 16)
            for l, w in enumerate(ws):
                sp.dma_start(w.wo[:], ins["L1_ffn_wo"][l].rearrange("(j p) d -> p j d", p=P)).then_inc(rest_in, 16)
                sp.dma_start(w.w2[:MW, 0:2, :], ins["L1_ffn_w2"][l][0:2 * MW, :].rearrange("(j p) d -> p j d", p=MW)).then_inc(rest_in, 16)
                sp.dma_start(w.w2[:HID - 2 * MW, 2, :], ins["L1_ffn_w2"][l][2 * MW:HID, :]).then_inc(rest_in, 16)
                sp.dma_start(w.b2[:], ins["b2_gated"][l]).then_inc(rest2_in, 16)
            sp.wait_ge(rest2_in, 32)

        @block.scalar
        def _(act):
            act.dma_start(scales[:], ins["qk_scales"]).then_inc(rest_in, 16)
            act.dma_start(lnw[:], ins["ln_w"]).then_inc(rest_in, 16)
            act.dma_start(b1[:], ins["b1_gated"]).then_inc(rest_in, 16)
            for w in ws:
                act.dma_start(w.tables[:], ins["rotary"]).then_inc(rest_in, 16)
            act.dma_start(raw_masks[:], ins["masks"]).then_inc(extras_in, 16)
            act.dma_start(m.per_head[:], ins["per_head"]).then_inc(extras_in, 16)

        @block.vector
        def _(dve):
            n = 0
            dve.memset(m.ps[:, 0:2, :2 * MC], 0.0).then_inc(cleared, 1)
            dve.memset(m.tiny[:], 2.0 ** -64)
            dve.memset(m.unscale[:, 0:1], 8 * math.log(2.0) + math.log(8.0))
            dve.memset(m.unscale[:, 1:2], 8 * math.log(2.0))
            dve.memset(m.u[:, NB * T:], 0.0)
            dve.tensor_copy(m.ident_bf[:], m.ident[:])
            for l, w in enumerate(ws):
                raw, raw1 = raws[:, l, :], raw1s[:, l, :]
                dve.wait_ge(raw_in[l], 32)
                sw = lambda t: t.rearrange("p (h s j) -> p h s j", s=2, j=DH // 2)
                pairs = [(raw[:, 2 * T:], w.vh[:], w.vl[:])]
                for i in range(2):
                    src = raw[:, i * T:(i + 1) * T]
                    pairs.append((src, w.qkh[:, 2 * i, :], w.qkl[:, 2 * i, :]))
                    for half in range(2):
                        pairs.append((sw(src)[:, :, 1 - half, :], sw(w.qkh[:, 2 * i + 1, :])[:, :, half, :],
                                      sw(w.qkl[:, 2 * i + 1, :])[:, :, half, :]))
                n = split_weights(dve, pairs, steps, n)
                if l == 0:
                    dve.wait_ge(rest_in, REST)
                for k in range(4):
                    dve.tensor_scalar(w.tables[:, k, :], w.tables[:, k, :], scales[:, l, k:k + 1], None,
                                      ALU.mult).then_inc(steps, 1)
                    n += 1
                dve.wait_ge(biased, l + 1)
                dve.tensor_tensor(w.bias[:], m.ps[:, l, :2 * MC], b1[:, l, :], ALU.add).then_inc(steps, 1)
                dve.tensor_scalar(raw1, raw1, lnw[:, l, 0:1], None, ALU.mult).then_inc(steps, 1)
                n += 2
                dve.wait_ge(steps, n)
                n = split_weights(dve, [(raw1, w.w1h[:], w.w1l[:])], steps, n)
            dve.wait_ge(extras_in, 32)
            dve.tensor_copy(m.masks[:], raw_masks[:])

        @block.tensor
        def _(pe):
            pe.wait_ge(rest_in, REST)
            pe.wait_ge(cleared, 1)
            for l in range(2):
                pe.wait_ge(raw_in[l], 32)
                for i in range(2 * MC):
                    lo = (i // MC) * HID + (i % MC) * MW
                    n = min(MW, HID - (i % MC) * MW)
                    mm = pe.matmul(m.ps[:n, l, i:i + 1], raw1s[:, l, lo:lo + n], lnw[:, l, 1:2], start=True, stop=True)
                mm.then_inc(biased, 1)
    return ws


def attention_phase(nc, m, app, l, w):
    Q, QR, K, KR, S, PT, O = 0, 1, 2, 3, 4, 6, 7
    HW = NW // 2
    NT = T // P
    ORDER = [1, 0, 3, 2]
    V_ORDER = [0, 2, 1, 3]
    V_BANK = [0, 1, 0, 0]
    V_TILES = [[t for t in V_ORDER if V_BANK[t] == k] for k in range(2)]
    with Phase(nc) as c:
        name = f"att{app}{l}"
        sb = lambda n, s, d=F32: c.enter_context(nc.sbuf_tensor(f"{name}_{n}", s, d))
        sem = lambda n: c.sem(f"{name}_{n}")
        hs = sb("hs", [P, T])
        hh, hl = sb("hh", [P, T], F32R), sb("hl", [P, T], F32R)
        v, v_even = sb("v", [P, NT, T]), sb("v_even", [P, NT, T])
        turned = sb("turned", [P, 4, T])
        sums = sb("sums", [P, 2, T])
        squares = sb("squares", [P, 2, T])
        rn = sb("rn", [P, 2, T])
        qn, kn = sb("qn", [P, 2, T]), sb("kn", [P, 2, 2 * (NT + 1), WIN])
        probs = sb("probs", [P, 2, NW, P])
        nmax, psum_, rsum = sb("nmax", [P, 2, NW]), sb("psum", [P, 2, NW]), sb("rsum", [P, 2, NW])
        pts = sb("pts", [P, 2, T])
        o = sb("o", [P, HP, T])
        zeroed, taken, hi_done, split = sem("zeroed"), sem("taken"), sem("hi_done"), sem("split")
        projected, rotated, squared, added = sem("projected"), sem("rotated"), sem("squared"), sem("added")
        ss_done, ss_logged, rn_done, qk_done = sem("ss_done"), sem("ss_logged"), sem("rn_done"), sem("qk_done")
        sim_done, maxed, exped, recip, normed = sem("sim_done"), sem("maxed"), sem("exped"), sem("recip"), sem("normed")
        pt_done, pt_kept0, pt_kept1, pv_done = sem("pt_done"), sem("pt_kept0"), sem("pt_kept1"), sem("pv_done")
        zeroed2 = sem("zeroed2")
        o_kept, wo_done, u_done = sem("o_kept"), sem("wo_done"), sem("u_done")
        v_done, v_kept0, v_kept1, v_copied = sem("v_done"), sem("v_kept0"), sem("v_kept1"), sem("v_copied")
        block = c.block()
        pt_kept = [pt_kept0, pt_kept1]
        v_kept = [v_kept0, v_kept1]

        @block.tensor
        def _(pe):
            def project(n, j, kinds):
                cols = slice(j * P, (j + 1) * P)
                for k in kinds:
                    if k % 2 == 0:
                        pe.wait_ge(ss_logged, START + 2 * n + k // 2 + 1)
                    else:
                        pe.wait_ge(rotated, START + 4 * n + k)
                    mm3(pe, m.ps[:, Q + k, :], (w.qkh[:, k, cols], w.qkl[:, k, cols]),
                        (hh[:], hl[:])).then_inc(projected, 1)

            def norms(n, i):
                pe.wait_ge(squared, START + 2 * n + i + 1)
                pe.wait_ge(rotated, START + 4 * n + 2 * i + 2 + 4)
                pe.matmul(m.ps[:, Q + 2 * i, :], m.per_head[:], squares[:, i, :], start=True, stop=True).then_inc(ss_done, 1)

            def sims(n, j):
                for half in range(2):
                    if half == 0:
                        pe.wait_ge(qk_done, START + 2 * n + 2)
                    pe.wait_ge(exped, START + NW * n + HW * (half + 1))
                    pe.matmul(m.ps[:, S + half, :], m.ident_bf[:], m.masks[:, half, :], start=True, stop=True)
                    for i in range(HW):
                        win = half * HW + i
                        even, apart = win // 2, NT + win % 2
                        for h in range(2):
                            r = slice(DH * h, DH * h + DH)
                            mm = pe.matmul(m.ps[r, S + half, i * P:(i + 1) * P], qn[r, j % 2, win * WIN:(win + 1) * WIN],
                                           kn[r, j % 2, even:even + apart + 1:apart, :], start=False,
                                           stop=True, skip_group_check=True)
                    mm.then_inc(sim_done, 1)

            def turn(n, j, half):
                pe.wait_ge(normed, START + 2 * n + half + 1)
                if half == 0:
                    pe.wait_ge(pt_kept[1], START + n + 1)
                else:
                    pe.wait_ge(pt_kept[0], START + n + 1 + 1)
                for i in range(HW):
                    tr = pe.transpose(m.ps[:, PT, i * P:(i + 1) * P], probs[:, j % 2, half * HW + i, :], m.ident[:])
                tr.then_inc(pt_done, 1)

            def values(n, j, half):
                pe.wait_ge(pt_kept[half], START + n + 1 + 1)
                if half == 0:
                    pe.wait_ge(o_kept, START + n + 1)
                for i in range(HW):
                    win = half * HW + i
                    for h in range(2):
                        mm = pe.matmul(m.ps[DH * h:DH * h + DH, O, win * WIN:(win + 1) * WIN],
                                       (v_even, v)[win % 2][:, win // 2, j * P + DH * h:j * P + DH * h + DH],
                                       pts[:, half, i * P + DH * h:i * P + DH * h + DH], start=True, stop=True)
                mm.then_inc(pv_done, 1)

            def make_values(b, tiles):
                for t in tiles:
                    k = V_BANK[t]
                    kept = V_TILES[k].index(t)
                    if kept == 0:
                        pe.wait_ge((pt_kept[1], u_done)[k], START + (HP * b + 1, b)[k])
                    else:
                        pe.wait_ge(v_kept[k], START + len(V_TILES[k]) * b + kept)
                    mm3(pe, m.ps[:, (PT, O)[k], :], (hh[:, t * P:(t + 1) * P], hl[:, t * P:(t + 1) * P]),
                        (w.vh[:], w.vl[:])).then_inc(v_done, 1)

            def output(b):
                pe.wait_ge(o_kept, START + HP * (b + 1) + 1)
                for j in range(HP):
                    mm = pe.matmul(m.ps[:, O, :], w.wo[:, j, :], o[:, j, :], start=(j == 0), stop=(j == HP - 1))
                mm.then_inc(wo_done, 1)

            def unit(b, j, first=False, ahead=True, own=True):
                n = b * HP + j
                before = (j - 1) % HP
                if ahead:
                    if j == HP - 1:
                        pe.wait_ge(split, START + b + 2)
                    project(n + 1, (j + 1) % HP, ORDER)
                if own:
                    sims(n, j)
                if j == 1:
                    for k in range(2):
                        pe.wait_ge(v_kept[k], START + len(V_TILES[k]) * (b + 1))
                    pe.wait_ge(v_copied, START + 32 * (b + 1))
                if not first:
                    turn(n - 1, before, 0)
                if ahead:
                    norms(n + 1, 0)
                if not first:
                    turn(n - 1, before, 1)
                    values(n - 1, before, 0)
                if ahead:
                    norms(n + 1, 1)
                if not first:
                    values(n - 1, before, 1)
                if j == 0:
                    if own:
                        make_values(b, V_ORDER[:1])
                    if not first:
                        output(b - 1)
                    if own:
                        make_values(b, V_ORDER[1:])

            pe.sem_inc(pt_done, 2)
            pe.wait_ge(split, START + 1)
            project(0, 0, ORDER)
            norms(0, 0)
            norms(0, 1)
            unit(0, 0, first=True)
            with pe.Fori(0, NB - 1) as b:
                for j in range(1, HP):
                    unit(b, j)
                unit(b + 1, 0)
            for j in range(1, HP):
                unit(NB - 1, j, ahead=(j < HP - 1))
            unit(NB, 0, ahead=False, own=False)

        @block.scalar
        def _(act):
            def square(n, i):
                act.wait_ge(projected, START + 4 * n + ORDER.index(2 * i) + 1)
                act.wait_ge(ss_done, START + 2 * n)
                act.activation(squares[:, i, :], m.ps[:, Q + 2 * i, :], ACT.Square).then_inc(squared, 1)

            def scale(n, i):
                act.wait_ge(ss_done, START + 2 * n + i + 1)
                act.wait_ge(qk_done, START + 2 * n)
                act.activation(rn[:, i, :], m.ps[:, Q + 2 * i, :], ACT.Ln, bias=m.tiny[:, 0:1],
                               scale=SS_SCALE).then_inc(ss_logged, 1)
                act.wait_ge(ss_logged, START + 2 * n + i + 1 + 2)
                act.activation(rn[:, i, :], rn[:, i, :], ACT.Exp, scale=-0.5,
                               bias=m.unscale[:, i:i + 1]).then_inc(rn_done, 1)

            def exps(n, j, half):
                for win in range(half * HW, (half + 1) * HW):
                    if win % HW == 0:
                        act.wait_ge(maxed, START + 2 * n + win // HW + 1)
                        act.wait_ge(pt_done, START + 2 * n)
                    act.activation(probs[:, j % 2, win, :], m.ps[:, S + win // HW, (win % HW) * P:(win % HW + 1) * P],
                                   ACT.Exp, bias=nmax[:, j % 2, win:win + 1],
                                   accum_out=psum_[:, j % 2, win:win + 1]).then_inc(exped, 1)

            def keep_turned(n):
                act.wait_ge(pt_done, START + 2 * n + 1 + 2)
                act.wait_ge(pv_done, START + 2 * n)
                act.activation(pts[:, 0, :], m.ps[:, PT, :], ACT.Copy).then_inc(pt_kept[0], 1)

            def unit(b, j, first=False, ahead=True, own=True):
                n = b * HP + j
                for i in range(2 if ahead else 0):
                    square(n + 1, i)
                if not first:
                    keep_turned(n - 1)
                if own:
                    exps(n, j, 0)
                for i in range(2 if ahead else 0):
                    scale(n + 1, i)
                if own:
                    exps(n, j, 1)
                if j == 0 and own:
                    act.wait_ge(v_copied, START + 32 * b)
                    for t in V_TILES[0]:
                        act.wait_ge(v_done, START + NT * b + V_ORDER.index(t) + 1)
                        act.activation(v[:, t, :], m.ps[:, PT, :], ACT.Copy).then_inc(v_kept[0], 1)
                    act.wait_ge(v_kept[1], START + len(V_TILES[1]) * (b + 1))
                    act.wait_ge(v_kept[0], START + len(V_TILES[0]) * (b + 1))
                    act.dma_start(v_even[:P // 2, :, :], v[:P // 2, :, :]).then_inc(v_copied, 16)
                    act.dma_start(v_even[P // 2:, 1:, :], v[P // 2:, :NT - 1, :]).then_inc(v_copied, 16)

            act.preload_act_table_set(EXP_LN)
            act.sem_inc(ss_logged, 2)
            act.sem_inc(exped, NW)
            act.sem_inc(pt_kept[0], 1)
            for i in range(2):
                square(0, i)
            for i in range(2):
                scale(0, i)
            unit(0, 0, first=True)
            with act.Fori(0, NB - 1) as b:
                for j in range(1, HP):
                    unit(b, j)
                unit(b + 1, 0)
            for j in range(1, HP):
                unit(NB - 1, j, ahead=(j < HP - 1))
            unit(NB, 0, ahead=False, own=False)
            act.wait_ge(v_copied, START + 32 * NB)

        @block.vector
        def _(dve):
            def halves(b):
                dve.wait_ge(taken, START + 2 * (b + 1))
                dve.wait_ge(projected, START + 4 * HP * b)
                dve.wait_ge(v_done, START + NT * b)
                dve.tensor_copy(hh[:], hs[:]).then_inc(hi_done, 1)
                dve.wait_ge(hi_done, START + b + 1)
                dve.tensor_tensor(hl[:], hs[:], hh[:], ALU.subtract).then_inc(split, 1)

            def rotate(n):
                for k in ORDER:
                    dve.wait_ge(projected, START + 4 * n + ORDER.index(k) + 1)
                    if k % 2 == 0:
                        dve.wait_ge(squared, START + 2 * n + k // 2 + 1)
                    dve.wait_ge(added, START + 2 * n)
                    dve.tensor_tensor(turned[:, k, :], m.ps[:, Q + k, :], w.tables[:, k, :], ALU.mult).then_inc(rotated, 1)

            def maxima(n, j):
                for half in range(2):
                    dve.wait_ge(sim_done, START + 2 * n + half + 1)
                    dve.wait_ge(exped, START + NW * n + HW * (half + 1))
                    dve.tensor_reduce(nmax[:, j % 2, half * HW:(half + 1) * HW],
                                      m.ps[:, S + half, :].rearrange("p (w k) -> p w k", k=P), AX.X, ALU.max,
                                      negate=True).then_inc(maxed, 1)

            def scale_qk(n, j):
                dve.wait_ge(sim_done, START + 2 * n)
                dve.wait_ge(rn_done, START + 2 * n + 1)
                dve.wait_ge(added, START + 2 * n + 1)
                dve.scalar_tensor_tensor(out=qn[:, j % 2, :], in0=rn[:, 0, :], scalar=8e12, in1=sums[:, 0, :], op0=ALU.min,
                                         op1=ALU.mult).then_inc(qk_done, 1)
                dve.wait_ge(rn_done, START + 2 * n + 2)
                dve.wait_ge(added, START + 2 * n + 2)
                blocks = lambda t: t.rearrange("p (t k c) -> p t k c", k=2, c=WIN)
                for k in range(2):
                    half = dve.scalar_tensor_tensor(out=kn[:, j % 2, k * (NT + 1):k * (NT + 1) + NT, :],
                                                    in0=blocks(rn[:, 1, :])[:, :, k, :], scalar=1e12,
                                                    in1=blocks(sums[:, 1, :])[:, :, k, :], op0=ALU.min, op1=ALU.mult)
                half.then_inc(qk_done, 1)

            def reciprocals(n, j):
                dve.wait_ge(exped, START + NW * (n + 2))
                dve.wait_ge(normed, START + 2 * n)
                dve.reciprocal(rsum[:, j % 2, :], psum_[:, j % 2, :]).then_inc(recip, 1)

            def keep_turned(n):
                dve.wait_ge(pt_done, START + 2 * n + 2 + 2)
                dve.wait_ge(pv_done, START + 2 * n)
                dve.tensor_copy(pts[:, 1, :], m.ps[:, PT, :]).then_inc(pt_kept[1], 1)

            def keep_out(n, j, b):
                dve.wait_ge(pv_done, START + 2 * n + 2)
                dve.wait_ge(wo_done, START + b)
                dve.tensor_copy(o[:, j, :], m.ps[:, O, :]).then_inc(o_kept, 1)

            def unit(b, j, first=False, ahead=True, own=True, last=False):
                n = b * HP + j
                if ahead:
                    rotate(n + 1)
                if own:
                    maxima(n, j)
                if j == HP - 2 and not last:
                    halves(b + 1)
                if not first:
                    keep_turned(n - 1)
                    keep_out(n - 1, (j - 1) % HP, b if j else b - 1)
                if ahead:
                    scale_qk(n + 1, (j + 1) % HP)
                if own:
                    reciprocals(n, j)
                if j == 0:
                    if not first:
                        dve.wait_ge(wo_done, START + b)
                        dve.tensor_tensor(seq(m.u, b - 1), m.ps[:, O, :], seq(m.u, b - 1), ALU.add).then_inc(u_done, 1)
                if j == 0 and own:
                    dve.wait_ge(v_copied, START + 32 * b)
                    for t in V_TILES[1]:
                        dve.wait_ge(v_done, START + NT * b + V_ORDER.index(t) + 1)
                        dve.tensor_copy(v[:, t, :], m.ps[:, O, :]).then_inc(v_kept[1], 1)

            dve.sem_inc(rotated, 4)
            dve.sem_inc(pt_kept[1], 1)
            dve.sem_inc(o_kept, 1)
            dve.memset(v_even[P // 2:, 0, :], 0.0).then_inc(zeroed, 1)
            for k in range(2):
                dve.memset(kn[:, k, NT, :], 0.0).then_inc(zeroed, 1)
            halves(0)
            rotate(0)
            scale_qk(0, 0)
            unit(0, 0, first=True)
            with dve.Fori(0, NB - 1) as b:
                for j in range(1, HP):
                    unit(b, j)
                unit(b + 1, 0)
            for j in range(1, HP):
                unit(NB - 1, j, ahead=(j < HP - 1), last=True)
            unit(NB, 0, ahead=False, own=False)

        @block.gpsimd
        def _(pool):
            def take(b):
                pool.wait_ge(split, START + b)
                pool.tensor_copy(hs[:P // 2, :], m.u[:P // 2, bass.ds(b * T, T)]).then_inc(taken, 1)
                pool.tensor_copy(hs[P // 2:, 1:], m.u[P // 2:, bass.ds(b * T, T - 1)]).then_inc(taken, 1)
                pool.wait_ge(taken, START + 2 * b + 2)

            def add(n):
                for i in range(2):
                    pool.wait_ge(rotated, START + 4 * n + 2 * i + 2 + 4)
                    pool.wait_ge(qk_done, START + 2 * n)
                    pool.tensor_tensor(sums[:, i, :], turned[:, 2 * i, :], turned[:, 2 * i + 1, :], ALU.add).then_inc(added, 1)

            def norm(n, j):
                pool.wait_ge(recip, START + n + 1)
                for half in range(2):
                    ws = slice(half * HW, (half + 1) * HW)
                    pool.tensor_tensor(probs[:, j % 2, ws, :], probs[:, j % 2, ws, :],
                                       rsum[:, j % 2, ws].unsqueeze(2).to_broadcast([P, HW, P]),
                                       ALU.mult).then_inc(normed, 1)

            pool.memset(hs[P // 2:, 0:1], 0.0).then_inc(zeroed2, 1)
            pool.wait_ge(zeroed2, START + 1)
            take(0)
            add(0)
            pool.wait_ge(added, START + 2)
            add(1)
            norm(0, 0)
            with pool.Fori(0, NB - 1) as b:
                pool.wait_ge(normed, START + 2 * (HP * b + 1))
                take(b + 1)
                for j in range(1, HP + 1):
                    n = b * HP + j
                    add(n + 1)
                    norm(n, j % HP)
            for j in range(1, HP):
                n = (NB - 1) * HP + j
                if j < HP - 1:
                    add(n + 1)
                norm(n, j)


def gated_phase(nc, m, app, l, w, last):
    A, G, Y = [2, 3, 2], [4, 5, 4], 6
    with Phase(nc) as c:
        name = f"ff{app}{l}"
        sb = lambda n, s, d=F32: c.enter_context(nc.sbuf_tensor(f"{name}_{n}", s, d))
        sem = lambda n: c.sem(f"{name}_{n}")
        ln = Norm(nc, c, m, name + "_ln", 0, 1, shift=True, switch=True)
        xh, xl = sb("xh", [P, T], F32R), sb("xl", [P, T], F32R)
        gate, prod = sb("gate", [P, MC, T]), sb("prod", [P, MC, T])
        hi_done, split, up_done, gelued, gated = sem("hi_done"), sem("split"), sem("up_done"), sem("gelued"), sem("gated")
        down_done, u_done, x_done = sem("down_done"), sem("u_done"), sem("x_done")
        block = c.block()
        width = [MW, MW, HID - 2 * MW]

        @block.gpsimd
        def _(pool):
            ln.start(pool)
            ln.take(pool, 0, m.u, 0)
            ln.take(pool, 1, m.u, 1)
            with pool.Fori(0, NB) as b:
                ln.take(pool, b + 2, m.u, b + 2)

        @block.tensor
        def _(pe):
            def up(b, i):
                pe.wait_ge(gated, START + MC * b + (i == 2))
                for k, bank in ((1, G[i]), (0, A[i])):
                    cols = slice(k * HID + i * MW, k * HID + i * MW + width[i])
                    mm3(pe, m.ps[:width[i], bank, :], (w.w1h[:, cols], w.w1l[:, cols]), (xh[:], xl[:])).then_inc(up_done, 1)

            def down(b, i):
                pe.wait_ge(gated, START + MC * b + i + 1)
                if i == 0:
                    pe.wait_ge(u_done, START + b)
                pe.matmul(m.ps[:, Y, :], w.w2[:width[i], i, :], prod[:width[i], i, :], start=(i == 0),
                          stop=(i == MC - 1)).then_inc(down_done, 1)

            ln.centre(pe, 0)
            ln.variance(pe, 0)
            ln.centre(pe, 1)
            with pe.Fori(0, NB) as b:
                pe.wait_ge(split, START + b + 1)
                up(b, 0)
                up(b, 1)
                up(b, 2)
                ln.variance(pe, b + 1)
                for i in range(MC):
                    down(b, i)
                ln.centre(pe, b + 2)

        @block.scalar
        def _(act):
            def gelu(b, i):
                act.wait_ge(up_done, START + 2 * (MC * b + i) + 1)
                act.wait_ge(gated, START + MC * b)
                act.activation(gate[:width[i], i, :], m.ps[:width[i], G[i], :], ACT.Gelu,
                               bias=w.bias[:width[i], MC + i:MC + i + 1]).then_inc(gelued, 1)

            ln.square(act, 0)
            ln.scale(act, 0)
            act.preload_act_table_set(GELU)
            with act.Fori(0, NB) as b:
                for i in range(MC):
                    gelu(b, i)
                    if i == 0:
                        ln.square(act, b + 1)
                ln.scale(act, b + 1)
                act.preload_act_table_set(GELU)

        @block.vector
        def _(dve):
            def halves(n):
                dve.wait_ge(up_done, START + 2 * MC * n)
                dve.wait_ge(ln.normed, START + n + 1)
                dve.tensor_copy(xh[:], ln.out[:]).then_inc(hi_done, 1)
                dve.wait_ge(hi_done, START + n + 1)
                dve.tensor_tensor(xl[:], ln.out[:], xh[:], ALU.subtract).then_inc(split, 1)

            ln.norm(dve, 0)
            halves(0)
            with dve.Fori(0, NB) as b:
                for i in range(MC):
                    dve.wait_ge(up_done, START + 2 * (MC * b + i) + 2)
                    dve.wait_ge(gelued, START + MC * b + i + 1)
                    dve.wait_ge(down_done, START + MC * b)
                    dve.scalar_tensor_tensor(out=prod[:width[i], i, :], in0=m.ps[:width[i], A[i], :],
                                             scalar=w.bias[:width[i], i:i + 1], in1=gate[:width[i], i, :],
                                             op0=ALU.add, op1=ALU.mult).then_inc(gated, 1)
                ln.norm(dve, b + 1)
                halves(b + 1)
                dve.wait_ge(down_done, START + MC * (b + 1))
                dve.scalar_tensor_tensor(out=seq(m.u, b), in0=m.ps[:, Y, :], scalar=w.b2[:, 0:1], in1=seq(m.u, b),
                                         op0=ALU.add, op1=ALU.add).then_inc(u_done, 1)
                if last:
                    dve.wait_ge(u_done, START + b + 1)
                    dve.scalar_tensor_tensor(out=seq(m.x, b), in0=seq(m.u, b), scalar=0.5, in1=seq(m.x, b),
                                             op0=ALU.mult, op1=ALU.add).then_inc(x_done, 1)


def global_phase(nc, m, ins):
    with Phase(nc) as c:
        sb = lambda n, s, d=F32: c.enter_context(nc.sbuf_tensor(f"glob_{n}", s, d))
        sem = lambda n: c.sem(f"glob_{n}")
        ln = Norm(nc, c, m, "glob_ln", 0, 1)
        raw = sb("raw", [P, 3, P])
        wh, wl = sb("wh", [P, 3, P], F32R), sb("wl", [P, 3, P], F32R)
        xh, xl = sb("xh", [P, T], F32R), sb("xl", [P, T], F32R)
        ones = sb("ones", [P, P])
        squares, rn, v = sb("squares", [P, 2, T]), sb("rn", [P, 2, T]), sb("v", [P, T])
        kn, kv, qn, feat = sb("kn", [P, T]), sb("kv", [P, T]), sb("qn", [P, T]), sb("feat", [P, 1])
        w_in, steps, hi_done, split, projected = sem("w_in"), sem("steps"), sem("hi_done"), sem("split"), sem("projected")
        squared, v_kept, ss_done, ss_logged, rn_done = sem("squared"), sem("v_kept"), sem("ss_done"), sem("ss_logged"), sem("rn_done")
        k_scaled, q_scaled, feated, x_done = sem("k_scaled"), sem("q_scaled"), sem("feated"), sem("x_done")
        block = c.block()
        Q, K, V, SS = 2, 3, 4, 5

        @block.sync
        def _(sp):
            sp.dma_start(raw[:], ins["qkv_global"]).then_inc(w_in, 16)

        @block.gpsimd
        def _(pool):
            ln.take(pool, 0, m.x, 0)
            ln.take(pool, 1, m.x, 1)
            with pool.Fori(0, NB) as b:
                ln.take(pool, b + 2, m.x, b + 2)

        @block.tensor
        def _(pe):
            ln.centre(pe, 0)
            ln.variance(pe, 0)
            ln.centre(pe, 1)
            with pe.Fori(0, NB) as b:
                ln.variance(pe, b + 1)
                pe.wait_ge(split, START + b + 1)
                for k in (1, 0, 2):
                    if k == Q - 2:
                        pe.wait_ge(q_scaled, START + b)
                    if k == K - 2:
                        pe.wait_ge(k_scaled, START + b)
                    if k == V - 2:
                        pe.wait_ge(v_kept, START + b)
                    mm3(pe, m.ps[:, Q + k, :], (wh[:, k, :], wl[:, k, :]), (xh[:], xl[:])).then_inc(projected, 1)
                for i in (1, 0):
                    pe.wait_ge(squared, START + 2 * b + 2 - i)
                    pe.wait_ge(ss_logged, START + 2 * b)
                    pe.matmul(m.ps[:, SS + i, :], ones[:], squares[:, i, :], start=True, stop=True).then_inc(ss_done, 1)
                ln.centre(pe, b + 2)

        @block.scalar
        def _(act):
            act.preload_act_table_set(EXP_LN)
            ln.square(act, 0)
            ln.scale(act, 0)
            ln.square(act, 1)
            with act.Fori(0, NB) as b:
                ln.scale(act, b + 1)
                for i in (1, 0):
                    act.wait_ge(projected, START + 3 * b + 2 - i)
                    act.wait_ge(ss_done, START + 2 * b)
                    act.activation(squares[:, i, :], m.ps[:, Q + i, :], ACT.Square).then_inc(squared, 1)
                act.wait_ge(projected, START + 3 * b + 3)
                act.wait_ge(feated, START + b)
                act.activation(v[:], m.ps[:, V, :], ACT.Copy).then_inc(v_kept, 1)
                for i in (1, 0):
                    act.wait_ge(ss_done, START + 2 * b + 2 - i)
                    act.wait_ge(k_scaled, START + b)
                    act.wait_ge(q_scaled, START + b)
                    act.activation(rn[:, i, :], m.ps[:, SS + i, :], ACT.Ln, bias=m.tiny[:, 0:1],
                                   scale=SS_SCALE).then_inc(ss_logged, 1)
                    act.wait_ge(ss_logged, START + 2 * b + 2 - i)
                    act.activation(rn[:, i, :], rn[:, i, :], ACT.Exp, scale=-0.5,
                                   bias=m.unscale[:, 1:2]).then_inc(rn_done, 1)
                ln.square(act, b + 2)

        @block.vector
        def _(dve):
            def halves(n):
                dve.wait_ge(projected, START + 3 * n)
                dve.wait_ge(ln.normed, START + n + 1)
                dve.tensor_copy(xh[:], ln.out[:]).then_inc(hi_done, 1)
                dve.wait_ge(hi_done, START + n + 1)
                dve.tensor_tensor(xl[:], ln.out[:], xh[:], ALU.subtract).then_inc(split, 1)

            dve.memset(ones[:], 1.0)
            dve.wait_ge(w_in, START + 16)
            split_weights(dve, [(raw[:], wh[:], wl[:])], steps, START)
            ln.norm(dve, 0)
            halves(0)
            with dve.Fori(0, NB) as b:
                dve.wait_ge(split, START + b + 1)
                ln.norm(dve, b + 1)
                dve.wait_ge(rn_done, START + 2 * b + 1)
                dve.scalar_tensor_tensor(out=kn[:], in0=rn[:, 1, :], scalar=1e12, in1=m.ps[:, K, :], op0=ALU.min,
                                         op1=ALU.mult).then_inc(k_scaled, 1)
                dve.wait_ge(v_kept, START + b + 1)
                dve.wait_ge(k_scaled, START + b + 1)
                dve.tensor_tensor_reduce(out=kv[:], in0=kn[:], in1=v[:], scale=1.0 / T, scalar=0.0, op0=ALU.mult,
                                         op1=ALU.add, accum_out=feat[:]).then_inc(feated, 1)
                halves(b + 1)
                dve.wait_ge(x_done, START + b)
                dve.wait_ge(rn_done, START + 2 * b + 2)
                dve.scalar_tensor_tensor(out=qn[:], in0=rn[:, 0, :], scalar=1e12, in1=m.ps[:, Q, :], op0=ALU.min,
                                         op1=ALU.mult).then_inc(q_scaled, 1)
                dve.wait_ge(feated, START + b + 1)
                dve.wait_ge(q_scaled, START + b + 1)
                dve.scalar_tensor_tensor(out=seq(m.x, b), in0=qn[:], scalar=feat[:, 0:1], in1=seq(m.x, b),
                                         op0=ALU.mult, op1=ALU.add).then_inc(x_done, 1)


IDENT = np.eye(P, dtype=np.float32)


def constants():
    k = {"ident": IDENT, "center": IDENT - np.float32(1.0 / P)}
    e = np.arange(NE)
    k["before"] = np.tile((e[None, :] < e[:, None]).astype(np.float32), (P, 1, 1))
    r = np.arange(P)
    sp = np.zeros((P, NS, P), np.float32)
    sh = np.zeros((P, NB, P), np.float32)
    for p in range(NS):
        for q in r:
            sp[(q // NS) * NS + p, p, q] = 1.0
    for b in range(NB):
        for q in r:
            sh[b * NH + q // NS, b, q] = 1.0
    k["spread_p"], k["spread_h"] = sp, sh
    k["gather_p"] = np.ascontiguousarray(sp.transpose(2, 1, 0))
    cm = np.ones((P, T), np.float32)
    cm[:, ::CHUNK] = 0.0
    k["chunk_mask"] = cm
    k["per_head"] = np.kron(np.eye(2), np.ones((DH, DH))).astype(np.float32)
    q, key = np.arange(WIN)[:, None], np.arange(2 * WIN)[None, :]
    seen = (key <= q + WIN) & (key >= q)
    later = np.where(seen, 0.0, MASKED)
    first = np.where(seen & (key >= WIN), 0.0, MASKED)
    own_first = lambda z: np.roll(z, WIN, axis=1)
    rows = np.stack([np.concatenate([own_first(w0), later, own_first(later), later], 1) for w0 in (first, later)], 1)
    k["masks"] = np.tile(rows, (2, 1, 1)).astype(np.float32)
    f32 = np.float32
    half = np.arange(0, DH, 2, dtype=f32)
    inv = (1.0 / (f32(10000.0) ** (half / f32(DH)))).astype(f32)
    t = np.arange(T, dtype=f32)
    freqs = (t[:, None] * inv[None, :]).astype(f32)
    base = (half + f32(0.4 * DH)) / f32(1.4 * DH)
    power = (t - T // 2) / f32(WIN // 2)
    scale = (base[None, :] ** power[:, None]).astype(f32)
    cos, sin = np.cos(freqs), np.sin(freqs)
    tab = []
    for sc in (scale, 1.0 / scale):
        cc, ss = (cos * sc).T, (sin * sc).T
        tab += [np.concatenate([cc, cc] * 2), np.concatenate([-ss, ss] * 2)]
    k["rotary"] = np.ascontiguousarray(np.stack(tab, 1).astype(f32))
    return k


def build(nc, ins, out):
    with ExitStack() as c:
        m = Mem()
        sb = lambda n, s, d=F32: c.enter_context(nc.sbuf_tensor(n, s, d))
        m.x = sb("x", [P, (NB + 2) * T])
        m.ident, m.center, m.mean_of = sb("ident", [P, P]), sb("center", [P, P]), sb("mean_of", [P, P])
        m.eps, m.before = sb("eps", [P, 1]), sb("before", [P, NE, NE])
        m.ps = c.enter_context(nc.psum_tensor("banks", [P, 8, T], F32))
        cw_dram = nc.dram_tensor("cw_dram", [NE, T], F32)
        with ExitStack() as moe:
            w = moe_weights(nc, moe)
            load_phase(nc, m, w, ins["L0_attn_x"], ins)
            moe_phase(nc, m, 0, w, cw_dram.ap())
            ssm_phase(nc, m, ins)
            moe_phase(nc, m, 1, w, cw_dram.ap())
        with ExitStack() as gated:
            m.u = gated.enter_context(nc.sbuf_tensor("u", [P, (NB + 2) * T], F32))
            ws = gated_weights(nc, gated, m, ins)
            for app in range(2):
                entry_phase(nc, m, app)
                for l in range(2):
                    attention_phase(nc, m, app, l, ws[l])
                    gated_phase(nc, m, app, l, ws[l], last=(l == 1))
                if app == 0:
                    global_phase(nc, m, ins)
        store_phase(nc, m, out)


def arrays(inp):
    import numpy as np
    a = {n: np.ascontiguousarray(np.asarray(v)) for n, v in inp.items()}
    t = np.ascontiguousarray
    a.update(constants())
    a["gate_t"] = t(a["L0_ffn_w_gate"].T)
    a["b1_t"] = t(a["L0_ffn_b1"].reshape(NE * HC, P).T)
    a["b2_t"] = t(a["L0_ffn_b2"].T)
    w_in = a["L0_attn_W_in"]
    a["ssm_w_in"] = t(w_in[:3 * P].T)
    a["ssm_w_dt"] = t(w_in[3 * P:].T)
    a["ssm_w_dtx"] = t(np.repeat(w_in[3 * P:], NS, axis=0).T)
    a["ssm_w_out"] = t(a["L0_attn_W_out"].T)
    a["ssm_conv_w"] = t(a["L0_attn_conv_w"].reshape(3, P, 4).transpose(1, 0, 2))
    a["ssm_conv_b"] = t(a["L0_attn_conv_b"].reshape(3, P).T)
    a["ssm_a"] = t(np.stack([np.tile(a["L0_attn_A_param"], NB), np.repeat(a["L0_attn_A_param"], NS)], 1))
    a["ssm_dt_b"] = t(np.stack([np.tile(a["L0_attn_dt_bias"], NB), np.repeat(a["L0_attn_dt_bias"], NS)], 1))
    a["b2_gated"] = t(a["L1_ffn_b2"][:, :, None])
    other = np.roll(np.arange(DH), DH // 2)
    qs, ks = a["L1_ffn_q_scale"], a["L1_ffn_k_scale"]
    a["qk_scales"] = t(np.stack([np.tile(z, (1, 2)) for z in (qs, qs[:, other], ks, ks[:, other])], 2).transpose(1, 0, 2))
    a["ln_w"] = t(np.stack([a["L1_ffn_ln_g"], a["L1_ffn_ln_b"]], 2).transpose(1, 0, 2))
    b1 = np.zeros((P, 2, 2 * MC), np.float32)
    for i in range(2 * MC):
        n = min(MW, HID - (i % MC) * MW)
        lo = (i // MC) * HID + (i % MC) * MW
        b1[:n, :, i] = a["L1_ffn_b1"][:, lo:lo + n].T
    a["b1_gated"] = b1
    a["qkv_global"] = t(np.stack([a[f"L1_attn_W_{n}"].T for n in "qkv"], 1))
    return a


USED = ["L0_attn_x", "L0_ffn_W1", "L0_ffn_W2", "gate_t", "b1_t", "b2_t", "before", "ident", "center",
        "ssm_w_in", "ssm_w_dt", "ssm_w_dtx", "ssm_w_out", "ssm_conv_w", "ssm_conv_b", "ssm_a", "ssm_dt_b",
        "spread_p", "gather_p", "spread_h", "chunk_mask", "per_head", "masks", "rotary", "b2_gated", "qk_scales", "ln_w", "b1_gated", "qkv_global",
        "L1_ffn_wqkv", "L1_ffn_wo", "L1_ffn_w1", "L1_ffn_w2"]


def kernel(**inputs):
    import numpy as np
    import concourse.bacc as bacc
    from concourse.bass_utils import run_bass_kernel_spmd

    nc = bacc.Bacc("TRN2", target_bir_lowering=False, num_devices=1)
    a = arrays(inputs)
    fed = {f"in_{n}": a[n] for n in USED}
    ins = {n: nc.dram_tensor(f"in_{n}", a[n].shape, mybir.dt.from_np(a[n].dtype), kind="ExternalInput").ap() for n in USED}
    out = nc.dram_tensor("out_0", (NB, T, P), F32, kind="ExternalOutput").ap()
    build(nc, ins, out)
    r = run_bass_kernel_spmd(nc, [fed], core_ids=[0])
    return r.results[0]["out_0"]
```
